# Optimizing a Trainium2 kernel written in Bass

```python
import numpy as np
import jax
import jax.numpy as jnp

def _softmax(x, axis=-1):
    return jax.nn.softmax(x, axis=axis)

def _gelu(x):
    return jax.nn.gelu(x, approximate=True)

def _silu(x):
    return jax.nn.silu(x)

def _sigmoid(x):
    return jax.nn.sigmoid(x)

def _layernorm(x, axis=-1, eps=1e-05):
    m = jnp.mean(x, axis=axis, keepdims=True)
    v = jnp.var(x, axis=axis, keepdims=True)
    return (x - m) / jnp.sqrt(v + eps)

def _scatter_add(tgt, idx, src, axis=0):
    return tgt.at[idx].add(src)

def _segment_sum(src, seg, n):
    return jax.ops.segment_sum(src, seg, n)
kernel_name = 'mk_gnn_resnorm_d1_gnn_r64_a9a081'

def setup_inputs(seed: int=0):
    np.random.seed(seed)
    _w = jnp.asarray

    def _rec_inputs():
        import jax
        import jax.numpy as jnp
        _gk = jax.random.key(seed)
        x = -0.000202 + 1 * jax.random.normal(jax.random.fold_in(_gk, 1), (100000, 64), jnp.float32)
        src = jax.random.randint(jax.random.fold_in(_gk, 2), (50000,), 0, 100000, jnp.int32)
        dst = jax.random.randint(jax.random.fold_in(_gk, 3), (50000,), 0, 100000, jnp.int32)
        _o = jnp.argsort(dst, stable=True)
        src = src[_o]
        dst = dst[_o]
        edge_attr_32 = -8.62073e-06 + 0.999901 * jax.random.normal(jax.random.fold_in(_gk, 12), (50000, 32), jnp.float32)
        return (x, src, dst, edge_attr_32)
    x, src, dst, edge_attr_32 = _rec_inputs()

    def _L0_gnn_setup():
        import jax, jax.numpy as jnp
        import numpy as np
        IN_DIM, E_DIM, OUT_DIM = (64, 32, 64)
        N_NODES, N_EDGES = (100000, 15625)
        NEG_SLOPE = 0.2
        key = jax.random.key(seed)
        ks = jax.random.split(key, 9)
        gain = float(np.sqrt(2.0))

        def xavier(k, shape):
            fan_out, fan_in = shape
            std = gain * np.sqrt(2.0 / (fan_in + fan_out))
            return jax.random.normal(k, shape, dtype=jnp.float32) * std
        nfeats = jax.random.normal(ks[0], (N_NODES, IN_DIM), dtype=jnp.float32)
        efeats = jax.random.normal(ks[1], (N_EDGES, E_DIM), dtype=jnp.float32)
        src = jax.random.randint(ks[2], (N_EDGES,), 0, N_NODES, dtype=jnp.int32)
        dst = jax.random.randint(ks[3], (N_EDGES,), 0, N_NODES, dtype=jnp.int32)
        proj_w = xavier(ks[4], (OUT_DIM, IN_DIM + E_DIM))
        attn_w = xavier(ks[5], (1, 2 * IN_DIM))
        attn_b = jnp.zeros((1,), dtype=jnp.float32)
        apply_w = xavier(ks[6], (OUT_DIM, IN_DIM + OUT_DIM))
        apply_b = jnp.zeros((OUT_DIM,), dtype=jnp.float32)
        return {'nfeats': nfeats, 'efeats': efeats, 'src': src, 'dst': dst, 'proj_w': proj_w, 'attn_w': attn_w, 'attn_b': attn_b, 'apply_w': apply_w, 'apply_b': apply_b}
    _L0_gnn_all = _L0_gnn_setup()
    _L0_gnn_in = {k: v for k, v in _L0_gnn_all.items() if k in ('proj_w', 'attn_w', 'attn_b', 'apply_w', 'apply_b')}
    del _L0_gnn_all
    return {'x': x, 'src': src, 'dst': dst, 'edge_attr_32': edge_attr_32, 'L0_gnn_proj_w': _L0_gnn_in['proj_w'], 'L0_gnn_attn_w': _L0_gnn_in['attn_w'], 'L0_gnn_attn_b': _L0_gnn_in['attn_b'], 'L0_gnn_apply_w': _L0_gnn_in['apply_w'], 'L0_gnn_apply_b': _L0_gnn_in['apply_b']}

def reference(x, src, dst, edge_attr_32, L0_gnn_proj_w, L0_gnn_attn_w, L0_gnn_attn_b, L0_gnn_apply_w, L0_gnn_apply_b):
    import jax
    import jax.numpy as jnp

    def _L0_gnn_ref(nfeats, efeats, src, dst, proj_w, attn_w, attn_b, apply_w, apply_b):
        import jax, jax.numpy as jnp
        import numpy as np
        IN_DIM, E_DIM, OUT_DIM = (64, 32, 64)
        N_NODES, N_EDGES = (100000, 15625)
        NEG_SLOPE = 0.2
        n_nodes = nfeats.shape[0]
        h_src = nfeats[src]
        h_dst = nfeats[dst]
        e = h_src @ attn_w[0, :IN_DIM] + h_dst @ attn_w[0, IN_DIM:] + attn_b[0]
        e = jnp.where(e >= 0, e, NEG_SLOPE * e)
        m = h_src @ proj_w[:, :IN_DIM].T + efeats @ proj_w[:, IN_DIM:].T
        e_max = jax.ops.segment_max(e, dst, num_segments=n_nodes)
        e_exp = jnp.exp(e - e_max[dst])
        denom = jax.ops.segment_sum(e_exp, dst, num_segments=n_nodes)
        alpha = e_exp / denom[dst]
        z = jax.ops.segment_sum(alpha[:, None] * m, dst, num_segments=n_nodes)
        out = jnp.concatenate([nfeats, z], axis=1) @ apply_w.T + apply_b
        return jax.nn.relu(out)
    x = _layernorm(x + _L0_gnn_ref(x, edge_attr_32, src, dst, L0_gnn_proj_w, L0_gnn_attn_w, L0_gnn_attn_b, L0_gnn_apply_w, L0_gnn_apply_b), axis=-1)
    return x

_drawn_inputs = setup_inputs


def setup_inputs(seed=0):
    import zlib

    import numpy as np

    out = dict(_drawn_inputs(seed))
    spreads = {'L0_gnn_apply_b': (0.0, 0.1)}
    factors = {}
    for name, (base, spread) in spreads.items():
        noise = np.random.default_rng([zlib.crc32(name.encode()), seed]).standard_normal(out[name].shape)
        drawn = base * np.exp(spread * noise) if base else spread * noise
        out[name] = jnp.asarray(drawn.astype(out[name].dtype))
    for name, factor in factors.items():
        out[name] = (out[name] * factor).astype(out[name].dtype)
    return out
```

```python
import concourse.bass as bass
from concourse import mybir
from contextlib import ExitStack

FP32, BF16, I32 = mybir.dt.float32, mybir.dt.bfloat16, mybir.dt.int32
ALU, ACT, AX = mybir.AluOpType, mybir.ActivationFunctionType, mybir.AxisListType

P = 128
N_NODES, N_EDGES, F, FE = 100000, 50000, 64, 32
FV = F + FE
NPB = 192
PW = NPB // 2
NW = -(-N_NODES // NPB)
NQ = -(-NW // 4)
LAST_NODES = N_NODES - (NW - 1) * NPB
RING = 12
NSB = -(-NQ // 4)
WC = -(-NSB * 16 // 5)
NWP = 5 * WC
RQ = -(-N_EDGES // 512)
R_TAIL = N_EDGES - (RQ - 1) * 512
PAD_NODE = 131072
BIG = 1.0e30
EPS = 1.0e-5
LEAK = 0.2


def gnn_kernel(nc, x, src, dst, ef, proj_w, attn_w, attn_b, apply_w, apply_b, out):
    ef_scratch = nc.dram_tensor("ef_scratch", (NWP, P * FE), FP32, kind="Internal").ap()
    pair_scratch = nc.dram_tensor("pair_scratch", (NWP, P), BF16, kind="Internal").ap()
    local_scratch = nc.dram_tensor("local_scratch", (NWP, P), BF16, kind="Internal").ap()
    first_scratch = nc.dram_tensor("first_scratch", (NWP,), FP32, kind="Internal").ap()

    ctx = ExitStack()
    with ctx:
        def sb(name, shape, dt=FP32):
            return ctx.enter_context(nc.sbuf_tensor(name, shape, dt))

        def sem(name):
            return ctx.enter_context(nc.semaphore(name))

        bank = [ctx.enter_context(nc.psum_tensor(f"bank{i}", [P, 512], FP32)) for i in range(8)]

        iota_i = sb("iota_i", [P, NWP], I32)
        ident = sb("ident", [P, P])
        order_i = sb("order_i", [P, PW], I32)
        order = sb("order", [P, PW])
        node_i = sb("node_i", [P, 2], I32)
        node_id = sb("node_id", [P, 2])
        base_i = sb("base_i", [P, 5], I32)
        base = sb("base", [P, 5])
        starts = sb("starts", [P, NWP])
        part_i = sb("part_i", [P, 1], I32)
        part_f = sb("part_f", [P, 1])
        pair_col_i = iota_i
        ones_col = sb("ones_col", [P, 1])
        ones3 = sb("ones3", [3, P], BF16)
        eps_col = sb("eps_col", [P, 1])
        proj_sb = sb("proj_sb", [F, FV])
        a1_twice = sb("a1_twice", [F, 2 * F])
        a2_sb = sb("a2_sb", [F, F])
        a2_t = sb("a2_t", [F, F])
        edge_w = sb("edge_w", [FV, F + 1])
        node_w = sb("node_w", [P, 2 * F])
        attn_dst = sb("attn_dst", [P, 2])
        attn_b_col = sb("attn_b_col", [P, 1])
        bias_f = sb("bias_f", [3, F])
        bias_rest = sb("bias_rest", [3, F])
        bias_lo = sb("bias_lo", [3, F])
        bias_sum = sb("bias_sum", [3, F])
        bias_hi = sb("bias_hi", [3, F], BF16)
        bias_mid = sb("bias_mid", [3, F], BF16)
        bias3 = sb("bias3", [3, 2 * F], BF16)
        pick = sb("pick", [3, 3])
        local_col = sb("local_col", [P, NWP])
        pair_col = sb("pair_col", [P, NWP])
        parity = sb("parity", [P, NWP, 2])
        src_col = sb("src_col", [P, NWP], I32)
        links = sb("links", [16, NSB, 3, P + 1], BF16)
        same = links[:, :, 0, :]
        apart = links[:, :, 1, :]
        wall = links[:, :, 2, :]
        links_now = sb("links_now", [16, 3, P + 1], BF16)
        first_row = sb("first_row", [P, NWP])
        src_now = sb("src_now", [P, 2, 24], I32)
        v_sb = sb("v_sb", [P, RING, 4, FV])
        x_sb = sb("x_sb", [PW, RING, 4, 2 * F])
        vt_sb = sb("vt_sb", [FV, 2, 4, P])
        xt_sb = sb("xt_sb", [P, RING, 4, PW])
        y_sb = sb("y_sb", [P, RING, 4, F + 1])
        pair_b = sb("pair_b", [PW, 4, 4 * P], BF16)
        hot_t = sb("hot_t", [PW, 2, 4 * P], BF16)
        sd_rest = sb("sd_rest", [PW, 2, 8])
        sd_parts = sb("sd_parts", [PW, 2, 8, 3], BF16)
        ds_parts = sb("ds_parts", [P, 16, 6])
        dst_score = sb("dst_score", [P, 16])
        logit = sb("logit", [P, 16])
        logit_l = sb("logit_l", [P, 16])
        run_max = sb("run_max", [16, P])
        seg_max = sb("seg_max", [16, P])
        shifted = sb("shifted", [16, P])
        weight = sb("weight", [16, P])
        run_sum = sb("run_sum", [16, P])
        last_sum = sb("last_sum", [16, P])
        seg_sum = sb("seg_sum", [16, P])
        seg_rcp = sb("seg_rcp", [16, P])
        alpha_row = sb("alpha_row", [16, P])
        alpha = sb("alpha", [P, 3, 16, 2])
        hot = sb("hot", [P, 2, 4, PW])
        y2 = sb("y2", [P, 2, 4, 2, F])
        r_sb = sb("r_sb", [PW, 4, 8, F])
        stats = sb("stats", [PW, 4, 8, 6])
        mean2 = sb("mean2", [PW, 4, 8])
        halves = sb("halves", [PW, 4, 8])
        moment = sb("moment", [PW, 4, 8])
        spread = sb("spread", [PW, 4, 8])
        var64 = sb("var64", [PW, 4, 8])
        ln_var = sb("ln_var", [PW, 4, 8])
        rstd = sb("rstd", [PW, 4, 8])
        shift = sb("shift", [PW, 4, 8])
        out_sb = sb("out_sb", [PW, 3, 8, F])

        early = ExitStack()

        def sb_early(name, shape, dt=FP32):
            return early.enter_context(nc.sbuf_tensor(name, shape, dt))

        dst_rows_i = sb_early("dst_rows_i", [RQ, 512], I32)
        dst_rows = sb_early("dst_rows", [RQ, 512])
        prev_i = sb_early("prev_i", [RQ, 1], I32)
        prev_f = sb_early("prev_f", [RQ, 1])
        above_last = sb_early("above_last", [RQ, NWP])
        holds = sb_early("holds", [RQ, NWP])
        below = sb_early("below", [WC, 512])
        count_in_row = sb_early("count_in_row", [WC, 5])
        first_edge = sb_early("first_edge", [WC, 5])
        start_f = sb_early("start_f", [WC, 5])
        start_i = sb_early("start_i", [WC, 5], I32)
        start_ef = sb_early("start_ef", [WC, 5], I32)
        win_dst_i = sb_early("win_dst_i", [WC, 5, P], I32)
        win_src_i = sb_early("win_src_i", [WC, 5, P], I32)
        win_dst = sb_early("win_dst", [WC, 5, P])
        win_src = win_dst
        win_ef = sb_early("win_ef", [WC, P * FE])
        local = sb_early("local", [WC, 5, P])
        local16 = sb_early("local16", [WC, 5, P], BF16)
        pair_i = win_dst_i
        pair16 = sb_early("pair16", [WC, 5, P], BF16)
        batch_local = sb_early("batch_local", [16, NSB, P], BF16)
        early.close()
        n_edges = sb("n_edges", [P, NW])
        crowded = sb("crowded", [P, NW])
        begin = sb("begin", [P, NW])
        span_i = sb("span_i", [P, NW], I32)
        rest = sb("rest", [P, NW])
        n_chunks = sb("n_chunks", [P, NW])
        ones_row = sb("ones_row", [P, NW])
        chunks_to = sb("chunks_to", [P, NW])
        key = sb("key", [P, NW])
        total_i = sb("total_i", [P, 1], I32)
        chunk_no = sb("chunk_no", [P, 1])
        block_no = sb("block_no", [P, 1])
        block_node = sb("block_node", [P, 1])
        last_node = sb("last_node", [P, 1])
        block_key = sb("block_key", [P, 1])
        chunk_begin = sb("chunk_begin", [P, 1])
        chunk_edge = sb("chunk_edge", [P, 1])
        chunk_node = sb("chunk_node", [P, 1])
        overlap = sb("overlap", [P, 1])
        goes_on = sb("goes_on", [P, 1])
        reset = sb("reset", [P, 1])
        chunk_i = sb("chunk_i", [P, 2], I32)
        node_now = sb("node_now", [P, 2])
        c_dst_i = sb("c_dst_i", [PW, P], I32)
        c_dst = sb("c_dst", [PW, P])
        c_src = sb("c_src", [P, 1], I32)
        c_v = sb("c_v", [P, FV])
        c_x = sb("c_x", [PW, 2 * F])
        c_vt = sb("c_vt", [FV, P])
        c_xt = sb("c_xt", [P, PW])
        c_y = sb("c_y", [P, F])
        attn_src_wide = sb("attn_src_wide", [FV, PW])
        valid = sb("valid", [P, P])
        c_mask = sb("c_mask", [PW, 2, P])
        c_wall = sb("c_wall", [PW, 2, P])
        c_own = sb("c_own", [PW, 2])
        c_logit = sb("c_logit", [PW, 2, P])
        c_leaky = sb("c_leaky", [PW, 2, P])
        c_max = sb("c_max", [PW, 2])
        old_max = sb("old_max", [PW, 2])
        new_max = sb("new_max", [PW, 2])
        minus_max = sb("minus_max", [PW, 2])
        drop = sb("drop", [PW, 2])
        scale = sb("scale", [PW, 2])
        c_exp = sb("c_exp", [PW, 2, P])
        c_weight = sb("c_weight", [PW, 2, P])
        c_sum = sb("c_sum", [PW, 2])
        z_sum = sb("z_sum", [PW, 2])
        z_acc = sb("z_acc", [PW, 2, F])
        c_weight_t = sb("c_weight_t", [P, 2, PW])
        divisor = sb("divisor", [PW, 2])
        inverse = sb("inverse", [PW, 2])
        c_h = sb("c_h", [PW, 2, F])
        c_r = sb("c_r", [PW, 2, F])
        c_stats = sb("c_stats", [PW, 2, 6])
        c_moments = sb("c_moments", [PW, 2, 2])
        c_ln = sb("c_ln", [PW, 2])
        c_rstd = sb("c_rstd", [PW, 2])
        c_out = sb("c_out", [PW, 2, F])

        vt_ps = bank[0][0:FV, :].rearrange("p (w e) -> p w e", w=4)
        xt_ps = bank[1][:, 0:4 * PW].rearrange("p (w n) -> p w n", w=4)
        y_ps = bank[2][:, 0:4 * (F + 1)].rearrange("p (w f) -> p w f", w=4)
        h_ps = [bank[3], bank[4]]
        sd_ps = bank[5][0:PW, 0:16].rearrange("p (r c) -> p r c", r=2)
        ds_ps = bank[6][:, 0:288].rearrange("p (r w c) -> p r w c", r=3, w=16)
        row_ps = bank[7][0:16, 0:P]
        col_ps = bank[7][:, P:P + 16]

        s_iota = sem("s_iota")
        s_weights = [sem(f"s_weights{i}") for i in range(11)]
        s_ds = sem("s_ds")
        s_pad = sem("s_pad")
        s_parted = sem("s_parted")
        s_ident = sem("s_ident")
        s_wt = sem("s_wt")
        s_a2t = sem("s_a2t")
        s_ew = sem("s_ew")
        s_holds = sem("s_holds")
        s_rows = sem("s_rows")
        s_local = sem("s_local")
        s_local16 = sem("s_local16")
        s_srcf = sem("s_srcf")
        s_loc_t = sem("s_loc_t")
        s_src_t = sem("s_src_t")
        s_starts = sem("s_starts")
        s_wdst = sem("s_wdst")
        s_wsrc = sem("s_wsrc")
        s_wef = sem("s_wef")
        s_wef_out = sem("s_wef_out")
        s_pair16 = sem("s_pair16")
        s_pair_out = sem("s_pair_out")
        s_local_out = sem("s_local_out")
        s_batch_local = sem("s_batch_local")
        s_setup = sem("s_setup")
        s_src = sem("s_src")
        s_gath = [sem(f"s_gath{i}") for i in range(RING)]
        s_ef = [sem(f"s_ef{i}") for i in range(RING)]
        s_x = [sem(f"s_x{i}") for i in range(RING)]
        s_loc = [sem(f"s_loc{i}") for i in range(4)]
        s_tr = sem("s_tr")
        s_cp = sem("s_cp")
        s_ys = sem("s_ys")
        s_ycp = sem("s_ycp")
        s_hot_t = sem("s_hot_t")
        s_parts = sem("s_parts")
        s_score = sem("s_score")
        s_dst_part = sem("s_dst_part")
        s_logit = sem("s_logit")
        s_links = sem("s_links")
        s_row = sem("s_row")
        s_soft = sem("s_soft")
        s_exp = sem("s_exp")
        s_col = sem("s_col")
        s_alpha = sem("s_alpha")
        s_hot = sem("s_hot")
        s_h = sem("s_h")
        s_r = sem("s_r")
        s_stat = sem("s_stat")
        s_ln = sem("s_ln")
        s_shift = sem("s_shift")
        s_norm = sem("s_norm")
        s_store = [sem(f"s_store{i}") for i in range(3)]

        s_first_out = sem("s_first_out")
        s_first_row = sem("s_first_row")
        s_total = sem("s_total")
        s_fix = sem("s_fix")
        s_where = sem("s_where")
        s_c_src = sem("s_c_src")
        s_c_dst = sem("s_c_dst")
        s_c_ef = sem("s_c_ef")
        s_c_x = sem("s_c_x")
        s_c_gath = sem("s_c_gath")
        s_c_tr = sem("s_c_tr")
        s_c_cp = sem("s_c_cp")
        s_c_prod = sem("s_c_prod")
        s_c_max = sem("s_c_max")
        s_c_exp = sem("s_c_exp")
        s_c_weight = sem("s_c_weight")
        s_c_wt = sem("s_c_wt")
        s_c_wcp = sem("s_c_wcp")
        s_c_z = sem("s_c_z")
        s_c_var = sem("s_c_var")
        s_c_ln = sem("s_c_ln")
        s_c_rstd = sem("s_c_rstd")
        s_c_out = sem("s_c_out")
        s_c_store = sem("s_c_store")
        FIX_STEPS = 29

        def ge(eng, s, n):
            if not (isinstance(n, int) and n <= 0):
                eng.wait_ge(s, n)

        def part(eng):
            eng.sem_inc(s_parted, 1)

        def quads(eng, step, last_step):
            for j in range(RING):
                step(j, j, 0)
            n_rounds = NQ // RING
            with eng.Fori(1, n_rounds) as i:
                for j in range(RING):
                    step(i * RING + j, j, i)
            for q in range(n_rounds * RING, last_step + 1):
                step(q, q % RING, q // RING)

        def repair(eng, fix):
            eng.wait_ge(s_total, 1)
            total = eng.value_load(total_i[0:1, 0:1], min_val=0, max_val=2 * NW + N_EDGES // P)
            with eng.If(total > 0):
                with eng.Fori(0, total) as g:
                    fix(g)

        def is_quad(q):
            return not isinstance(q, int) or 0 <= q < NQ

        def is_batch_step(q, j, lag):
            return (j - lag) % 4 == 3 and (not isinstance(q, int) or 3 <= q - lag < 4 * NSB)

        def slot_round(j, i, lag, ring):
            k = j - lag
            return k % ring, i * (RING // ring) + k // ring + 1

        block = ctx.enter_context(nc.Block())

        @block.sync
        def _(sp):
            for slot in range(3):
                sp.sem_inc(s_store[slot], 16)
            sp.wait_ge(s_pad, 1)
            sp.dma_start(dst_rows_i[0:RQ - 1, :],
                         dst[0:(RQ - 1) * 512].rearrange("(q e) -> q e", e=512)).then_inc(s_weights[0], 16)
            sp.dma_start(dst_rows_i[RQ - 1:RQ, 0:R_TAIL],
                         dst[(RQ - 1) * 512:N_EDGES].unsqueeze(0)).then_inc(s_weights[1], 16)
            sp.dma_start(prev_i[1:RQ, :], dst[0:(RQ - 1) * 512].rearrange("(q e) -> q e", e=512)[:, 511:512],
                         allow_slow_non_contiguous=True).then_inc(s_weights[2], 16)
            sp.dma_start(proj_sb[:], proj_w).then_inc(s_weights[3], 16)
            sp.dma_start(a2_sb[:], apply_w[:, F:2 * F]).then_inc(s_weights[4], 16)
            sp.dma_start(a1_twice[:, 0:F], apply_w[:, 0:F]).then_inc(s_weights[5], 16)
            sp.dma_start(a1_twice[:, F:2 * F], apply_w[:, 0:F]).then_inc(s_weights[6], 16)
            sp.dma_start(edge_w[0:F, F:F + 1], attn_w[:, 0:F].rearrange("o f -> f o"),
                         allow_slow_non_contiguous=True).then_inc(s_weights[7], 16)
            sp.dma_start(attn_dst[0:F, 0:1], attn_w[:, F:2 * F].rearrange("o f -> f o"),
                         allow_slow_non_contiguous=True).then_inc(s_weights[8], 16)
            sp.dma_start(attn_dst[F:P, 1:2], attn_w[:, F:2 * F].rearrange("o f -> f o"),
                         allow_slow_non_contiguous=True).then_inc(s_weights[8], 16)
            sp.dma_start(attn_b_col[:], attn_b.unsqueeze(0).to_broadcast([P, 1])).then_inc(s_weights[9], 16)
            sp.dma_start(bias_f[:], apply_b.unsqueeze(0).to_broadcast([3, F])).then_inc(s_weights[10], 16)
            sp.wait_ge(s_starts, 1)
            sp.dma_start(first_scratch.rearrange("(c p) -> p c", c=5), first_edge[:],
                         allow_slow_non_contiguous=True).then_inc(s_first_out, 16)
            sp.wait_ge(s_local16, 1)
            sp.dma_start(local_scratch.rearrange("(c p) e -> p c e", c=5), local16[:]).then_inc(s_local_out, 16)
            sp.wait_ge(s_pair16, 1)
            sp.dma_start(pair_scratch.rearrange("(c p) e -> p c e", c=5), pair16[:]).then_inc(s_pair_out, 16)

            def edge_features(c):
                sp.wait_ge(s_wef, 16 * (c + 1))
                sp.dma_start(ef_scratch[c * WC:(c + 1) * WC, :], win_ef[:]).then_inc(s_wef_out, 16)
            edge_features(0)
            sp.wait_ge(s_local_out, 16)
            sp.dma_start(batch_local[:], local_scratch[0:NSB * 16, :].rearrange("(k g) e -> g k e", g=16)
                         ).then_inc(s_batch_local, 16)
            sp.wait_ge(s_pair_out, 16)
            sp.wait_ge(s_wef_out, 16)

            sp.wait_ge(s_first_out, 16)
            sp.dma_start(first_row[:], first_scratch.unsqueeze(0).to_broadcast([P, NWP])).then_inc(s_first_row, 16)

            def store(q, j, i):
                slot, n = slot_round(j, i, RING, 3)
                m = q - RING
                if isinstance(m, int) and not 0 <= m < NQ:
                    return
                sp.wait_ge(s_norm, m + 1)
                if isinstance(m, int) and m == NQ - 1:
                    for w in range(NW - 4 * (NQ - 1)):
                        g = 4 * m + w
                        n_here = min(NPB, N_NODES - g * NPB)
                        sp.dma_start(out[g * NPB:g * NPB + n_here, :].rearrange("(p j) f -> p (j f)", j=2),
                                     out_sb[0:n_here // 2, slot, 2 * w:2 * w + 2, :].rearrange("p c f -> p (c f)")
                                     ).then_inc(s_store[slot], 16)
                else:
                    sp.dma_start(out[bass.ds(m * (4 * NPB), 4 * NPB), :].rearrange("(w p j) f -> p w (j f)", w=4, j=2),
                                 out_sb[:, slot, :, :].rearrange("p (w j) f -> p w (j f)", w=4)
                                 ).then_inc(s_store[slot], 16)

            def step(q, j, i):
                if is_quad(q):
                    ge(sp, s_r, q - RING + 1)
                    ge(sp, s_tr, q - RING + 1)
                    if isinstance(q, int) and q == NQ - 1:
                        for w in range(NW - 4 * (NQ - 1)):
                            g = 4 * q + w
                            n_here = min(NPB, N_NODES - g * NPB)
                            sp.dma_start(x_sb[0:n_here // 2, j, w, :],
                                         x[g * NPB:g * NPB + n_here, :].rearrange("(p j) f -> p (j f)", j=2)
                                         ).then_inc(s_x[j], 16)
                    else:
                        sp.dma_start(x_sb[:, j, :, :],
                                     x[bass.ds(q * (4 * NPB), 4 * NPB), :].rearrange("(w p j) f -> p w (j f)", w=4, j=2)
                                     ).then_inc(s_x[j], 16)
                    sp.dma_start(v_sb[:, j, :, F:FV],
                                 ef_scratch[bass.ds(q * 4, 4), :].rearrange("w (e f) -> e w f", f=FE)
                                 ).then_inc(s_ef[j], 16)
                    ge(sp, s_hot_t, q - 3)
                    sp.dma_start(pair_b[:, j % 4, :],
                                 pair_scratch[bass.ds(q * 4, 4), :].rearrange("w e -> (w e)").unsqueeze(0)
                                 .to_broadcast([PW, 4 * P])).then_inc(s_loc[j % 4], 16)
                if isinstance(q, int) and q in (5, 7, 9, 11):
                    edge_features((q - 3) // 2)
                if isinstance(q, int) and q == RING - 1:
                    sp.wait_ge(s_wef_out, 80)
                store(q, j, i)
            quads(sp, step, NQ - 1 + RING)
            for slot in range(3):
                n = len(range(slot, NQ, 3))
                extra = NW - 4 * (NQ - 1) - 1 if (NQ - 1) % 3 == slot else 0
                sp.wait_ge(s_store[slot], 16 * (n + extra + 1))

            def fix(g):
                sp.wait_ge(s_where, g + 1)
                part(sp)
                edge = sp.value_load(chunk_i[0:1, 0:1], min_val=0, max_val=N_EDGES - P)
                node = sp.value_load(chunk_i[0:1, 1:2], min_val=0, max_val=N_NODES - NPB)
                sp.dma_start(c_src[:], src[bass.ds(edge, P)].unsqueeze(1),
                             allow_slow_non_contiguous=True).then_inc(s_c_src, 16)
                sp.dma_start(c_v[:, F:FV], ef[bass.ds(edge, P), :]).then_inc(s_c_ef, 16)
                sp.dma_start(c_x[:], x[bass.ds(node, NPB), :].rearrange("(p j) f -> p (j f)", j=2)
                             ).then_inc(s_c_x, 16)
                sp.dma_start(c_dst_i[:], dst[bass.ds(edge, P)].unsqueeze(0).to_broadcast([PW, P])
                             ).then_inc(s_c_dst, 16)
                sp.wait_ge(s_c_out, g + 1)
                sp.dma_start(out[bass.ds(node, NPB), :].rearrange("(p j) f -> p (j f)", j=2),
                             c_out[:].rearrange("p j f -> p (j f)")).then_inc(s_c_store, 16)
                sp.wait_ge(s_c_store, g * 16 + 16)
                part(sp)
            repair(sp, fix)

        @block.gpsimd
        def _(pool):
            nc.gpsimd.iota(iota_i[:, 0:P], pattern=[[1, P]], base=0, channel_multiplier=-1).then_inc(s_iota, 1)
            nc.gpsimd.iota(order_i[:], pattern=[[1, PW]], base=0, channel_multiplier=0).then_inc(s_iota, 1)
            nc.gpsimd.iota(node_i[:], pattern=[[1, 2]], base=0, channel_multiplier=2).then_inc(s_iota, 1)
            nc.gpsimd.iota(base_i[:], pattern=[[NPB * WC, 5]], base=0, channel_multiplier=NPB).then_inc(s_iota, 1)
            nc.gpsimd.iota(part_i[:], pattern=[[0, 1]], base=0, channel_multiplier=1).then_inc(s_iota, 1)
            pool.wait_ge(s_ident, 1)
            nc.gpsimd.iota(iota_i[:], pattern=[[NPB, NWP]], base=0, channel_multiplier=0).then_inc(s_iota, 1)
            pool.wait_ge(s_starts, 1)
            for c in range(5):
                pool.indirect_dma_start(out=win_dst_i[:, c, :], out_offset=None, in_=dst.unsqueeze(0),
                                        in_offset=bass.IndirectOffsetOnAxis(ap=start_i[:, c:c + 1], axis=1)
                                        ).then_inc(s_wdst, 16)
            for c in range(5):
                pool.indirect_dma_start(out=win_src_i[:, c, :], out_offset=None, in_=src.unsqueeze(0),
                                        in_offset=bass.IndirectOffsetOnAxis(ap=start_i[:, c:c + 1], axis=1)
                                        ).then_inc(s_wsrc, 16)

            def edge_features(c):
                ge(pool, s_wef_out, 16 * c)
                pool.indirect_dma_start(out=win_ef[:], out_offset=None,
                                        in_=ef.rearrange("a b -> (a b)").unsqueeze(0),
                                        in_offset=bass.IndirectOffsetOnAxis(ap=start_ef[:, c:c + 1], axis=1)
                                        ).then_inc(s_wef, 16)
            edge_features(0)

            def step(q, j, i):
                if not is_quad(q):
                    return
                if isinstance(q, int) and q in (4, 6, 8, 10):
                    edge_features(q // 2 - 1)
                if j % 6 == 0:
                    pool.wait_ge(s_src, i * 2 + j // 6 + 1)
                ge(pool, s_tr, q - RING + 1)
                part(pool)
                for w in range(4):
                    pool.indirect_dma_start(out=v_sb[:, j, w, 0:F], out_offset=None, in_=x,
                                            in_offset=bass.IndirectOffsetOnAxis(
                                                ap=src_now[:, j // 6, 4 * (j % 6) + w:4 * (j % 6) + w + 1], axis=0)
                                            ).then_inc(s_gath[j], 16)
            quads(pool, step, NQ - 1)

            def fix(g):
                pool.wait_ge(s_c_src, g * 16 + 16)
                part(pool)
                pool.indirect_dma_start(out=c_v[:, 0:F], out_offset=None, in_=x,
                                        in_offset=bass.IndirectOffsetOnAxis(ap=c_src[:, 0:1], axis=0)
                                        ).then_inc(s_c_gath, 16)
            repair(pool, fix)

        @block.scalar
        def _(act):
            nc.scalar.preload_act_table_set("natural_log_exp_and_others")

            def step(q, j, i):
                a, c = q - 1, q - 7
                if is_quad(q):
                    act.wait_ge(s_tr, q + 1)
                    ge(act, s_ys, q - 1)
                    nc.scalar.copy(vt_sb[:, j % 2, :, :], vt_ps)
                    ge(act, s_h, q - RING + 1)
                    nc.scalar.copy(xt_sb[:, j, :, :], xt_ps).then_inc(s_cp, 1)
                    if j % 6 == 5 and not (isinstance(q, int) and q + 7 >= NQ):
                        act.wait_ge(s_setup, 1)
                        nc.scalar.copy(src_now[:, j // 6, :], src_col[:, bass.ds((q + 7) * 4, 24)]).then_inc(s_src, 1)
                if is_quad(a):
                    act.wait_ge(s_ys, a + 1)
                    nc.scalar.copy(y_sb[:, (j - 1) % RING, :, :], y_ps).then_inc(s_ycp, 1)
                if is_batch_step(q, j, 2):
                    k = i * 3 + (j - 5) // 4
                    act.wait_ge(s_soft, k * 8 + 3)
                    nc.scalar.activation(weight[:], shifted[:], ACT.Exp).then_inc(s_exp, 1)
                e = q - 9
                if is_quad(e):
                    act.wait_ge(s_stat, e * 4 + 4)
                    nc.scalar.activation(ln_var[:, (j - 9) % 4, :], var64[:, (j - 9) % 4, :], ACT.Ln,
                                         bias=eps_col[0:PW, :], scale=1.0 / F).then_inc(s_ln, 1)
                m = q - 10
                if is_quad(m):
                    act.wait_ge(s_shift, m + 1)
                    slot, n = slot_round(j, i, 10, 3)
                    act.wait_ge(s_store[slot], 16 * n)
                    for b in range(8):
                        last = nc.scalar.activation(out_sb[:, slot, b, :], r_sb[:, (j - 10) % 4, b, :], ACT.Identity,
                                                    bias=shift[:, (j - 10) % 4, b:b + 1],
                                                    scale=rstd[:, (j - 10) % 4, b:b + 1])
                    last.then_inc(s_norm, 1)
                if is_quad(e):
                    act.wait_ge(s_ln, e * 2 + 1)
                    nc.scalar.activation(rstd[:, (j - 9) % 4, :], ln_var[:, (j - 9) % 4, :], ACT.Exp,
                                         scale=-0.5).then_inc(s_ln, 1)
            quads(act, step, NQ - 1 + 10)

            def fix(g):
                act.wait_ge(s_c_max, g + 1)
                nc.scalar.activation(scale[:], drop[:], ACT.Exp)
                for half in range(2):
                    last = nc.scalar.activation(c_exp[:, half, :], c_logit[:, half, :], ACT.Exp,
                                                bias=minus_max[:, half:half + 1])
                last.then_inc(s_c_exp, 1)
                act.wait_ge(s_c_var, g + 1)
                nc.scalar.activation(c_ln[:], c_moments[:, :, 1], ACT.Ln, bias=eps_col[0:PW, :]
                                     ).then_inc(s_c_ln, 1)
                act.wait_ge(s_c_ln, g + 1)
                nc.scalar.activation(c_rstd[:], c_ln[:], ACT.Exp, scale=-0.5).then_inc(s_c_rstd, 1)
            repair(act, fix)

        @block.tensor
        def _(pe):
            pe.wait_ge(s_ident, 2)
            pe.wait_ge(s_weights[4], 16)
            nc.tensor.transpose(bank[0][0:F, 0:F], a2_sb[:], ident[0:F, 0:F])
            pe.wait_ge(s_weights[5], 16)
            pe.wait_ge(s_weights[6], 16)
            nc.tensor.transpose(bank[0][:, 64:128], a1_twice[:], ident[0:F, 0:F]).then_inc(s_wt, 1)
            pe.wait_ge(s_a2t, 1)
            pe.wait_ge(s_weights[3], 16)
            nc.tensor.matmul(bank[1][0:FV, 0:F], proj_sb[:], a2_t[:], start=True, stop=True).then_inc(s_ew, 1)
            pe.wait_ge(s_holds, 1)
            for c in range(5):
                nc.tensor.matmul(bank[2][0:WC, c:c + 1], above_last[:, c * WC:(c + 1) * WC], ones_col[0:RQ, :],
                                 start=True, stop=True)
            for c in range(5):
                nc.tensor.matmul(bank[3 + c][0:WC, :], holds[:, c * WC:(c + 1) * WC], dst_rows[:],
                                 start=True, stop=True).then_inc(s_rows, 1)
            pe.wait_ge(s_local, 1)
            for c in range(4):
                nc.tensor.transpose(bank[0][:, c * WC:(c + 1) * WC], local[:, c, :], ident[0:WC, 0:WC])
            nc.tensor.transpose(bank[2][:, 0:WC], local[:, 4, :], ident[0:WC, 0:WC]).then_inc(s_loc_t, 1)
            pe.wait_ge(s_srcf, 1)
            for c in range(4):
                nc.tensor.transpose(bank[1][:, c * WC:(c + 1) * WC], win_src[:, c, :], ident[0:WC, 0:WC])
            nc.tensor.transpose(bank[3][:, 0:WC], win_src[:, 4, :], ident[0:WC, 0:WC]).then_inc(s_src_t, 1)
            pe.wait_ge(s_setup, 1)

            def step(q, j, i):
                a, c = q - 1, q - 7
                if is_quad(q):
                    pe.wait_ge(s_gath[j], i * 64 + 64)
                    pe.wait_ge(s_ef[j], i * 16 + 16)
                    ge(pe, s_cp, q)
                    for w in range(4):
                        nc.tensor.transpose(vt_ps[:, w, :], v_sb[:, j, w, :], ident[:])
                    pe.wait_ge(s_x[j], i * 16 + 16)
                    for w in range(4):
                        last = nc.tensor.transpose(xt_ps[:, w, :], x_sb[:, j, w, :], ident[0:PW, 0:PW])
                    last.then_inc(s_tr, 1)
                if is_quad(a):
                    pe.wait_ge(s_cp, a + 1)
                    ge(pe, s_ycp, a)
                    ge(pe, s_parts, a * 4 - 2)
                    for w in range(4):
                        nc.tensor.matmul(y_ps[:, w, :], vt_sb[:, (j - 1) % 2, w, :], edge_w[:], start=True, stop=True)
                    for w in range(4):
                        last = nc.tensor.matmul(sd_ps[:, (j - 1) % 2, 2 * w:2 * w + 2],
                                                xt_sb[:, (j - 1) % RING, w, :], attn_dst[:], start=True, stop=True)
                    last.then_inc(s_ys, 1)
                if is_quad(c):
                    h = h_ps[(j - 7) % 2]
                    ge(pe, s_r, c - 1)
                    for w in range(4):
                        at = w * 2 * F
                        nc.tensor.matmul(h[0:PW, at:at + 2 * F], xt_sb[:, (j - 7) % RING, w, :], node_w[:],
                                         start=True, stop=False)
                        if w == 0:
                            pe.wait_ge(s_hot, c + 1)
                        nc.tensor.matmul(h[0:PW, at:at + 2 * F], hot[:, (j - 7) % 2, w, :],
                                         y2[:, (j - 7) % 2, w, :, :].rearrange("p j f -> p (j f)"),
                                         start=False, stop=False)
                        last = nc.tensor.matmul(h[0:PW, at:at + 2 * F], ones3[:, 0:PW], bias3[:],
                                                start=False, stop=True)
                    last.then_inc(s_h, 1)
                if is_quad(a):
                    pe.wait_ge(s_parts, a * 4 + 4)
                    pe.wait_ge(s_hot_t, a + 1)
                    kd = (j - 1) // 4 % 3
                    if (j - 1) % 4 == 0:
                        ge(pe, s_logit, (i * 3 + (j - 1) // 4) * 3 - 2)
                    for w in range(4):
                        last = nc.tensor.matmul(ds_ps[:, kd, 4 * ((j - 1) % 4) + w, :],
                                                hot_t[:, (j - 1) % 2, w * P:(w + 1) * P],
                                                sd_parts[:, (j - 1) % 2, 2 * w:2 * w + 2, :]
                                                .rearrange("p j t -> p (j t)"), start=True, stop=True)
                    last.then_inc(s_score, 1)
                if is_batch_step(q, j, 2):
                    k = i * 3 + (j - 5) // 4
                    pe.wait_ge(s_logit, k * 3 + 3)
                    ge(pe, s_alpha, k)
                    nc.tensor.transpose(row_ps, logit_l[:], ident[:]).then_inc(s_row, 1)
                if is_batch_step(q, j, 3):
                    k = i * 3 + (j - 6) // 4
                    pe.wait_ge(s_soft, k * 8 + 8)
                    part(pe)
                    nc.tensor.transpose(col_ps, alpha_row[:], ident[0:16, 0:16]).then_inc(s_col, 1)
            quads(pe, step, NQ - 1 + 7)

            def fix(g):
                pe.wait_ge(s_c_x, g * 16 + 16)
                nc.tensor.transpose(bank[1][:, 0:PW], c_x[:], ident[0:PW, 0:PW])
                pe.wait_ge(s_c_gath, g * 16 + 16)
                pe.wait_ge(s_c_ef, g * 16 + 16)
                nc.tensor.transpose(bank[1][0:FV, P:2 * P], c_v[:], ident[:]).then_inc(s_c_tr, 1)
                pe.wait_ge(s_c_cp, g + 1)
                nc.tensor.matmul(bank[5][0:PW, 0:P], attn_src_wide[:], c_vt[:], start=True, stop=True)
                nc.tensor.matmul(bank[5][0:PW, P:P + 2], c_xt[:], attn_dst[:], start=True, stop=True)
                nc.tensor.matmul(bank[5][:, 256:256 + F], c_vt[:], edge_w[:, 0:F], start=True, stop=True
                                 ).then_inc(s_c_prod, 1)
                nc.tensor.matmul(bank[3][0:PW, 0:2 * F], c_xt[:], node_w[:], start=True, stop=False)
                nc.tensor.matmul(bank[3][0:PW, 0:2 * F], ones3[:, 0:PW], bias3[:], start=False, stop=True)
                pe.wait_ge(s_c_weight, g + 1)
                for half in range(2):
                    last = nc.tensor.transpose(bank[1][:, half * PW:(half + 1) * PW], c_weight[:, half, :],
                                               ident[0:PW, 0:PW])
                last.then_inc(s_c_wt, 1)
                pe.wait_ge(s_c_wcp, g + 1)
                for half in range(2):
                    last = nc.tensor.matmul(bank[4][0:PW, half * F:(half + 1) * F], c_weight_t[:, half, :], c_y[:],
                                            start=True, stop=True)
                last.then_inc(s_c_z, 1)
            repair(pe, fix)

        @block.vector
        def _(dve):
            steps = [0]

            def done(ins):
                steps[0] += 1
                ins.then_inc(s_ds, 1)
                dve.wait_ge(s_ds, steps[0])

            nc.vector.memset(prev_i[:], -1)
            nc.vector.memset(node_w[:], 0.0)
            nc.vector.memset(edge_w[:, F:F + 1], 0.0)
            nc.vector.memset(attn_dst[:], 0.0)
            nc.vector.memset(ones_col[:], 1.0)
            nc.vector.memset(ones3[:], 1.0)
            nc.vector.memset(eps_col[:], EPS)
            nc.vector.memset(same, 0.0)
            nc.vector.memset(dst_rows_i[:], PAD_NODE).then_inc(s_pad, 1)
            dve.wait_ge(s_iota, 1)
            nc.vector.tensor_copy(ident[:], iota_i[:, 0:P]).then_inc(s_ident, 1)
            dve.wait_ge(s_ident, 1)
            nc.vector.tensor_scalar(ident[:], ident[:], 0.0, None, ALU.is_equal).then_inc(s_ident, 1)
            dve.wait_ge(s_iota, 6)
            nc.vector.tensor_copy(order[:], order_i[:])
            nc.vector.tensor_copy(node_id[:], node_i[:])
            nc.vector.tensor_copy(base[:], base_i[:])
            nc.vector.tensor_copy(part_f[:], part_i[:])
            nc.vector.tensor_copy(starts[:], iota_i[:])
            for s in range(3):
                dve.wait_ge(s_weights[s], 16)
            nc.vector.tensor_copy(dst_rows[:], dst_rows_i[:])
            done(nc.vector.tensor_copy(prev_f[:], prev_i[:]))
            nc.vector.tensor_scalar(above_last[:], starts[0:RQ, :], dst_rows[:, 511:512], None, ALU.is_gt)
            done(nc.vector.tensor_scalar(holds[:], starts[0:RQ, :], prev_f[:], None, ALU.is_gt))
            nc.vector.tensor_tensor(holds[:], holds[:], above_last[:], ALU.subtract).then_inc(s_holds, 1)
            dve.wait_ge(s_wt, 1)
            nc.vector.tensor_copy(a2_t[:], bank[0][0:F, 0:F]).then_inc(s_a2t, 1)
            nc.vector.tensor_copy(node_w[0:F, 0:F], bank[0][0:F, 64:128])
            nc.vector.tensor_copy(node_w[F:P, F:2 * F], bank[0][F:P, 64:128])
            for c in range(5):
                dve.wait_ge(s_rows, c + 1)
                done(nc.vector.tensor_scalar(below[:], bank[3 + c][0:WC, :], base[0:WC, c:c + 1], None, ALU.is_lt,
                                             ALU.add, accum_out=count_in_row[:, c:c + 1]))
            done(nc.vector.scalar_tensor_tensor(first_edge[:], bank[2][0:WC, 0:5], 512.0, count_in_row[:],
                                                ALU.mult, ALU.add))
            done(nc.vector.tensor_scalar(start_f[:], first_edge[:], float(N_EDGES - P), None, ALU.min))
            nc.vector.tensor_copy(start_i[:], start_f[:])
            nc.vector.tensor_scalar(start_ef[:], start_f[:], float(FE), None, ALU.mult).then_inc(s_starts, 1)
            dve.wait_ge(s_ew, 1)
            dve.wait_ge(s_weights[7], 16)
            nc.vector.tensor_copy(edge_w[:, 0:F], bank[1][0:FV, 0:F])
            dve.wait_ge(s_weights[10], 16)
            done(nc.vector.tensor_copy(bias_hi[:], bias_f[:]))
            done(nc.vector.tensor_tensor(bias_rest[:], bias_f[:], bias_hi[:], ALU.subtract))
            done(nc.vector.tensor_copy(bias_mid[:], bias_rest[:]))
            nc.vector.tensor_tensor(bias_lo[:], bias_rest[:], bias_mid[:], ALU.subtract)
            for k in range(3):
                last = nc.vector.tensor_scalar(pick[:, k:k + 1], part_f[0:3, :], float(k), None, ALU.is_equal)
            done(last)
            done(nc.vector.tensor_scalar(bias_sum[:], bias_hi[:], pick[:, 0:1], None, ALU.mult))
            done(nc.vector.scalar_tensor_tensor(bias_sum[:], bias_mid[:], pick[:, 1:2], bias_sum[:],
                                                ALU.mult, ALU.add))
            done(nc.vector.scalar_tensor_tensor(bias_sum[:], bias_lo[:], pick[:, 2:3], bias_sum[:],
                                                ALU.mult, ALU.add))
            nc.vector.tensor_copy(bias3[:, 0:F], bias_sum[:])
            done(nc.vector.tensor_copy(bias3[:, F:2 * F], bias_sum[:]))
            dve.wait_ge(s_wdst, 80)
            done(nc.vector.tensor_copy(win_dst[:], win_dst_i[:]))
            for c in range(5):
                last = nc.vector.tensor_scalar(local[:, c, :], win_dst[:, c, :], base[0:WC, c:c + 1], -1.0,
                                               ALU.subtract, ALU.max)
            done(last)
            nc.vector.tensor_scalar(local[:], local[:], float(NPB), None, ALU.min).then_inc(s_local, 1)
            dve.wait_ge(s_local, 1)
            nc.vector.tensor_copy(local16[:], local[:]).then_inc(s_local16, 1)
            done(nc.vector.tensor_copy(pair_i[:], local[:]))
            done(nc.vector.tensor_scalar(pair_i[:], pair_i[:], 1, None, ALU.arith_shift_right))
            nc.vector.tensor_copy(pair16[:], pair_i[:]).then_inc(s_pair16, 1)
            dve.wait_ge(s_wsrc, 80)
            nc.vector.tensor_copy(win_src[:], win_src_i[:]).then_inc(s_srcf, 1)
            dve.wait_ge(s_loc_t, 1)
            nc.vector.tensor_copy(local_col[:, 0:4 * WC], bank[0][:, 0:4 * WC])
            nc.vector.tensor_copy(local_col[:, 4 * WC:NWP], bank[2][:, 0:WC])
            dve.wait_ge(s_src_t, 1)
            nc.vector.tensor_copy(src_col[:, 0:4 * WC], bank[1][:, 0:4 * WC])
            done(nc.vector.tensor_copy(src_col[:, 4 * WC:NWP], bank[3][:, 0:WC]))
            dve.wait_ge(s_weights[8], 32)
            dve.wait_ge(s_weights[9], 16)
            nc.vector.tensor_copy(src_now[:].rearrange("p h c -> p (h c)"), src_col[:, 0:48]).then_inc(s_src, 2)
            nc.vector.memset(alpha[:], 0.0).then_inc(s_setup, 1)
            done(nc.vector.tensor_copy(pair_col_i[:], local_col[:]))
            done(nc.vector.tensor_scalar(pair_col_i[:], pair_col_i[:], 1, None, ALU.arith_shift_right))
            done(nc.vector.tensor_copy(pair_col[:], pair_col_i[:]))
            done(nc.vector.scalar_tensor_tensor(parity[:, :, 1], pair_col[:], -2.0, local_col[:],
                                                ALU.mult, ALU.add))
            nc.vector.tensor_scalar(parity[:, :, 0], parity[:, :, 1], -1.0, 1.0, ALU.mult, ALU.add)
            dve.wait_ge(s_batch_local, 16)
            done(nc.vector.tensor_tensor(same[:, :, 1:P], batch_local[:, :, 1:P], batch_local[:, :, 0:P - 1],
                                         ALU.is_equal))
            nc.vector.tensor_scalar(apart, same, -1.0, 1.0, ALU.mult, ALU.add)
            done(nc.vector.tensor_scalar(wall, same, -1.0, BIG, ALU.add, ALU.mult))

            def step(q, j, i):
                a, c, e, m = q - 1, q - 7, q - 8, q - 10
                if is_quad(m):
                    dve.wait_ge(s_ln, m * 2 + 2)
                    nc.vector.scalar_tensor_tensor(shift[:, (j - 10) % 4, :], mean2[:, (j - 10) % 4, :], -0.5,
                                                   rstd[:, (j - 10) % 4, :], ALU.mult, ALU.mult
                                                   ).then_inc(s_shift, 1)
                if is_quad(c):
                    kc, at = (j - 7) // 4, 4 * ((j - 7) % 4)
                    ge(dve, s_h, c - 1)
                    nc.vector.tensor_tensor(hot[:, (j - 7) % 2, :, :],
                                            order[:].unsqueeze(1).to_broadcast([P, 4, PW]),
                                            pair_col[:, bass.ds(c * 4, 4)].unsqueeze(2).to_broadcast([P, 4, PW]),
                                            ALU.is_equal)
                    dve.wait_ge(s_alpha, i * 3 + kc + 1)
                    nc.vector.tensor_tensor(y2[:, (j - 7) % 2, :, :, :],
                                            y_sb[:, (j - 7) % RING, :, 0:F].unsqueeze(2)
                                            .to_broadcast([P, 4, 2, F]),
                                            alpha[:, kc % 3, at:at + 4, :].unsqueeze(3).to_broadcast([P, 4, 2, F]),
                                            ALU.mult).then_inc(s_hot, 1)
                if is_quad(e):
                    dve.wait_ge(s_h, e + 1)
                    ge(dve, s_norm, e - 3)
                    nc.vector.scalar_tensor_tensor(r_sb[:, (j - 8) % 4, :, :].rearrange("p c f -> p (c f)"),
                                                   h_ps[(j - 8) % 2][0:PW, :], 0.0,
                                                   x_sb[:, (j - 8) % RING, :, :].rearrange("p w f -> p (w f)"),
                                                   ALU.max, ALU.add).then_inc(s_r, 1)
                if is_quad(a):
                    slot, n = slot_round(j, i, 1, 4)
                    dve.wait_ge(s_loc[slot], n * 16)
                    ge(dve, s_score, a - 1)
                    nc.vector.tensor_scalar(hot_t[:, (j - 1) % 2, :], pair_b[:, slot, :], part_f[0:PW, :], None,
                                            ALU.is_equal).then_inc(s_hot_t, 1)
                    part = [sd_parts[:, (j - 1) % 2, :, t] for t in range(3)]
                    dve.wait_ge(s_ys, a + 1)
                    nc.vector.tensor_copy(part[0], sd_ps[:, (j - 1) % 2, :]).then_inc(s_parts, 1)
                if is_quad(e):
                    dve.wait_ge(s_r, e + 1)
                    for b in range(4):
                        nc.vector.bn_stats(stats[:, (j - 8) % 4, b, :], r_sb[:, (j - 8) % 4, b, :])
                if is_quad(a):
                    dve.wait_ge(s_parts, a * 4 + 1)
                    nc.vector.tensor_tensor(sd_rest[:, (j - 1) % 2, :], sd_ps[:, (j - 1) % 2, :], part[0],
                                            ALU.subtract).then_inc(s_parts, 1)
                if is_quad(e):
                    for b in range(4, 6):
                        nc.vector.bn_stats(stats[:, (j - 8) % 4, b, :], r_sb[:, (j - 8) % 4, b, :])
                if is_quad(a):
                    dve.wait_ge(s_parts, a * 4 + 2)
                    nc.vector.tensor_copy(part[1], sd_rest[:, (j - 1) % 2, :]).then_inc(s_parts, 1)
                if is_quad(e):
                    for b in range(6, 8):
                        last = nc.vector.bn_stats(stats[:, (j - 8) % 4, b, :], r_sb[:, (j - 8) % 4, b, :])
                    last.then_inc(s_stat, 1)
                if is_quad(a):
                    dve.wait_ge(s_parts, a * 4 + 3)
                    nc.vector.tensor_tensor(part[2], sd_rest[:, (j - 1) % 2, :], part[1],
                                            ALU.subtract).then_inc(s_parts, 1)
                if is_batch_step(q, j, 2):
                    k = i * 3 + (j - 5) // 4

                    same_now, apart_now, wall_now = [links_now[:, t, :] for t in range(3)]
                    dve.wait_ge(s_links, k + 1)
                    dve.wait_ge(s_row, k + 1)
                    nc.vector.tensor_tensor_scan(run_max[:], wall_now[:, 0:P], row_ps, -BIG, ALU.add, ALU.max
                                                 ).then_inc(s_soft, 1)
                    dve.wait_ge(s_soft, k * 8 + 1)
                    nc.vector.tensor_tensor_scan(seg_max[:, ::-1], wall_now[:, P:0:-1], run_max[:, ::-1], -BIG, ALU.add,
                                                 ALU.max).then_inc(s_soft, 1)
                    dve.wait_ge(s_soft, k * 8 + 2)
                    nc.vector.tensor_tensor(shifted[:], row_ps, seg_max[:], ALU.subtract).then_inc(s_soft, 1)
                if is_quad(e):
                    st = stats[:, (j - 8) % 4, :, :]
                    dve.wait_ge(s_stat, e * 4 + 1)
                    nc.vector.tensor_tensor(halves[:, (j - 8) % 4, :], st[:, :, 1], st[:, :, 4], ALU.subtract)
                    nc.vector.tensor_tensor(mean2[:, (j - 8) % 4, :], st[:, :, 1], st[:, :, 4], ALU.add)
                    nc.vector.tensor_tensor(moment[:, (j - 8) % 4, :], st[:, :, 2], st[:, :, 5],
                                            ALU.add).then_inc(s_stat, 1)
                    dve.wait_ge(s_stat, e * 4 + 2)
                    nc.vector.scalar_tensor_tensor(spread[:, (j - 8) % 4, :], halves[:, (j - 8) % 4, :], F / 4.0,
                                                   halves[:, (j - 8) % 4, :], ALU.mult, ALU.mult
                                                   ).then_inc(s_stat, 1)
                    dve.wait_ge(s_stat, e * 4 + 3)
                    nc.vector.tensor_tensor(var64[:, (j - 8) % 4, :], spread[:, (j - 8) % 4, :],
                                            moment[:, (j - 8) % 4, :], ALU.add).then_inc(s_stat, 1)
                if is_batch_step(q, j, 2):
                    dve.wait_ge(s_exp, k + 1)
                    nc.vector.tensor_tensor_scan(run_sum[:], same_now[:, 0:P], weight[:], 0.0, ALU.mult, ALU.add
                                                 ).then_inc(s_soft, 1)
                    dve.wait_ge(s_soft, k * 8 + 4)
                    nc.vector.tensor_tensor(last_sum[:], run_sum[:], apart_now[:, 1:P + 1], ALU.mult).then_inc(s_soft, 1)
                    dve.wait_ge(s_soft, k * 8 + 5)
                    nc.vector.tensor_tensor_scan(seg_sum[:, ::-1], same_now[:, P:0:-1], last_sum[:, ::-1], 0.0,
                                                 ALU.mult, ALU.add).then_inc(s_soft, 1)
                    dve.wait_ge(s_soft, k * 8 + 6)
                    nc.vector.reciprocal(seg_rcp[:], seg_sum[:]).then_inc(s_soft, 1)
                    dve.wait_ge(s_soft, k * 8 + 7)
                    ge(dve, s_col, k)
                    nc.vector.tensor_tensor(alpha_row[:], weight[:], seg_rcp[:], ALU.mult).then_inc(s_soft, 1)
                if is_batch_step(q, j, 1):
                    k = i * 3 + (j - 4) // 4
                    sl = (j - 4) % RING
                    upto = min(q, NQ) if isinstance(q, int) else q
                    dve.wait_ge(s_score, upto)
                    dve.wait_ge(s_ycp, upto)
                    nc.vector.tensor_tensor(ds_parts[:].rearrange("p w (j t) -> p w j t", j=2),
                                            ds_ps[:, (j - 4) // 4 % 3, :, :].rearrange("p w (j t) -> p w j t", j=2),
                                            parity[:, bass.ds(k * 16, 16), :].unsqueeze(3)
                                            .to_broadcast([P, 16, 2, 3]), ALU.mult).then_inc(s_dst_part, 1)
                    dve.wait_ge(s_dst_part, k + 1)
                    nc.vector.tensor_reduce(dst_score[:], ds_parts[:], AX.X, ALU.add).then_inc(s_logit, 1)
                    nc.vector.tensor_copy(links_now[:].rearrange("p t e -> p (t e)"),
                                          links[:, bass.ds(k, 1), :, :].rearrange("p o t e -> p (o t e)")
                                          ).then_inc(s_links, 1)
                    dve.wait_ge(s_logit, k * 3 + 1)
                    nc.vector.scalar_tensor_tensor(logit[:].rearrange("p (a w) -> p a w", w=4),
                                                   dst_score[:].rearrange("p (a w) -> p a w", w=4), attn_b_col[:],
                                                   y_sb[:, sl:sl + 4, :, F], ALU.add, ALU.add).then_inc(s_logit, 1)
                    dve.wait_ge(s_logit, k * 3 + 2)
                    ge(dve, s_row, k)
                    nc.vector.scalar_tensor_tensor(logit_l[:], logit[:], LEAK, logit[:], ALU.mult, ALU.max
                                                   ).then_inc(s_logit, 1)
                if is_batch_step(q, j, 3):
                    k = i * 3 + (j - 6) // 4
                    dve.wait_ge(s_col, k + 1)
                    nc.vector.tensor_tensor(alpha[:, (j - 6) // 4 % 3, :, :],
                                            col_ps.unsqueeze(2).to_broadcast([P, 16, 2]),
                                            parity[:, bass.ds(k * 16, 16), :], ALU.mult).then_inc(s_alpha, 1)
            quads(dve, step, NQ - 1 + 10)

            dve.wait_ge(s_first_row, 16)
            nc.vector.memset(ones_row[:], 1.0)
            nc.vector.tensor_copy(begin[:], first_row[:, 0:NW])
            done(nc.vector.tensor_tensor(n_edges[:], first_row[:, 1:NW + 1], first_row[:, 0:NW], ALU.subtract))
            nc.vector.tensor_copy(begin[:, NW - 1:NW], first_row[:, NW - 2:NW - 1])
            done(nc.vector.tensor_scalar(crowded[:], n_edges[:], float(P), None, ALU.is_gt))
            done(nc.vector.scalar_tensor_tensor(span_i[:], first_row[:, 1:NW + 1], float(P - 1), begin[:],
                                                ALU.add, ALU.subtract))
            done(nc.vector.tensor_scalar(span_i[:], span_i[:], 7, None, ALU.arith_shift_right))
            done(nc.vector.tensor_tensor(n_chunks[:], span_i[:], crowded[:], ALU.mult))
            done(nc.vector.tensor_tensor_scan(chunks_to[:], ones_row[:], n_chunks[:], 0.0, ALU.mult, ALU.add))
            nc.vector.tensor_copy(total_i[:], chunks_to[:, NW - 1:NW]).then_inc(s_total, 1)
            done(nc.vector.tensor_tensor(rest[:], n_chunks[:], chunks_to[:], ALU.subtract))
            nc.vector.scalar_tensor_tensor(key[:], rest[:], float(P), begin[:], ALU.mult, ALU.add)
            nc.vector.tensor_copy(attn_src_wide[:], edge_w[:, F:F + 1].to_broadcast([FV, PW]))
            nc.vector.memset(chunk_no[:], 0.0)
            nc.vector.memset(last_node[:], -1.0)
            nc.vector.memset(new_max[:], -BIG)
            nc.vector.memset(z_sum[:], 0.0)
            dve.wait_ge(s_norm, NQ)
            done(nc.vector.memset(z_acc[:], 0.0))

            def fix(g):
                fixed = [0]

                def then(ins):
                    fixed[0] += 1
                    ins.then_inc(s_fix, 1)
                    dve.wait_ge(s_fix, g * FIX_STEPS + fixed[0])

                then(nc.vector.tensor_scalar(rest[:], chunks_to[:], chunk_no[:], None, ALU.is_le, ALU.add,
                                             accum_out=block_no[:]))
                then(nc.vector.tensor_scalar(block_node[:], block_no[:], float(NPB), None, ALU.mult))
                then(nc.vector.tensor_scalar(rest[:], starts[:, 0:NW], block_node[:], None, ALU.is_equal))
                then(nc.vector.tensor_tensor(rest[:], rest[:], key[:], ALU.mult))
                then(nc.vector.tensor_reduce(block_key[:], rest[:], AX.X, ALU.add))
                then(nc.vector.scalar_tensor_tensor(chunk_begin[:], chunk_no[:], float(P), block_key[:],
                                                    ALU.mult, ALU.add))
                then(nc.vector.tensor_scalar(chunk_edge[:], chunk_begin[:], float(N_EDGES - P), None, ALU.min))
                then(nc.vector.tensor_scalar(chunk_node[:], block_node[:], float(N_NODES - NPB), None, ALU.min))
                nc.vector.tensor_copy(chunk_i[:, 0:1], chunk_edge[:])
                nc.vector.tensor_copy(chunk_i[:, 1:2], chunk_node[:]).then_inc(s_where, 1)
                nc.vector.tensor_scalar(node_now[:], node_id[:], chunk_node[:], None, ALU.add)
                nc.vector.tensor_tensor(goes_on[:], block_node[:], last_node[:], ALU.is_equal)
                then(nc.vector.tensor_tensor(overlap[:], chunk_begin[:], chunk_edge[:], ALU.subtract))
                nc.vector.tensor_scalar(overlap[:], overlap[:], float(NPB), None, ALU.mult)
                nc.vector.tensor_copy(last_node[:], block_node[:])
                nc.vector.tensor_scalar(chunk_no[:], chunk_no[:], 1.0, None, ALU.add)
                then(nc.vector.tensor_scalar(reset[:], goes_on[:], -1.0, BIG, ALU.add, ALU.mult))
                nc.vector.tensor_scalar(old_max[:], new_max[:], goes_on[0:PW, :], reset[0:PW, :],
                                        ALU.mult, ALU.add)
                then(nc.vector.tensor_scalar(valid[:], starts[:, 0:P], overlap[:], None, ALU.is_ge))
                dve.wait_ge(s_c_dst, g * 16 + 16)
                then(nc.vector.tensor_copy(c_dst[:], c_dst_i[:]))
                for half in range(2):
                    last = nc.vector.scalar_tensor_tensor(c_mask[:, half, :], c_dst[:],
                                                          node_now[0:PW, half:half + 1], valid[0:PW, :],
                                                          ALU.is_equal, ALU.mult)
                then(last)
                nc.vector.tensor_scalar(c_wall[:], c_mask[:], -1.0, BIG, ALU.add, ALU.mult)
                dve.wait_ge(s_c_tr, g + 1)
                nc.vector.tensor_copy(c_xt[:], bank[1][:, 0:PW])
                nc.vector.tensor_copy(c_vt[:], bank[1][0:FV, P:2 * P]).then_inc(s_c_cp, 1)
                dve.wait_ge(s_c_prod, g + 1)
                nc.vector.tensor_copy(c_y[:], bank[5][:, 256:256 + F])
                then(nc.vector.tensor_scalar(c_own[:], bank[5][0:PW, P:P + 2], attn_b_col[0:PW, :], None, ALU.add))
                for half in range(2):
                    last = nc.vector.tensor_scalar(c_logit[:, half, :], bank[5][0:PW, 0:P],
                                                   c_own[:, half:half + 1], None, ALU.add)
                then(last)
                then(nc.vector.scalar_tensor_tensor(c_leaky[:], c_logit[:], LEAK, c_logit[:], ALU.mult, ALU.max))
                then(nc.vector.tensor_tensor(c_leaky[:], c_leaky[:], c_mask[:], ALU.mult))
                then(nc.vector.tensor_tensor(c_logit[:], c_leaky[:], c_wall[:], ALU.add))
                then(nc.vector.tensor_reduce(c_max[:], c_logit[:], AX.X, ALU.max))
                then(nc.vector.tensor_tensor(new_max[:], old_max[:], c_max[:], ALU.max))
                nc.vector.tensor_scalar(minus_max[:], new_max[:], -1.0, None, ALU.mult)
                nc.vector.tensor_tensor(drop[:], old_max[:], new_max[:], ALU.subtract).then_inc(s_c_max, 1)
                dve.wait_ge(s_c_exp, g + 1)
                nc.vector.tensor_tensor(c_weight[:], c_exp[:], c_mask[:], ALU.mult).then_inc(s_c_weight, 1)
                dve.wait_ge(s_c_weight, g + 1)
                nc.vector.tensor_reduce(c_sum[:], c_weight[:], AX.X, ALU.add)
                then(nc.vector.tensor_scalar(scale[:], scale[:], goes_on[0:PW, :], None, ALU.mult))
                then(nc.vector.tensor_tensor(z_sum[:], z_sum[:], scale[:], ALU.mult))
                then(nc.vector.tensor_tensor(z_sum[:], z_sum[:], c_sum[:], ALU.add))
                then(nc.vector.scalar_tensor_tensor(divisor[:], z_sum[:], 0.0, z_sum[:], ALU.is_equal, ALU.add))
                then(nc.vector.reciprocal(inverse[:], divisor[:]))
                dve.wait_ge(s_c_wt, g + 1)
                nc.vector.tensor_copy(c_weight_t[:].rearrange("p j n -> p (j n)"), bank[1][:, 0:2 * PW]
                                      ).then_inc(s_c_wcp, 1)
                dve.wait_ge(s_c_z, g + 1)
                for half in range(2):
                    last = nc.vector.scalar_tensor_tensor(z_acc[:, half, :], z_acc[:, half, :],
                                                          scale[:, half:half + 1],
                                                          bank[4][0:PW, half * F:(half + 1) * F],
                                                          ALU.mult, ALU.add)
                then(last)
                for half in range(2):
                    last = nc.vector.scalar_tensor_tensor(c_h[:, half, :], z_acc[:, half, :],
                                                          inverse[:, half:half + 1],
                                                          bank[3][0:PW, half * F:(half + 1) * F],
                                                          ALU.mult, ALU.add)
                then(last)
                then(nc.vector.scalar_tensor_tensor(c_r[:].rearrange("p j f -> p (j f)"),
                                                    c_h[:].rearrange("p j f -> p (j f)"), 0.0, c_x[:],
                                                    ALU.max, ALU.add))
                for half in range(2):
                    last = nc.vector.bn_stats(c_stats[:, half, :], c_r[:, half, :])
                then(last)
                part(dve)
                for half in range(2):
                    last = nc.vector.bn_aggr(c_moments[:, half, :], c_stats[:, half, :])
                last.then_inc(s_c_var, 1)
                dve.wait_ge(s_c_rstd, g + 1)
                for half in range(2):
                    last = nc.vector.tensor_scalar(c_out[:, half, :], c_r[:, half, :], c_moments[:, half, 0:1],
                                                   c_rstd[:, half:half + 1], ALU.subtract, ALU.mult)
                last.then_inc(s_c_out, 1)
                assert fixed[0] == FIX_STEPS, fixed[0]
            repair(dve, fix)


_INS = ["x", "src", "dst", "edge_attr_32", "L0_gnn_proj_w", "L0_gnn_attn_w", "L0_gnn_attn_b", "L0_gnn_apply_w",
        "L0_gnn_apply_b"]


def kernel(**inputs):
    import numpy as _np
    import concourse.bacc as _bacc
    from concourse import mybir as _mybir
    from concourse.bass_utils import run_bass_kernel_spmd as _run

    nc = _bacc.Bacc("TRN2", target_bir_lowering=False, num_devices=1)
    arrays, args = {}, []
    for name in _INS:
        a = _np.ascontiguousarray(inputs[name])
        arrays[f"in_{name}"] = a
        args.append(nc.dram_tensor(f"in_{name}", a.shape, _mybir.dt.from_np(a.dtype), kind="ExternalInput").ap())
    args.append(nc.dram_tensor("out_0", (N_NODES, F), _mybir.dt.float32, kind="ExternalOutput").ap())
    gnn_kernel(nc, *args)
    r = _run(nc, [arrays], core_ids=[0])
    return r.results[0]["out_0"]
```

```python
import concourse.bass as bass
from concourse import mybir
from contextlib import ExitStack

FP32, BF16, I32 = mybir.dt.float32, mybir.dt.bfloat16, mybir.dt.int32
ALU, ACT, AX = mybir.AluOpType, mybir.ActivationFunctionType, mybir.AxisListType

P = 128
N_NODES, N_EDGES, F, FE = 100000, 50000, 64, 32
FV = F + FE
NPB = 192
PW = NPB // 2
NW = -(-N_NODES // NPB)
NQ = -(-NW // 4)
LAST_NODES = N_NODES - (NW - 1) * NPB
RING = 12
NSB = -(-NQ // 4)
WC = -(-NSB * 16 // 5)
NWP = 5 * WC
RQ = -(-N_EDGES // 512)
R_TAIL = N_EDGES - (RQ - 1) * 512
PAD_NODE = 131072
BIG = 1.0e30
EPS = 1.0e-5
LEAK = 0.2


def gnn_kernel(nc, x, src, dst, ef, proj_w, attn_w, attn_b, apply_w, apply_b, out):
    ef_scratch = nc.dram_tensor("ef_scratch", (NWP, P * FE), FP32, kind="Internal").ap()
    pair_scratch = nc.dram_tensor("pair_scratch", (NWP, P), BF16, kind="Internal").ap()
    local_scratch = nc.dram_tensor("local_scratch", (NWP, P), BF16, kind="Internal").ap()
    first_scratch = nc.dram_tensor("first_scratch", (NWP,), FP32, kind="Internal").ap()

    ctx = ExitStack()
    with ctx:
        def sb(name, shape, dt=FP32):
            return ctx.enter_context(nc.sbuf_tensor(name, shape, dt))

        def sem(name):
            return ctx.enter_context(nc.semaphore(name))

        bank = [ctx.enter_context(nc.psum_tensor(f"bank{i}", [P, 512], FP32)) for i in range(8)]

        iota_i = sb("iota_i", [P, NWP], I32)
        ident = sb("ident", [P, P])
        order_i = sb("order_i", [P, PW], I32)
        order = sb("order", [P, PW])
        node_i = sb("node_i", [P, 2], I32)
        node_id = sb("node_id", [P, 2])
        base_i = sb("base_i", [P, 5], I32)
        base = sb("base", [P, 5])
        starts = sb("starts", [P, NWP])
        part_i = sb("part_i", [P, 1], I32)
        part_f = sb("part_f", [P, 1])
        pair_col_i = iota_i
        ones_col = sb("ones_col", [P, 1])
        ones3 = sb("ones3", [3, P], BF16)
        eps_col = sb("eps_col", [P, 1])
        proj_sb = sb("proj_sb", [F, FV])
        a1_twice = sb("a1_twice", [F, 2 * F])
        a2_sb = sb("a2_sb", [F, F])
        a2_t = sb("a2_t", [F, F])
        edge_w = sb("edge_w", [FV, P])
        node_w = sb("node_w", [P, 2 * F])
        attn_dst = sb("attn_dst", [P, PW])
        attn_b_col = sb("attn_b_col", [P, 1])
        bias_f = sb("bias_f", [3, F])
        bias_rest = sb("bias_rest", [3, F])
        bias_lo = sb("bias_lo", [3, F])
        bias_sum = sb("bias_sum", [3, F])
        bias_hi = sb("bias_hi", [3, F], BF16)
        bias_mid = sb("bias_mid", [3, F], BF16)
        bias3 = sb("bias3", [3, 2 * F], BF16)
        pick = sb("pick", [3, 3])
        local_col = sb("local_col", [P, NWP])
        pair_col = sb("pair_col", [P, NWP])
        parity = sb("parity", [P, NWP, 2])
        src_col = sb("src_col", [P, NWP], I32)
        links = sb("links", [16, NSB, 3, P + 1], BF16)
        same = links[:, :, 0, :]
        apart = links[:, :, 1, :]
        wall = links[:, :, 2, :]
        links_now = sb("links_now", [16, 3, P + 1], BF16)
        first_row = sb("first_row", [P, NWP])
        src_now = sb("src_now", [P, 2, 24], I32)
        v_sb = sb("v_sb", [P, RING, 4, FV])
        x_sb = sb("x_sb", [PW, RING, 4, 2 * F])
        vt_sb = sb("vt_sb", [FV, 2, 4, P])
        xt_sb = sb("xt_sb", [P, RING, 4, PW])
        y_sb = sb("y_sb", [P, RING, 4, F + 1])
        pair_b = sb("pair_b", [PW, 4, 4 * P], BF16)
        hot_t = sb("hot_t", [PW, 2, 4 * P], BF16)
        sd_rest = sb("sd_rest", [PW, 2, 8])
        sd_parts = sb("sd_parts", [PW, 2, 8, 3], BF16)
        ds_parts = sb("ds_parts", [P, 16, 6])
        dst_score = sb("dst_score", [P, 16])
        logit = sb("logit", [P, 16])
        logit_l = sb("logit_l", [P, 16])
        run_max = sb("run_max", [16, P])
        seg_max = sb("seg_max", [16, P])
        shifted = sb("shifted", [16, P])
        weight = sb("weight", [16, P])
        run_sum = sb("run_sum", [16, P])
        last_sum = sb("last_sum", [16, P])
        seg_sum = sb("seg_sum", [16, P])
        col_rcp = sb("col_rcp", [P, 16])
        col_alpha = sb("col_alpha", [P, 16])
        alpha = sb("alpha", [P, 3, 16, 2])
        hot = sb("hot", [P, 2, 4, PW])
        y2 = sb("y2", [P, 2, 4, 2, F])
        r_sb = sb("r_sb", [PW, 4, 8, F])
        stats = sb("stats", [PW, 4, 8, 6])
        mean2 = sb("mean2", [PW, 4, 8])
        halves = sb("halves", [PW, 4, 8])
        moment = sb("moment", [PW, 4, 8])
        spread = sb("spread", [PW, 4, 8])
        var64 = sb("var64", [PW, 4, 8])
        ln_var = sb("ln_var", [PW, 4, 8])
        rstd = sb("rstd", [PW, 4, 8])
        shift = sb("shift", [PW, 4, 8])
        out_sb = sb("out_sb", [PW, 3, 8, F])

        early = ExitStack()

        def sb_early(name, shape, dt=FP32):
            return early.enter_context(nc.sbuf_tensor(name, shape, dt))

        dst_rows_i = sb_early("dst_rows_i", [RQ, 512], I32)
        dst_rows = sb_early("dst_rows", [RQ, 512])
        prev_i = sb_early("prev_i", [RQ, 1], I32)
        prev_f = sb_early("prev_f", [RQ, 1])
        above_last = sb_early("above_last", [RQ, NWP])
        holds = sb_early("holds", [RQ, NWP])
        below = sb_early("below", [WC, 512])
        count_in_row = sb_early("count_in_row", [WC, 5])
        first_edge = sb_early("first_edge", [WC, 5])
        start_f = sb_early("start_f", [WC, 5])
        start_i = sb_early("start_i", [WC, 5], I32)
        start_ef = sb_early("start_ef", [WC, 5], I32)
        win_dst_i = sb_early("win_dst_i", [WC, 5, P], I32)
        win_src_i = sb_early("win_src_i", [WC, 5, P], I32)
        win_dst = sb_early("win_dst", [WC, 5, P])
        win_src = win_dst
        win_ef = sb_early("win_ef", [WC, P * FE])
        local = sb_early("local", [WC, 5, P])
        local16 = sb_early("local16", [WC, 5, P], BF16)
        pair_i = win_dst_i
        pair16 = sb_early("pair16", [WC, 5, P], BF16)
        batch_local = sb_early("batch_local", [16, NSB, P], BF16)
        early.close()
        n_edges = sb("n_edges", [P, NW])
        crowded = sb("crowded", [P, NW])
        begin = sb("begin", [P, NW])
        span_i = sb("span_i", [P, NW], I32)
        rest = sb("rest", [P, NW])
        n_chunks = sb("n_chunks", [P, NW])
        ones_row = sb("ones_row", [P, NW])
        chunks_to = sb("chunks_to", [P, NW])
        key = sb("key", [P, NW])
        total_i = sb("total_i", [P, 1], I32)
        chunk_no = sb("chunk_no", [P, 1])
        block_no = sb("block_no", [P, 1])
        block_node = sb("block_node", [P, 1])
        last_node = sb("last_node", [P, 1])
        block_key = sb("block_key", [P, 1])
        chunk_begin = sb("chunk_begin", [P, 1])
        chunk_edge = sb("chunk_edge", [P, 1])
        chunk_node = sb("chunk_node", [P, 1])
        overlap = sb("overlap", [P, 1])
        goes_on = sb("goes_on", [P, 1])
        reset = sb("reset", [P, 1])
        chunk_i = sb("chunk_i", [P, 2], I32)
        node_now = sb("node_now", [P, 2])
        c_dst_i = sb("c_dst_i", [PW, P], I32)
        c_dst = sb("c_dst", [PW, P])
        c_src = sb("c_src", [P, 1], I32)
        c_v = sb("c_v", [P, FV])
        c_x = sb("c_x", [PW, 2 * F])
        c_vt = sb("c_vt", [FV, P])
        c_xt = sb("c_xt", [P, PW])
        c_y = sb("c_y", [P, F])
        attn_src_wide = sb("attn_src_wide", [FV, PW])
        valid = sb("valid", [P, P])
        c_mask = sb("c_mask", [PW, 2, P])
        c_wall = sb("c_wall", [PW, 2, P])
        c_own = sb("c_own", [PW, 2])
        c_logit = sb("c_logit", [PW, 2, P])
        c_leaky = sb("c_leaky", [PW, 2, P])
        c_max = sb("c_max", [PW, 2])
        old_max = sb("old_max", [PW, 2])
        new_max = sb("new_max", [PW, 2])
        minus_max = sb("minus_max", [PW, 2])
        drop = sb("drop", [PW, 2])
        scale = sb("scale", [PW, 2])
        c_exp = sb("c_exp", [PW, 2, P])
        c_weight = sb("c_weight", [PW, 2, P])
        c_sum = sb("c_sum", [PW, 2])
        z_sum = sb("z_sum", [PW, 2])
        z_acc = sb("z_acc", [PW, 2, F])
        c_weight_t = sb("c_weight_t", [P, 2, PW])
        divisor = sb("divisor", [PW, 2])
        inverse = sb("inverse", [PW, 2])
        c_h = sb("c_h", [PW, 2, F])
        c_r = sb("c_r", [PW, 2, F])
        c_stats = sb("c_stats", [PW, 2, 6])
        c_moments = sb("c_moments", [PW, 2, 2])
        c_ln = sb("c_ln", [PW, 2])
        c_rstd = sb("c_rstd", [PW, 2])
        c_out = sb("c_out", [PW, 2, F])

        vt_ps = bank[0][0:FV, :].rearrange("p (w e) -> p w e", w=4)
        xt_ps = bank[1][:, 0:4 * PW].rearrange("p (w n) -> p w n", w=4)
        y_ps = bank[2][:, 0:4 * (F + 1)].rearrange("p (w f) -> p w f", w=4)
        h_ps = [bank[3], bank[4]]
        sd_ps = bank[5][0:PW, :].rearrange("p (r c) -> p r c", r=2)[:, :, 0:8]
        ds_ps = bank[6][:, 0:288].rearrange("p (r w c) -> p r w c", r=3, w=16)
        row_ps = bank[7][0:16, 0:P]
        weight_ps = bank[7][:, P:P + 16]
        sum_ps = bank[7][:, P + 16:P + 32]

        s_iota = sem("s_iota")
        s_weights = [sem(f"s_weights{i}") for i in range(11)]
        s_ds = sem("s_ds")
        s_pad = sem("s_pad")
        s_parted = sem("s_parted")
        s_ident = sem("s_ident")
        s_wt = sem("s_wt")
        s_a2t = sem("s_a2t")
        s_ew = sem("s_ew")
        s_holds = sem("s_holds")
        s_rows = sem("s_rows")
        s_local = sem("s_local")
        s_local16 = sem("s_local16")
        s_srcf = sem("s_srcf")
        s_loc_t = sem("s_loc_t")
        s_src_t = sem("s_src_t")
        s_starts = sem("s_starts")
        s_wdst = sem("s_wdst")
        s_wsrc = sem("s_wsrc")
        s_wef = sem("s_wef")
        s_wef_out = sem("s_wef_out")
        s_pair16 = sem("s_pair16")
        s_pair_out = sem("s_pair_out")
        s_local_out = sem("s_local_out")
        s_batch_local = sem("s_batch_local")
        s_setup = sem("s_setup")
        s_src = sem("s_src")
        s_gath = [sem(f"s_gath{i}") for i in range(RING)]
        s_ef = [sem(f"s_ef{i}") for i in range(RING)]
        s_x = [sem(f"s_x{i}") for i in range(RING)]
        s_loc = [sem(f"s_loc{i}") for i in range(4)]
        s_tr = sem("s_tr")
        s_cp = sem("s_cp")
        s_ys = sem("s_ys")
        s_ycp = sem("s_ycp")
        s_hot_t = sem("s_hot_t")
        s_parts = sem("s_parts")
        s_score = sem("s_score")
        s_dst_part = sem("s_dst_part")
        s_logit = sem("s_logit")
        s_links = sem("s_links")
        s_row = sem("s_row")
        s_soft = sem("s_soft")
        s_exp = sem("s_exp")
        s_col = sem("s_col")
        s_alpha_step = sem("s_alpha_step")
        s_alpha = sem("s_alpha")
        s_hot = sem("s_hot")
        s_h = sem("s_h")
        s_r = sem("s_r")
        s_stat = sem("s_stat")
        s_ln = sem("s_ln")
        s_shift = sem("s_shift")
        s_norm = sem("s_norm")
        s_store = [sem(f"s_store{i}") for i in range(3)]

        s_first_out = sem("s_first_out")
        s_first_row = sem("s_first_row")
        s_total = sem("s_total")
        s_fix = sem("s_fix")
        s_where = sem("s_where")
        s_c_src = sem("s_c_src")
        s_c_dst = sem("s_c_dst")
        s_c_ef = sem("s_c_ef")
        s_c_x = sem("s_c_x")
        s_c_gath = sem("s_c_gath")
        s_c_tr = sem("s_c_tr")
        s_c_cp = sem("s_c_cp")
        s_c_prod = sem("s_c_prod")
        s_c_max = sem("s_c_max")
        s_c_exp = sem("s_c_exp")
        s_c_weight = sem("s_c_weight")
        s_c_wt = sem("s_c_wt")
        s_c_wcp = sem("s_c_wcp")
        s_c_z = sem("s_c_z")
        s_c_var = sem("s_c_var")
        s_c_ln = sem("s_c_ln")
        s_c_rstd = sem("s_c_rstd")
        s_c_out = sem("s_c_out")
        s_c_store = sem("s_c_store")
        FIX_STEPS = 29

        def ge(eng, s, n):
            if not (isinstance(n, int) and n <= 0):
                eng.wait_ge(s, n)

        def part(eng):
            eng.sem_inc(s_parted, 1)

        def quads(eng, step, last_step):
            for j in range(RING):
                step(j, j, 0)
            n_rounds = NQ // RING
            with eng.Fori(1, n_rounds) as i:
                for j in range(RING):
                    step(i * RING + j, j, i)
            for q in range(n_rounds * RING, last_step + 1):
                step(q, q % RING, q // RING)

        def repair(eng, fix):
            eng.wait_ge(s_total, 1)
            total = eng.value_load(total_i[0:1, 0:1], min_val=0, max_val=2 * NW + N_EDGES // P)
            with eng.If(total > 0):
                with eng.Fori(0, total) as g:
                    fix(g)

        def is_quad(q):
            return not isinstance(q, int) or 0 <= q < NQ

        def is_batch_step(q, j, lag):
            return (j - lag) % 4 == 3 and (not isinstance(q, int) or 3 <= q - lag < 4 * NSB)

        def slot_round(j, i, lag, ring):
            k = j - lag
            return k % ring, i * (RING // ring) + k // ring + 1

        block = ctx.enter_context(nc.Block())

        @block.sync
        def _(sp):
            for slot in range(3):
                sp.sem_inc(s_store[slot], 16)
            sp.wait_ge(s_pad, 1)
            sp.dma_start(dst_rows_i[0:RQ - 1, :],
                         dst[0:(RQ - 1) * 512].rearrange("(q e) -> q e", e=512)).then_inc(s_weights[0], 16)
            sp.dma_start(dst_rows_i[RQ - 1:RQ, 0:R_TAIL],
                         dst[(RQ - 1) * 512:N_EDGES].unsqueeze(0)).then_inc(s_weights[1], 16)
            sp.dma_start(prev_i[1:RQ, :], dst[0:(RQ - 1) * 512].rearrange("(q e) -> q e", e=512)[:, 511:512],
                         allow_slow_non_contiguous=True).then_inc(s_weights[2], 16)
            sp.dma_start(proj_sb[:], proj_w).then_inc(s_weights[3], 16)
            sp.dma_start(a2_sb[:], apply_w[:, F:2 * F]).then_inc(s_weights[4], 16)
            sp.dma_start(a1_twice[:, 0:F], apply_w[:, 0:F]).then_inc(s_weights[5], 16)
            sp.dma_start(a1_twice[:, F:2 * F], apply_w[:, 0:F]).then_inc(s_weights[6], 16)
            sp.dma_start(edge_w[0:F, F:F + 1], attn_w[:, 0:F].rearrange("o f -> f o"),
                         allow_slow_non_contiguous=True).then_inc(s_weights[7], 16)
            sp.dma_start(attn_dst[0:F, 0:1], attn_w[:, F:2 * F].rearrange("o f -> f o"),
                         allow_slow_non_contiguous=True).then_inc(s_weights[8], 16)
            sp.dma_start(attn_dst[F:P, 1:2], attn_w[:, F:2 * F].rearrange("o f -> f o"),
                         allow_slow_non_contiguous=True).then_inc(s_weights[8], 16)
            sp.dma_start(attn_b_col[:], attn_b.unsqueeze(0).to_broadcast([P, 1])).then_inc(s_weights[9], 16)
            sp.dma_start(bias_f[:], apply_b.unsqueeze(0).to_broadcast([3, F])).then_inc(s_weights[10], 16)
            sp.wait_ge(s_starts, 1)
            sp.dma_start(first_scratch.rearrange("(c p) -> p c", c=5), first_edge[:],
                         allow_slow_non_contiguous=True).then_inc(s_first_out, 16)
            sp.wait_ge(s_local16, 1)
            sp.dma_start(local_scratch.rearrange("(c p) e -> p c e", c=5), local16[:]).then_inc(s_local_out, 16)
            sp.wait_ge(s_pair16, 1)
            sp.dma_start(pair_scratch.rearrange("(c p) e -> p c e", c=5), pair16[:]).then_inc(s_pair_out, 16)

            def edge_features(c):
                sp.wait_ge(s_wef, 16 * (c + 1))
                sp.dma_start(ef_scratch[c * WC:(c + 1) * WC, :], win_ef[:]).then_inc(s_wef_out, 16)
            edge_features(0)
            sp.wait_ge(s_local_out, 16)
            sp.dma_start(batch_local[:], local_scratch[0:NSB * 16, :].rearrange("(k g) e -> g k e", g=16)
                         ).then_inc(s_batch_local, 16)
            sp.wait_ge(s_pair_out, 16)
            sp.wait_ge(s_wef_out, 16)

            sp.wait_ge(s_first_out, 16)
            sp.dma_start(first_row[:], first_scratch.unsqueeze(0).to_broadcast([P, NWP])).then_inc(s_first_row, 16)

            def store(q, j, i):
                slot, n = slot_round(j, i, RING, 3)
                m = q - RING
                if isinstance(m, int) and not 0 <= m < NQ:
                    return
                sp.wait_ge(s_norm, m + 1)
                if isinstance(m, int) and m == NQ - 1:
                    for w in range(NW - 4 * (NQ - 1)):
                        g = 4 * m + w
                        n_here = min(NPB, N_NODES - g * NPB)
                        sp.dma_start(out[g * NPB:g * NPB + n_here, :].rearrange("(p j) f -> p (j f)", j=2),
                                     out_sb[0:n_here // 2, slot, 2 * w:2 * w + 2, :].rearrange("p c f -> p (c f)")
                                     ).then_inc(s_store[slot], 16)
                else:
                    sp.dma_start(out[bass.ds(m * (4 * NPB), 4 * NPB), :].rearrange("(w p j) f -> p w (j f)", w=4, j=2),
                                 out_sb[:, slot, :, :].rearrange("p (w j) f -> p w (j f)", w=4)
                                 ).then_inc(s_store[slot], 16)

            def step(q, j, i):
                if is_quad(q):
                    ge(sp, s_r, q - RING + 1)
                    ge(sp, s_tr, q - RING + 1)
                    if isinstance(q, int) and q == NQ - 1:
                        for w in range(NW - 4 * (NQ - 1)):
                            g = 4 * q + w
                            n_here = min(NPB, N_NODES - g * NPB)
                            sp.dma_start(x_sb[0:n_here // 2, j, w, :],
                                         x[g * NPB:g * NPB + n_here, :].rearrange("(p j) f -> p (j f)", j=2)
                                         ).then_inc(s_x[j], 16)
                    else:
                        sp.dma_start(x_sb[:, j, :, :],
                                     x[bass.ds(q * (4 * NPB), 4 * NPB), :].rearrange("(w p j) f -> p w (j f)", w=4, j=2)
                                     ).then_inc(s_x[j], 16)
                    sp.dma_start(v_sb[:, j, :, F:FV],
                                 ef_scratch[bass.ds(q * 4, 4), :].rearrange("w (e f) -> e w f", f=FE)
                                 ).then_inc(s_ef[j], 16)
                    ge(sp, s_hot_t, q - 3)
                    sp.dma_start(pair_b[:, j % 4, :],
                                 pair_scratch[bass.ds(q * 4, 4), :].rearrange("w e -> (w e)").unsqueeze(0)
                                 .to_broadcast([PW, 4 * P])).then_inc(s_loc[j % 4], 16)
                if isinstance(q, int) and q in (5, 7, 9, 11):
                    edge_features((q - 3) // 2)
                if isinstance(q, int) and q == RING - 1:
                    sp.wait_ge(s_wef_out, 80)
                store(q, j, i)
            quads(sp, step, NQ - 1 + RING)
            for slot in range(3):
                n = len(range(slot, NQ, 3))
                extra = NW - 4 * (NQ - 1) - 1 if (NQ - 1) % 3 == slot else 0
                sp.wait_ge(s_store[slot], 16 * (n + extra + 1))

            def fix(g):
                sp.wait_ge(s_where, g + 1)
                part(sp)
                edge = sp.value_load(chunk_i[0:1, 0:1], min_val=0, max_val=N_EDGES - P)
                node = sp.value_load(chunk_i[0:1, 1:2], min_val=0, max_val=N_NODES - NPB)
                sp.dma_start(c_src[:], src[bass.ds(edge, P)].unsqueeze(1),
                             allow_slow_non_contiguous=True).then_inc(s_c_src, 16)
                sp.dma_start(c_v[:, F:FV], ef[bass.ds(edge, P), :]).then_inc(s_c_ef, 16)
                sp.dma_start(c_x[:], x[bass.ds(node, NPB), :].rearrange("(p j) f -> p (j f)", j=2)
                             ).then_inc(s_c_x, 16)
                sp.dma_start(c_dst_i[:], dst[bass.ds(edge, P)].unsqueeze(0).to_broadcast([PW, P])
                             ).then_inc(s_c_dst, 16)
                sp.wait_ge(s_c_out, g + 1)
                sp.dma_start(out[bass.ds(node, NPB), :].rearrange("(p j) f -> p (j f)", j=2),
                             c_out[:].rearrange("p j f -> p (j f)")).then_inc(s_c_store, 16)
                sp.wait_ge(s_c_store, g * 16 + 16)
                part(sp)
            repair(sp, fix)

        @block.gpsimd
        def _(pool):
            nc.gpsimd.iota(iota_i[:, 0:P], pattern=[[1, P]], base=0, channel_multiplier=-1).then_inc(s_iota, 1)
            nc.gpsimd.iota(order_i[:], pattern=[[1, PW]], base=0, channel_multiplier=0).then_inc(s_iota, 1)
            nc.gpsimd.iota(node_i[:], pattern=[[1, 2]], base=0, channel_multiplier=2).then_inc(s_iota, 1)
            nc.gpsimd.iota(base_i[:], pattern=[[NPB * WC, 5]], base=0, channel_multiplier=NPB).then_inc(s_iota, 1)
            nc.gpsimd.iota(part_i[:], pattern=[[0, 1]], base=0, channel_multiplier=1).then_inc(s_iota, 1)
            pool.wait_ge(s_ident, 1)
            nc.gpsimd.iota(iota_i[:], pattern=[[NPB, NWP]], base=0, channel_multiplier=0).then_inc(s_iota, 1)
            pool.wait_ge(s_starts, 1)
            for c in range(5):
                pool.indirect_dma_start(out=win_dst_i[:, c, :], out_offset=None, in_=dst.unsqueeze(0),
                                        in_offset=bass.IndirectOffsetOnAxis(ap=start_i[:, c:c + 1], axis=1)
                                        ).then_inc(s_wdst, 16)
            for c in range(5):
                pool.indirect_dma_start(out=win_src_i[:, c, :], out_offset=None, in_=src.unsqueeze(0),
                                        in_offset=bass.IndirectOffsetOnAxis(ap=start_i[:, c:c + 1], axis=1)
                                        ).then_inc(s_wsrc, 16)

            def edge_features(c):
                ge(pool, s_wef_out, 16 * c)
                pool.indirect_dma_start(out=win_ef[:], out_offset=None,
                                        in_=ef.rearrange("a b -> (a b)").unsqueeze(0),
                                        in_offset=bass.IndirectOffsetOnAxis(ap=start_ef[:, c:c + 1], axis=1)
                                        ).then_inc(s_wef, 16)
            edge_features(0)

            def step(q, j, i):
                if not is_quad(q):
                    return
                if isinstance(q, int) and q in (4, 6, 8, 10):
                    edge_features(q // 2 - 1)
                if j % 6 == 0:
                    pool.wait_ge(s_src, i * 2 + j // 6 + 1)
                ge(pool, s_tr, q - RING + 1)
                part(pool)
                for w in range(4):
                    pool.indirect_dma_start(out=v_sb[:, j, w, 0:F], out_offset=None, in_=x,
                                            in_offset=bass.IndirectOffsetOnAxis(
                                                ap=src_now[:, j // 6, 4 * (j % 6) + w:4 * (j % 6) + w + 1], axis=0)
                                            ).then_inc(s_gath[j], 16)
            quads(pool, step, NQ - 1)

            def fix(g):
                pool.wait_ge(s_c_src, g * 16 + 16)
                part(pool)
                pool.indirect_dma_start(out=c_v[:, 0:F], out_offset=None, in_=x,
                                        in_offset=bass.IndirectOffsetOnAxis(ap=c_src[:, 0:1], axis=0)
                                        ).then_inc(s_c_gath, 16)
            repair(pool, fix)

        @block.scalar
        def _(act):
            nc.scalar.preload_act_table_set("natural_log_exp_and_others")

            def step(q, j, i):
                a, e, m = q - 1, q - 10, q - 11
                if is_quad(a):
                    act.wait_ge(s_ys, a + 1)
                    nc.scalar.copy(y_sb[:, (j - 1) % RING, :, :], y_ps).then_inc(s_ycp, 1)
                if is_quad(q):
                    act.wait_ge(s_tr, q + 1)
                    ge(act, s_ys, q - 1)
                    nc.scalar.copy(vt_sb[:, j % 2, :, :], vt_ps)
                    ge(act, s_h, q - RING + 1)
                    nc.scalar.copy(xt_sb[:, j, :, :], xt_ps).then_inc(s_cp, 1)
                    if j % 6 == 5 and not (isinstance(q, int) and q + 7 >= NQ):
                        act.wait_ge(s_setup, 1)
                        nc.scalar.copy(src_now[:, j // 6, :], src_col[:, bass.ds((q + 7) * 4, 24)]).then_inc(s_src, 1)
                if is_quad(e):
                    act.wait_ge(s_stat, e * 4 + 4)
                    nc.scalar.activation(ln_var[:, (j - 10) % 4, :], var64[:, (j - 10) % 4, :], ACT.Ln,
                                         bias=eps_col[0:PW, :], scale=1.0 / F).then_inc(s_ln, 1)
                if is_quad(e):
                    act.wait_ge(s_ln, e * 2 + 1)
                    nc.scalar.activation(rstd[:, (j - 10) % 4, :], ln_var[:, (j - 10) % 4, :], ACT.Exp,
                                         scale=-0.5).then_inc(s_ln, 1)
                if is_quad(m):
                    act.wait_ge(s_shift, m + 1)
                    slot, n = slot_round(j, i, 11, 3)
                    act.wait_ge(s_store[slot], 16 * n)
                    for b in range(8):
                        last = nc.scalar.activation(out_sb[:, slot, b, :], r_sb[:, (j - 11) % 4, b, :], ACT.Identity,
                                                    bias=shift[:, (j - 11) % 4, b:b + 1],
                                                    scale=rstd[:, (j - 11) % 4, b:b + 1])
                    last.then_inc(s_norm, 1)
                if is_batch_step(q, j, 3):
                    k = i * 3 + (j - 6) // 4
                    act.wait_ge(s_soft, k * 6 + 3)
                    ge(act, s_col, k)
                    nc.scalar.activation(weight[:], shifted[:], ACT.Exp).then_inc(s_exp, 1)
            quads(act, step, NQ - 1 + 11)

            def fix(g):
                act.wait_ge(s_c_max, g + 1)
                nc.scalar.activation(scale[:], drop[:], ACT.Exp)
                for half in range(2):
                    last = nc.scalar.activation(c_exp[:, half, :], c_logit[:, half, :], ACT.Exp,
                                                bias=minus_max[:, half:half + 1])
                last.then_inc(s_c_exp, 1)
                act.wait_ge(s_c_var, g + 1)
                nc.scalar.activation(c_ln[:], c_moments[:, :, 1], ACT.Ln, bias=eps_col[0:PW, :]
                                     ).then_inc(s_c_ln, 1)
                act.wait_ge(s_c_ln, g + 1)
                nc.scalar.activation(c_rstd[:], c_ln[:], ACT.Exp, scale=-0.5).then_inc(s_c_rstd, 1)
            repair(act, fix)

        @block.tensor
        def _(pe):
            pe.wait_ge(s_ident, 2)
            pe.wait_ge(s_weights[4], 16)
            nc.tensor.transpose(bank[0][0:F, 0:F], a2_sb[:], ident[0:F, 0:F])
            pe.wait_ge(s_weights[5], 16)
            pe.wait_ge(s_weights[6], 16)
            nc.tensor.transpose(bank[0][:, 64:128], a1_twice[:], ident[0:F, 0:F]).then_inc(s_wt, 1)
            pe.wait_ge(s_a2t, 1)
            pe.wait_ge(s_weights[3], 16)
            nc.tensor.matmul(bank[1][0:FV, 0:F], proj_sb[:], a2_t[:], start=True, stop=True).then_inc(s_ew, 1)
            pe.wait_ge(s_holds, 1)
            for c in range(5):
                nc.tensor.matmul(bank[2][0:WC, c:c + 1], above_last[:, c * WC:(c + 1) * WC], ones_col[0:RQ, :],
                                 start=True, stop=True)
            for c in range(5):
                nc.tensor.matmul(bank[3 + c][0:WC, :], holds[:, c * WC:(c + 1) * WC], dst_rows[:],
                                 start=True, stop=True).then_inc(s_rows, 1)
            pe.wait_ge(s_local, 1)
            for c in range(4):
                nc.tensor.transpose(bank[0][:, c * WC:(c + 1) * WC], local[:, c, :], ident[0:WC, 0:WC])
            nc.tensor.transpose(bank[2][:, 0:WC], local[:, 4, :], ident[0:WC, 0:WC]).then_inc(s_loc_t, 1)
            pe.wait_ge(s_srcf, 1)
            for c in range(4):
                nc.tensor.transpose(bank[1][:, c * WC:(c + 1) * WC], win_src[:, c, :], ident[0:WC, 0:WC])
            nc.tensor.transpose(bank[3][:, 0:WC], win_src[:, 4, :], ident[0:WC, 0:WC]).then_inc(s_src_t, 1)
            pe.wait_ge(s_setup, 1)

            def step(q, j, i):
                a, b, c = q - 1, q - 2, q - 8
                if is_quad(a):
                    pe.wait_ge(s_cp, a + 1)
                    ge(pe, s_ycp, a)
                    ge(pe, s_parts, a * 4 - 2)
                    for w in range(4):
                        at = w * (F + 1)
                        nc.tensor.matmul(bank[2][:, at:at + P], vt_sb[:, (j - 1) % 2, w, :], edge_w[:],
                                         start=True, stop=True)
                    for w in range(4):
                        at = 256 * ((j - 1) % 2) + 2 * w
                        last = nc.tensor.matmul(bank[5][0:PW, at:at + PW],
                                                xt_sb[:, (j - 1) % RING, w, :], attn_dst[:], start=True, stop=True)
                    last.then_inc(s_ys, 1)
                if is_quad(b):
                    pe.wait_ge(s_parts, b * 4 + 4)
                    pe.wait_ge(s_hot_t, b + 1)
                    kd = (j - 2) // 4 % 3
                    if (j - 2) % 4 == 0:
                        ge(pe, s_dst_part, i * 3 + (j - 2) // 4)
                    for w in range(4):
                        last = nc.tensor.matmul(ds_ps[:, kd, 4 * ((j - 2) % 4) + w, :],
                                                hot_t[:, (j - 2) % 2, w * P:(w + 1) * P],
                                                sd_parts[:, (j - 2) % 2, 2 * w:2 * w + 2, :]
                                                .rearrange("p j t -> p (j t)"), start=True, stop=True)
                    last.then_inc(s_score, 1)
                if is_batch_step(q, j, 3):
                    k = i * 3 + (j - 6) // 4
                    pe.wait_ge(s_logit, k * 3 + 3)
                    ge(pe, s_alpha, k)
                    nc.tensor.transpose(row_ps, logit_l[:], ident[:]).then_inc(s_row, 1)
                if is_quad(q):
                    pe.wait_ge(s_gath[j], i * 64 + 64)
                    pe.wait_ge(s_ef[j], i * 16 + 16)
                    ge(pe, s_cp, q)
                    for w in range(4):
                        nc.tensor.transpose(vt_ps[:, w, :], v_sb[:, j, w, :], ident[:])
                    pe.wait_ge(s_x[j], i * 16 + 16)
                    for w in range(4):
                        last = nc.tensor.transpose(xt_ps[:, w, :], x_sb[:, j, w, :], ident[0:PW, 0:PW])
                    last.then_inc(s_tr, 1)
                if is_batch_step(q, j, 5):
                    k = i * 3 + (j - 8) // 4
                    pe.wait_ge(s_soft, k * 6 + 6)
                    part(pe)
                    nc.tensor.transpose(weight_ps, weight[:], ident[0:16, 0:16])
                    nc.tensor.transpose(sum_ps, seg_sum[:], ident[0:16, 0:16]).then_inc(s_col, 1)
                if is_quad(c):
                    h = h_ps[(j - 8) % 2]
                    ge(pe, s_r, c - 1)
                    for w in range(4):
                        at = w * 2 * F
                        nc.tensor.matmul(h[0:PW, at:at + 2 * F], xt_sb[:, (j - 8) % RING, w, :], node_w[:],
                                         start=True, stop=False)
                        if w == 0:
                            pe.wait_ge(s_hot, c + 1)
                        nc.tensor.matmul(h[0:PW, at:at + 2 * F], hot[:, (j - 8) % 2, w, :],
                                         y2[:, (j - 8) % 2, w, :, :].rearrange("p j f -> p (j f)"),
                                         start=False, stop=False)
                        last = nc.tensor.matmul(h[0:PW, at:at + 2 * F], ones3[:, 0:PW], bias3[:],
                                                start=False, stop=True)
                    last.then_inc(s_h, 1)
            quads(pe, step, NQ - 1 + 8)

            def fix(g):
                pe.wait_ge(s_c_x, g * 16 + 16)
                nc.tensor.transpose(bank[1][:, 0:PW], c_x[:], ident[0:PW, 0:PW])
                pe.wait_ge(s_c_gath, g * 16 + 16)
                pe.wait_ge(s_c_ef, g * 16 + 16)
                nc.tensor.transpose(bank[1][0:FV, P:2 * P], c_v[:], ident[:]).then_inc(s_c_tr, 1)
                pe.wait_ge(s_c_cp, g + 1)
                nc.tensor.matmul(bank[5][0:PW, 0:P], attn_src_wide[:], c_vt[:], start=True, stop=True)
                nc.tensor.matmul(bank[5][0:PW, P:P + 2], c_xt[:], attn_dst[:, 0:2], start=True, stop=True)
                nc.tensor.matmul(bank[5][:, 256:256 + F], c_vt[:], edge_w[:, 0:F], start=True, stop=True
                                 ).then_inc(s_c_prod, 1)
                nc.tensor.matmul(bank[3][0:PW, 0:2 * F], c_xt[:], node_w[:], start=True, stop=False)
                nc.tensor.matmul(bank[3][0:PW, 0:2 * F], ones3[:, 0:PW], bias3[:], start=False, stop=True)
                pe.wait_ge(s_c_weight, g + 1)
                for half in range(2):
                    last = nc.tensor.transpose(bank[1][:, half * PW:(half + 1) * PW], c_weight[:, half, :],
                                               ident[0:PW, 0:PW])
                last.then_inc(s_c_wt, 1)
                pe.wait_ge(s_c_wcp, g + 1)
                for half in range(2):
                    last = nc.tensor.matmul(bank[4][0:PW, half * F:(half + 1) * F], c_weight_t[:, half, :], c_y[:],
                                            start=True, stop=True)
                last.then_inc(s_c_z, 1)
            repair(pe, fix)

        @block.vector
        def _(dve):
            steps = [0]

            def done(ins):
                steps[0] += 1
                ins.then_inc(s_ds, 1)
                dve.wait_ge(s_ds, steps[0])

            nc.vector.memset(prev_i[:], -1)
            nc.vector.memset(node_w[:], 0.0)
            nc.vector.memset(edge_w[:], 0.0)
            nc.vector.memset(attn_dst[:], 0.0)
            nc.vector.memset(ones_col[:], 1.0)
            nc.vector.memset(ones3[:], 1.0)
            nc.vector.memset(eps_col[:], EPS)
            nc.vector.memset(same, 0.0)
            nc.vector.memset(dst_rows_i[:], PAD_NODE).then_inc(s_pad, 1)
            dve.wait_ge(s_iota, 1)
            nc.vector.tensor_copy(ident[:], iota_i[:, 0:P]).then_inc(s_ident, 1)
            dve.wait_ge(s_ident, 1)
            nc.vector.tensor_scalar(ident[:], ident[:], 0.0, None, ALU.is_equal).then_inc(s_ident, 1)
            dve.wait_ge(s_iota, 6)
            nc.vector.tensor_copy(order[:], order_i[:])
            nc.vector.tensor_copy(node_id[:], node_i[:])
            nc.vector.tensor_copy(base[:], base_i[:])
            nc.vector.tensor_copy(part_f[:], part_i[:])
            nc.vector.tensor_copy(starts[:], iota_i[:])
            for s in range(3):
                dve.wait_ge(s_weights[s], 16)
            nc.vector.tensor_copy(dst_rows[:], dst_rows_i[:])
            done(nc.vector.tensor_copy(prev_f[:], prev_i[:]))
            nc.vector.tensor_scalar(above_last[:], starts[0:RQ, :], dst_rows[:, 511:512], None, ALU.is_gt)
            done(nc.vector.tensor_scalar(holds[:], starts[0:RQ, :], prev_f[:], None, ALU.is_gt))
            nc.vector.tensor_tensor(holds[:], holds[:], above_last[:], ALU.subtract).then_inc(s_holds, 1)
            dve.wait_ge(s_wt, 1)
            nc.vector.tensor_copy(a2_t[:], bank[0][0:F, 0:F]).then_inc(s_a2t, 1)
            nc.vector.tensor_copy(node_w[0:F, 0:F], bank[0][0:F, 64:128])
            nc.vector.tensor_copy(node_w[F:P, F:2 * F], bank[0][F:P, 64:128])
            for c in range(5):
                dve.wait_ge(s_rows, c + 1)
                done(nc.vector.tensor_scalar(below[:], bank[3 + c][0:WC, :], base[0:WC, c:c + 1], None, ALU.is_lt,
                                             ALU.add, accum_out=count_in_row[:, c:c + 1]))
            done(nc.vector.scalar_tensor_tensor(first_edge[:], bank[2][0:WC, 0:5], 512.0, count_in_row[:],
                                                ALU.mult, ALU.add))
            done(nc.vector.tensor_scalar(start_f[:], first_edge[:], float(N_EDGES - P), None, ALU.min))
            nc.vector.tensor_copy(start_i[:], start_f[:])
            nc.vector.tensor_scalar(start_ef[:], start_f[:], float(FE), None, ALU.mult).then_inc(s_starts, 1)
            dve.wait_ge(s_ew, 1)
            dve.wait_ge(s_weights[7], 16)
            nc.vector.tensor_copy(edge_w[:, 0:F], bank[1][0:FV, 0:F])
            dve.wait_ge(s_weights[10], 16)
            done(nc.vector.tensor_copy(bias_hi[:], bias_f[:]))
            done(nc.vector.tensor_tensor(bias_rest[:], bias_f[:], bias_hi[:], ALU.subtract))
            done(nc.vector.tensor_copy(bias_mid[:], bias_rest[:]))
            nc.vector.tensor_tensor(bias_lo[:], bias_rest[:], bias_mid[:], ALU.subtract)
            for k in range(3):
                last = nc.vector.tensor_scalar(pick[:, k:k + 1], part_f[0:3, :], float(k), None, ALU.is_equal)
            done(last)
            done(nc.vector.tensor_scalar(bias_sum[:], bias_hi[:], pick[:, 0:1], None, ALU.mult))
            done(nc.vector.scalar_tensor_tensor(bias_sum[:], bias_mid[:], pick[:, 1:2], bias_sum[:],
                                                ALU.mult, ALU.add))
            done(nc.vector.scalar_tensor_tensor(bias_sum[:], bias_lo[:], pick[:, 2:3], bias_sum[:],
                                                ALU.mult, ALU.add))
            nc.vector.tensor_copy(bias3[:, 0:F], bias_sum[:])
            done(nc.vector.tensor_copy(bias3[:, F:2 * F], bias_sum[:]))
            dve.wait_ge(s_wdst, 80)
            done(nc.vector.tensor_copy(win_dst[:], win_dst_i[:]))
            for c in range(5):
                last = nc.vector.tensor_scalar(local[:, c, :], win_dst[:, c, :], base[0:WC, c:c + 1], -1.0,
                                               ALU.subtract, ALU.max)
            done(last)
            nc.vector.tensor_scalar(local[:], local[:], float(NPB), None, ALU.min).then_inc(s_local, 1)
            dve.wait_ge(s_local, 1)
            nc.vector.tensor_copy(local16[:], local[:]).then_inc(s_local16, 1)
            done(nc.vector.tensor_copy(pair_i[:], local[:]))
            done(nc.vector.tensor_scalar(pair_i[:], pair_i[:], 1, None, ALU.arith_shift_right))
            nc.vector.tensor_copy(pair16[:], pair_i[:]).then_inc(s_pair16, 1)
            dve.wait_ge(s_wsrc, 80)
            nc.vector.tensor_copy(win_src[:], win_src_i[:]).then_inc(s_srcf, 1)
            dve.wait_ge(s_loc_t, 1)
            nc.vector.tensor_copy(local_col[:, 0:4 * WC], bank[0][:, 0:4 * WC])
            nc.vector.tensor_copy(local_col[:, 4 * WC:NWP], bank[2][:, 0:WC])
            dve.wait_ge(s_src_t, 1)
            nc.vector.tensor_copy(src_col[:, 0:4 * WC], bank[1][:, 0:4 * WC])
            done(nc.vector.tensor_copy(src_col[:, 4 * WC:NWP], bank[3][:, 0:WC]))
            dve.wait_ge(s_weights[8], 32)
            dve.wait_ge(s_weights[9], 16)
            nc.vector.tensor_copy(src_now[:].rearrange("p h c -> p (h c)"), src_col[:, 0:48]).then_inc(s_src, 2)
            nc.vector.memset(alpha[:], 0.0).then_inc(s_setup, 1)
            done(nc.vector.tensor_copy(pair_col_i[:], local_col[:]))
            done(nc.vector.tensor_scalar(pair_col_i[:], pair_col_i[:], 1, None, ALU.arith_shift_right))
            done(nc.vector.tensor_copy(pair_col[:], pair_col_i[:]))
            done(nc.vector.scalar_tensor_tensor(parity[:, :, 1], pair_col[:], -2.0, local_col[:],
                                                ALU.mult, ALU.add))
            nc.vector.tensor_scalar(parity[:, :, 0], parity[:, :, 1], -1.0, 1.0, ALU.mult, ALU.add)
            dve.wait_ge(s_batch_local, 16)
            done(nc.vector.tensor_tensor(same[:, :, 1:P], batch_local[:, :, 1:P], batch_local[:, :, 0:P - 1],
                                         ALU.is_equal))
            nc.vector.tensor_scalar(apart, same, -1.0, 1.0, ALU.mult, ALU.add)
            done(nc.vector.tensor_scalar(wall, same, -1.0, BIG, ALU.add, ALU.mult))

            def step(q, j, i):
                a, c, e, m = q - 1, q - 8, q - 9, q - 11
                if is_quad(m):
                    dve.wait_ge(s_ln, m * 2 + 2)
                    nc.vector.scalar_tensor_tensor(shift[:, (j - 11) % 4, :], mean2[:, (j - 11) % 4, :], -0.5,
                                                   rstd[:, (j - 11) % 4, :], ALU.mult, ALU.mult
                                                   ).then_inc(s_shift, 1)
                if is_quad(c):
                    ge(dve, s_h, c - 1)
                    nc.vector.tensor_tensor(hot[:, (j - 8) % 2, :, :],
                                            order[:].unsqueeze(1).to_broadcast([P, 4, PW]),
                                            pair_col[:, bass.ds(c * 4, 4)].unsqueeze(2).to_broadcast([P, 4, PW]),
                                            ALU.is_equal)
                if is_quad(e):
                    dve.wait_ge(s_h, e + 1)
                    ge(dve, s_norm, e - 3)
                    nc.vector.scalar_tensor_tensor(r_sb[:, (j - 9) % 4, :, :].rearrange("p c f -> p (c f)"),
                                                   h_ps[(j - 9) % 2][0:PW, :], 0.0,
                                                   x_sb[:, (j - 9) % RING, :, :].rearrange("p w f -> p (w f)"),
                                                   ALU.max, ALU.add).then_inc(s_r, 1)
                if is_batch_step(q, j, 5):
                    k = i * 3 + (j - 8) // 4
                    dve.wait_ge(s_col, k + 1)
                    nc.vector.reciprocal(col_rcp[:], sum_ps).then_inc(s_alpha_step, 1)
                    dve.wait_ge(s_alpha_step, k * 2 + 1)
                    nc.vector.tensor_tensor(col_alpha[:], weight_ps, col_rcp[:], ALU.mult).then_inc(s_alpha_step, 1)
                    dve.wait_ge(s_alpha_step, k * 2 + 2)
                    nc.vector.tensor_tensor(alpha[:, (j - 8) // 4 % 3, :, :],
                                            col_alpha[:].unsqueeze(2).to_broadcast([P, 16, 2]),
                                            parity[:, bass.ds(k * 16, 16), :], ALU.mult).then_inc(s_alpha, 1)
                if is_quad(c):
                    kc, at = (j - 8) // 4, 4 * ((j - 8) % 4)
                    dve.wait_ge(s_alpha, i * 3 + kc + 1)
                    nc.vector.tensor_tensor(y2[:, (j - 8) % 2, :, :, :],
                                            y_sb[:, (j - 8) % RING, :, 0:F].unsqueeze(2)
                                            .to_broadcast([P, 4, 2, F]),
                                            alpha[:, kc % 3, at:at + 4, :].unsqueeze(3).to_broadcast([P, 4, 2, F]),
                                            ALU.mult).then_inc(s_hot, 1)
                if is_quad(a):
                    slot, n = slot_round(j, i, 1, 4)
                    dve.wait_ge(s_loc[slot], n * 16)
                    ge(dve, s_score, a - 1)
                    nc.vector.tensor_scalar(hot_t[:, (j - 1) % 2, :], pair_b[:, slot, :], part_f[0:PW, :], None,
                                            ALU.is_equal).then_inc(s_hot_t, 1)

                part16 = [sd_parts[:, (j - 1) % 2, :, t] for t in range(3)]
                scores = sd_ps[:, (j - 1) % 2, :]
                same_now, apart_now, wall_now = [links_now[:, t, :] for t in range(3)]

                def moments(first, end):
                    if not is_quad(e):
                        return
                    if first == 0:
                        dve.wait_ge(s_r, e + 1)
                    for b in range(first, end):
                        last = nc.vector.bn_stats(stats[:, (j - 9) % 4, b, :], r_sb[:, (j - 9) % 4, b, :])
                    if end == 8:
                        last.then_inc(s_stat, 1)

                def split(n):
                    if not is_quad(a):
                        return
                    if n == 0:
                        dve.wait_ge(s_ys, a + 1)
                        nc.vector.tensor_copy(part16[0], scores).then_inc(s_parts, 1)
                        return
                    dve.wait_ge(s_parts, a * 4 + n)
                    if n == 1:
                        nc.vector.tensor_tensor(sd_rest[:, (j - 1) % 2, :], scores, part16[0],
                                                ALU.subtract).then_inc(s_parts, 1)
                    elif n == 2:
                        nc.vector.tensor_copy(part16[1], sd_rest[:, (j - 1) % 2, :]).then_inc(s_parts, 1)
                    else:
                        nc.vector.tensor_tensor(part16[2], sd_rest[:, (j - 1) % 2, :], part16[1],
                                                ALU.subtract).then_inc(s_parts, 1)

                def batch(n):
                    if is_batch_step(q, j, 2):
                        logits(n, i * 3 + (j - 5) // 4)
                    elif is_batch_step(q, j, 3):
                        maxima(n, i * 3 + (j - 6) // 4)
                    elif is_batch_step(q, j, 4):
                        sums(n, i * 3 + (j - 7) // 4)

                def logits(n, k):
                    if n == 1:
                        upto = min(q - 1, NQ) if isinstance(q, int) else q - 1
                        dve.wait_ge(s_score, upto)
                        nc.vector.tensor_tensor(ds_parts[:].rearrange("p w (j t) -> p w j t", j=2),
                                                ds_ps[:, (j - 5) // 4 % 3, :, :]
                                                .rearrange("p w (j t) -> p w j t", j=2),
                                                parity[:, bass.ds(k * 16, 16), :].unsqueeze(3)
                                                .to_broadcast([P, 16, 2, 3]), ALU.mult).then_inc(s_dst_part, 1)
                    elif n == 2:
                        dve.wait_ge(s_dst_part, k + 1)
                        nc.vector.tensor_reduce(dst_score[:], ds_parts[:], AX.X, ALU.add).then_inc(s_logit, 1)
                    elif n == 3:
                        sl = (j - 5) % RING
                        upto = min(q - 1, NQ) if isinstance(q, int) else q - 1
                        dve.wait_ge(s_ycp, upto)
                        dve.wait_ge(s_logit, k * 3 + 1)
                        nc.vector.scalar_tensor_tensor(logit[:].rearrange("p (a w) -> p a w", w=4),
                                                       dst_score[:].rearrange("p (a w) -> p a w", w=4),
                                                       attn_b_col[:], y_sb[:, sl:sl + 4, :, F], ALU.add, ALU.add
                                                       ).then_inc(s_logit, 1)
                    elif n == 4:
                        dve.wait_ge(s_logit, k * 3 + 2)
                        ge(dve, s_row, k)
                        nc.vector.scalar_tensor_tensor(logit_l[:], logit[:], LEAK, logit[:], ALU.mult, ALU.max
                                                       ).then_inc(s_logit, 1)
                    elif n == 5:
                        nc.vector.tensor_copy(links_now[:].rearrange("p t e -> p (t e)"),
                                              links[:, bass.ds(k, 1), :, :].rearrange("p o t e -> p (o t e)")
                                              ).then_inc(s_links, 1)

                def maxima(n, k):
                    if n == 1:
                        dve.wait_ge(s_links, k + 1)
                        dve.wait_ge(s_row, k + 1)
                        nc.vector.tensor_tensor_scan(run_max[:], wall_now[:, 0:P], row_ps, -BIG, ALU.add, ALU.max
                                                     ).then_inc(s_soft, 1)
                    elif n == 2:
                        dve.wait_ge(s_soft, k * 6 + 1)
                        nc.vector.tensor_tensor_scan(seg_max[:, ::-1], wall_now[:, P:0:-1], run_max[:, ::-1], -BIG,
                                                     ALU.add, ALU.max).then_inc(s_soft, 1)
                    elif n == 3:
                        dve.wait_ge(s_soft, k * 6 + 2)
                        nc.vector.tensor_tensor(shifted[:], row_ps, seg_max[:], ALU.subtract).then_inc(s_soft, 1)

                def sums(n, k):
                    if n == 1:
                        dve.wait_ge(s_exp, k + 1)
                        nc.vector.tensor_tensor_scan(run_sum[:], same_now[:, 0:P], weight[:], 0.0, ALU.mult, ALU.add
                                                     ).then_inc(s_soft, 1)
                    elif n == 2:
                        dve.wait_ge(s_soft, k * 6 + 4)
                        nc.vector.tensor_tensor(last_sum[:], run_sum[:], apart_now[:, 1:P + 1], ALU.mult
                                                ).then_inc(s_soft, 1)
                    elif n == 3:
                        dve.wait_ge(s_soft, k * 6 + 5)
                        ge(dve, s_col, k)
                        nc.vector.tensor_tensor_scan(seg_sum[:, ::-1], same_now[:, P:0:-1], last_sum[:, ::-1], 0.0,
                                                     ALU.mult, ALU.add).then_inc(s_soft, 1)

                def variance(n):
                    if not is_quad(e):
                        return
                    st = stats[:, (j - 9) % 4, :, :]
                    at = (j - 9) % 4
                    dve.wait_ge(s_stat, e * 4 + n)
                    if n == 1:
                        nc.vector.tensor_tensor(halves[:, at, :], st[:, :, 1], st[:, :, 4], ALU.subtract)
                        nc.vector.tensor_tensor(mean2[:, at, :], st[:, :, 1], st[:, :, 4], ALU.add)
                        nc.vector.tensor_tensor(moment[:, at, :], st[:, :, 2], st[:, :, 5], ALU.add
                                                ).then_inc(s_stat, 1)
                    elif n == 2:
                        nc.vector.scalar_tensor_tensor(spread[:, at, :], halves[:, at, :], F / 4.0,
                                                       halves[:, at, :], ALU.mult, ALU.mult).then_inc(s_stat, 1)
                    else:
                        nc.vector.tensor_tensor(var64[:, at, :], spread[:, at, :], moment[:, at, :], ALU.add
                                                ).then_inc(s_stat, 1)

                batch(1)
                moments(0, 2)
                split(0)
                batch(2)
                moments(2, 4)
                split(1)
                batch(3)
                moments(4, 6)
                split(2)
                batch(4)
                moments(6, 8)
                split(3)
                variance(1)
                batch(5)
                variance(2)
                variance(3)
            quads(dve, step, NQ - 1 + 11)

            dve.wait_ge(s_first_row, 16)
            nc.vector.memset(ones_row[:], 1.0)
            nc.vector.tensor_copy(begin[:], first_row[:, 0:NW])
            done(nc.vector.tensor_tensor(n_edges[:], first_row[:, 1:NW + 1], first_row[:, 0:NW], ALU.subtract))
            nc.vector.tensor_copy(begin[:, NW - 1:NW], first_row[:, NW - 2:NW - 1])
            done(nc.vector.tensor_scalar(crowded[:], n_edges[:], float(P), None, ALU.is_gt))
            done(nc.vector.scalar_tensor_tensor(span_i[:], first_row[:, 1:NW + 1], float(P - 1), begin[:],
                                                ALU.add, ALU.subtract))
            done(nc.vector.tensor_scalar(span_i[:], span_i[:], 7, None, ALU.arith_shift_right))
            done(nc.vector.tensor_tensor(n_chunks[:], span_i[:], crowded[:], ALU.mult))
            done(nc.vector.tensor_tensor_scan(chunks_to[:], ones_row[:], n_chunks[:], 0.0, ALU.mult, ALU.add))
            nc.vector.tensor_copy(total_i[:], chunks_to[:, NW - 1:NW]).then_inc(s_total, 1)
            done(nc.vector.tensor_tensor(rest[:], n_chunks[:], chunks_to[:], ALU.subtract))
            nc.vector.scalar_tensor_tensor(key[:], rest[:], float(P), begin[:], ALU.mult, ALU.add)
            nc.vector.tensor_copy(attn_src_wide[:], edge_w[:, F:F + 1].to_broadcast([FV, PW]))
            nc.vector.memset(chunk_no[:], 0.0)
            nc.vector.memset(last_node[:], -1.0)
            nc.vector.memset(new_max[:], -BIG)
            nc.vector.memset(z_sum[:], 0.0)
            dve.wait_ge(s_norm, NQ)
            done(nc.vector.memset(z_acc[:], 0.0))

            def fix(g):
                fixed = [0]

                def then(ins):
                    fixed[0] += 1
                    ins.then_inc(s_fix, 1)
                    dve.wait_ge(s_fix, g * FIX_STEPS + fixed[0])

                then(nc.vector.tensor_scalar(rest[:], chunks_to[:], chunk_no[:], None, ALU.is_le, ALU.add,
                                             accum_out=block_no[:]))
                then(nc.vector.tensor_scalar(block_node[:], block_no[:], float(NPB), None, ALU.mult))
                then(nc.vector.tensor_scalar(rest[:], starts[:, 0:NW], block_node[:], None, ALU.is_equal))
                then(nc.vector.tensor_tensor(rest[:], rest[:], key[:], ALU.mult))
                then(nc.vector.tensor_reduce(block_key[:], rest[:], AX.X, ALU.add))
                then(nc.vector.scalar_tensor_tensor(chunk_begin[:], chunk_no[:], float(P), block_key[:],
                                                    ALU.mult, ALU.add))
                then(nc.vector.tensor_scalar(chunk_edge[:], chunk_begin[:], float(N_EDGES - P), None, ALU.min))
                then(nc.vector.tensor_scalar(chunk_node[:], block_node[:], float(N_NODES - NPB), None, ALU.min))
                nc.vector.tensor_copy(chunk_i[:, 0:1], chunk_edge[:])
                nc.vector.tensor_copy(chunk_i[:, 1:2], chunk_node[:]).then_inc(s_where, 1)
                nc.vector.tensor_scalar(node_now[:], node_id[:], chunk_node[:], None, ALU.add)
                nc.vector.tensor_tensor(goes_on[:], block_node[:], last_node[:], ALU.is_equal)
                then(nc.vector.tensor_tensor(overlap[:], chunk_begin[:], chunk_edge[:], ALU.subtract))
                nc.vector.tensor_scalar(overlap[:], overlap[:], float(NPB), None, ALU.mult)
                nc.vector.tensor_copy(last_node[:], block_node[:])
                nc.vector.tensor_scalar(chunk_no[:], chunk_no[:], 1.0, None, ALU.add)
                then(nc.vector.tensor_scalar(reset[:], goes_on[:], -1.0, BIG, ALU.add, ALU.mult))
                nc.vector.tensor_scalar(old_max[:], new_max[:], goes_on[0:PW, :], reset[0:PW, :],
                                        ALU.mult, ALU.add)
                then(nc.vector.tensor_scalar(valid[:], starts[:, 0:P], overlap[:], None, ALU.is_ge))
                dve.wait_ge(s_c_dst, g * 16 + 16)
                then(nc.vector.tensor_copy(c_dst[:], c_dst_i[:]))
                for half in range(2):
                    last = nc.vector.scalar_tensor_tensor(c_mask[:, half, :], c_dst[:],
                                                          node_now[0:PW, half:half + 1], valid[0:PW, :],
                                                          ALU.is_equal, ALU.mult)
                then(last)
                nc.vector.tensor_scalar(c_wall[:], c_mask[:], -1.0, BIG, ALU.add, ALU.mult)
                dve.wait_ge(s_c_tr, g + 1)
                nc.vector.tensor_copy(c_xt[:], bank[1][:, 0:PW])
                nc.vector.tensor_copy(c_vt[:], bank[1][0:FV, P:2 * P]).then_inc(s_c_cp, 1)
                dve.wait_ge(s_c_prod, g + 1)
                nc.vector.tensor_copy(c_y[:], bank[5][:, 256:256 + F])
                then(nc.vector.tensor_scalar(c_own[:], bank[5][0:PW, P:P + 2], attn_b_col[0:PW, :], None, ALU.add))
                for half in range(2):
                    last = nc.vector.tensor_scalar(c_logit[:, half, :], bank[5][0:PW, 0:P],
                                                   c_own[:, half:half + 1], None, ALU.add)
                then(last)
                then(nc.vector.scalar_tensor_tensor(c_leaky[:], c_logit[:], LEAK, c_logit[:], ALU.mult, ALU.max))
                then(nc.vector.tensor_tensor(c_leaky[:], c_leaky[:], c_mask[:], ALU.mult))
                then(nc.vector.tensor_tensor(c_logit[:], c_leaky[:], c_wall[:], ALU.add))
                then(nc.vector.tensor_reduce(c_max[:], c_logit[:], AX.X, ALU.max))
                then(nc.vector.tensor_tensor(new_max[:], old_max[:], c_max[:], ALU.max))
                nc.vector.tensor_scalar(minus_max[:], new_max[:], -1.0, None, ALU.mult)
                nc.vector.tensor_tensor(drop[:], old_max[:], new_max[:], ALU.subtract).then_inc(s_c_max, 1)
                dve.wait_ge(s_c_exp, g + 1)
                nc.vector.tensor_tensor(c_weight[:], c_exp[:], c_mask[:], ALU.mult).then_inc(s_c_weight, 1)
                dve.wait_ge(s_c_weight, g + 1)
                nc.vector.tensor_reduce(c_sum[:], c_weight[:], AX.X, ALU.add)
                then(nc.vector.tensor_scalar(scale[:], scale[:], goes_on[0:PW, :], None, ALU.mult))
                then(nc.vector.tensor_tensor(z_sum[:], z_sum[:], scale[:], ALU.mult))
                then(nc.vector.tensor_tensor(z_sum[:], z_sum[:], c_sum[:], ALU.add))
                then(nc.vector.scalar_tensor_tensor(divisor[:], z_sum[:], 0.0, z_sum[:], ALU.is_equal, ALU.add))
                then(nc.vector.reciprocal(inverse[:], divisor[:]))
                dve.wait_ge(s_c_wt, g + 1)
                nc.vector.tensor_copy(c_weight_t[:].rearrange("p j n -> p (j n)"), bank[1][:, 0:2 * PW]
                                      ).then_inc(s_c_wcp, 1)
                dve.wait_ge(s_c_z, g + 1)
                for half in range(2):
                    last = nc.vector.scalar_tensor_tensor(z_acc[:, half, :], z_acc[:, half, :],
                                                          scale[:, half:half + 1],
                                                          bank[4][0:PW, half * F:(half + 1) * F],
                                                          ALU.mult, ALU.add)
                then(last)
                for half in range(2):
                    last = nc.vector.scalar_tensor_tensor(c_h[:, half, :], z_acc[:, half, :],
                                                          inverse[:, half:half + 1],
                                                          bank[3][0:PW, half * F:(half + 1) * F],
                                                          ALU.mult, ALU.add)
                then(last)
                then(nc.vector.scalar_tensor_tensor(c_r[:].rearrange("p j f -> p (j f)"),
                                                    c_h[:].rearrange("p j f -> p (j f)"), 0.0, c_x[:],
                                                    ALU.max, ALU.add))
                for half in range(2):
                    last = nc.vector.bn_stats(c_stats[:, half, :], c_r[:, half, :])
                then(last)
                part(dve)
                for half in range(2):
                    last = nc.vector.bn_aggr(c_moments[:, half, :], c_stats[:, half, :])
                last.then_inc(s_c_var, 1)
                dve.wait_ge(s_c_rstd, g + 1)
                for half in range(2):
                    last = nc.vector.tensor_scalar(c_out[:, half, :], c_r[:, half, :], c_moments[:, half, 0:1],
                                                   c_rstd[:, half:half + 1], ALU.subtract, ALU.mult)
                last.then_inc(s_c_out, 1)
                assert fixed[0] == FIX_STEPS, fixed[0]
            repair(dve, fix)


_INS = ["x", "src", "dst", "edge_attr_32", "L0_gnn_proj_w", "L0_gnn_attn_w", "L0_gnn_attn_b", "L0_gnn_apply_w",
        "L0_gnn_apply_b"]


def kernel(**inputs):
    import numpy as _np
    import concourse.bacc as _bacc
    from concourse import mybir as _mybir
    from concourse.bass_utils import run_bass_kernel_spmd as _run

    nc = _bacc.Bacc("TRN2", target_bir_lowering=False, num_devices=1)
    arrays, args = {}, []
    for name in _INS:
        a = _np.ascontiguousarray(inputs[name])
        arrays[f"in_{name}"] = a
        args.append(nc.dram_tensor(f"in_{name}", a.shape, _mybir.dt.from_np(a.dtype), kind="ExternalInput").ap())
    args.append(nc.dram_tensor("out_0", (N_NODES, F), _mybir.dt.float32, kind="ExternalOutput").ap())
    gnn_kernel(nc, *args)
    r = _run(nc, [arrays], core_ids=[0])
    return r.results[0]["out_0"]
```

```python
import concourse.bass as bass
from concourse import mybir
from contextlib import ExitStack

FP32, BF16, I32 = mybir.dt.float32, mybir.dt.bfloat16, mybir.dt.int32
ALU, ACT, AX = mybir.AluOpType, mybir.ActivationFunctionType, mybir.AxisListType

P = 128
N_NODES, N_EDGES, F, FE = 100000, 50000, 64, 32
FV = F + FE
NPB = 192
PW = NPB // 2
NW = -(-N_NODES // NPB)
NQ = -(-NW // 4)
LAST_NODES = N_NODES - (NW - 1) * NPB
RING = 12
NSB = -(-NQ // 4)
WC = -(-NSB * 16 // 5)
NWP = 5 * WC
RE = 400
RQ = N_EDGES // RE
BIG = 1.0e30
EPS = 1.0e-5
LEAK = 0.2


def gnn_kernel(nc, x, src, dst, ef, proj_w, attn_w, attn_b, apply_w, apply_b, out):
    ef_scratch = nc.dram_tensor("ef_scratch", (NWP, P * FE), FP32, kind="Internal").ap()
    pair_scratch = nc.dram_tensor("pair_scratch", (NWP, P), BF16, kind="Internal").ap()
    local_scratch = nc.dram_tensor("local_scratch", (NWP, P), BF16, kind="Internal").ap()
    first_scratch = nc.dram_tensor("first_scratch", (NWP,), FP32, kind="Internal").ap()

    ctx = ExitStack()
    with ctx:
        def sb(name, shape, dt=FP32):
            return ctx.enter_context(nc.sbuf_tensor(name, shape, dt))

        def sem(name):
            return ctx.enter_context(nc.semaphore(name))

        bank = [ctx.enter_context(nc.psum_tensor(f"bank{i}", [P, 512], FP32)) for i in range(8)]

        iota_i = sb("iota_i", [P, NWP], I32)
        ident = sb("ident", [P, P])
        order_i = sb("order_i", [P, PW], I32)
        order = sb("order", [P, PW])
        node_i = sb("node_i", [P, 2], I32)
        node_id = sb("node_id", [P, 2])
        base_i = sb("base_i", [P, 5], I32)
        base = sb("base", [P, 5])
        starts = sb("starts", [P, NWP])
        part_i = sb("part_i", [P, 1], I32)
        part_f = sb("part_f", [P, 1])
        pair_col_i = iota_i
        ones_col = sb("ones_col", [P, 1])
        ones3 = sb("ones3", [3, P], BF16)
        eps_col = sb("eps_col", [P, 1])
        proj_sb = sb("proj_sb", [F, FV])
        a1_twice = sb("a1_twice", [F, 2 * F])
        a2_sb = sb("a2_sb", [F, F])
        a2_t = sb("a2_t", [F, F])
        edge_w = sb("edge_w", [FV, P])
        node_w = sb("node_w", [P, 2 * F])
        attn_dst = sb("attn_dst", [P, PW])
        attn_b_col = sb("attn_b_col", [P, 1])
        bias_f = sb("bias_f", [3, F])
        bias_rest = sb("bias_rest", [3, F])
        bias_lo = sb("bias_lo", [3, F])
        bias_sum = sb("bias_sum", [3, F])
        bias_hi = sb("bias_hi", [3, F], BF16)
        bias_mid = sb("bias_mid", [3, F], BF16)
        bias3 = sb("bias3", [3, 8 * F], BF16)
        pick = sb("pick", [3, 3])
        local_col = sb("local_col", [P, NWP])
        pair_col = sb("pair_col", [P, NWP])
        parity = sb("parity", [P, NWP, 2])
        src_col = sb("src_col", [P, NWP], I32)
        links = sb("links", [16, NSB, 3, P + 1], BF16)
        same = links[:, :, 0, :]
        apart = links[:, :, 1, :]
        wall = links[:, :, 2, :]
        links_now = sb("links_now", [16, 3, P + 1], BF16)
        first_row = sb("first_row", [P, NWP])
        chunk_no = sb("chunk_no", [P, 1])
        block_no = sb("block_no", [P, 1])
        block_node = sb("block_node", [P, 1])
        last_node = sb("last_node", [P, 1])
        block_key = sb("block_key", [P, 1])
        chunk_begin = sb("chunk_begin", [P, 1])
        chunk_edge = sb("chunk_edge", [P, 1])
        chunk_node = sb("chunk_node", [P, 1])
        total_i = sb("total_i", [P, 1], I32)
        chunk_i = sb("chunk_i", [P, 2], I32)
        src_now = sb("src_now", [P, 2, 24], I32)
        v_sb = sb("v_sb", [P, RING, 4, FV])
        x_sb = sb("x_sb", [PW, RING, 4, 2 * F])
        vt_sb = sb("vt_sb", [FV, 2, 4, P])
        xt_sb = sb("xt_sb", [P, RING, 4, PW])
        y_sb = sb("y_sb", [P, RING, 4, F + 1])
        pair_b = sb("pair_b", [PW, 4, 4 * P], BF16)
        hot_t = sb("hot_t", [PW, 2, 4 * P], BF16)
        sd_rest = sb("sd_rest", [PW, 2, 8])
        sd_parts = sb("sd_parts", [PW, 2, 8, 3], BF16)
        ds_parts = sb("ds_parts", [P, 16, 6])
        dst_score = sb("dst_score", [P, 16])
        logit = sb("logit", [P, 16])
        logit_l = sb("logit_l", [P, 16])
        run_max = sb("run_max", [16, P])
        seg_max = sb("seg_max", [16, P])
        shifted = sb("shifted", [16, P])
        weight = sb("weight", [16, P])
        run_sum = sb("run_sum", [16, P])
        last_sum = sb("last_sum", [16, P])
        seg_sum = sb("seg_sum", [16, P])
        col_rcp = sb("col_rcp", [P, 16])
        col_alpha = sb("col_alpha", [P, 16])
        alpha = sb("alpha", [P, 3, 16, 2])
        hot = sb("hot", [P, 2, 4, PW])
        y2 = sb("y2", [P, 2, 4, 2, F])
        r_sb = sb("r_sb", [PW, 4, 8, F])
        stats = sb("stats", [PW, 4, 8, 6])
        mean2 = sb("mean2", [PW, 4, 8])
        halves = sb("halves", [PW, 4, 8])
        moment = sb("moment", [PW, 4, 8])
        spread = sb("spread", [PW, 4, 8])
        var64 = sb("var64", [PW, 4, 8])
        ln_var = sb("ln_var", [PW, 4, 8])
        rstd = sb("rstd", [PW, 4, 8])
        shift = sb("shift", [PW, 4, 8])
        out_sb = sb("out_sb", [PW, 3, 8, F])

        early = ExitStack()

        def sb_early(name, shape, dt=FP32):
            return early.enter_context(nc.sbuf_tensor(name, shape, dt))

        dst_rows_i = sb_early("dst_rows_i", [RQ, RE], I32)
        dst_rows = sb_early("dst_rows", [RQ, RE])
        prev_i = sb_early("prev_i", [RQ, 1], I32)
        prev_f = sb_early("prev_f", [RQ, 1])
        above_last = sb_early("above_last", [RQ, NWP])
        holds = sb_early("holds", [RQ, NWP])
        below = sb_early("below", [WC, RE])
        count_in_row = sb_early("count_in_row", [WC, 5])
        first_edge = sb_early("first_edge", [WC, 5])
        start_f = sb_early("start_f", [WC, 5])
        start_i = sb_early("start_i", [WC, 5], I32)
        win_dst_i = sb_early("win_dst_i", [WC, 5, P], I32)
        win_src_i = sb_early("win_src_i", [WC, 5, P], I32)
        win_src = sb_early("win_src", [WC, 5, P])
        win_dst = win_src
        local = sb_early("local", [WC, 5, P])
        local16 = sb_early("local16", [WC, 5, P], BF16)
        pair_i = win_dst_i
        pair16 = sb_early("pair16", [WC, 5, P], BF16)
        batch_local = sb_early("batch_local", [16, NSB, P], BF16)
        start_ef = sb_early("start_ef", [WC, 5], I32)
        win_ef = sb_early("win_ef", [WC, P * FE])
        early.close()
        n_edges = sb("n_edges", [P, NW])
        crowded = sb("crowded", [P, NW])
        begin = sb("begin", [P, NW])
        span_i = sb("span_i", [P, NW], I32)
        rest = sb("rest", [P, NW])
        n_chunks = sb("n_chunks", [P, NW])
        ones_row = sb("ones_row", [P, NW])
        chunks_to = sb("chunks_to", [P, NW])
        key = sb("key", [P, NW])
        overlap = sb("overlap", [P, 1])
        goes_on = sb("goes_on", [P, 1])
        reset = sb("reset", [P, 1])
        node_now = sb("node_now", [P, 2])
        c_dst_i = sb("c_dst_i", [PW, P], I32)
        c_dst = sb("c_dst", [PW, P])
        c_src = sb("c_src", [P, 1], I32)
        c_v = sb("c_v", [P, FV])
        c_x = sb("c_x", [PW, 2 * F])
        c_vt = sb("c_vt", [FV, P])
        c_xt = sb("c_xt", [P, PW])
        c_y = sb("c_y", [P, F])
        attn_src_wide = sb("attn_src_wide", [FV, PW])
        valid = sb("valid", [P, P])
        c_mask = sb("c_mask", [PW, 2, P])
        c_wall = sb("c_wall", [PW, 2, P])
        c_own = sb("c_own", [PW, 2])
        c_logit = sb("c_logit", [PW, 2, P])
        c_leaky = sb("c_leaky", [PW, 2, P])
        c_max = sb("c_max", [PW, 2])
        old_max = sb("old_max", [PW, 2])
        new_max = sb("new_max", [PW, 2])
        minus_max = sb("minus_max", [PW, 2])
        drop = sb("drop", [PW, 2])
        scale = sb("scale", [PW, 2])
        c_exp = sb("c_exp", [PW, 2, P])
        c_weight = sb("c_weight", [PW, 2, P])
        c_sum = sb("c_sum", [PW, 2])
        z_sum = sb("z_sum", [PW, 2])
        z_acc = sb("z_acc", [PW, 2, F])
        c_weight_t = sb("c_weight_t", [P, 2, PW])
        divisor = sb("divisor", [PW, 2])
        inverse = sb("inverse", [PW, 2])
        c_h = sb("c_h", [PW, 2, F])
        c_r = sb("c_r", [PW, 2, F])
        c_stats = sb("c_stats", [PW, 2, 6])
        c_moments = sb("c_moments", [PW, 2, 2])
        c_ln = sb("c_ln", [PW, 2])
        c_rstd = sb("c_rstd", [PW, 2])
        c_out = sb("c_out", [PW, 2, F])

        vt_ps = bank[0][0:FV, :].rearrange("p (w e) -> p w e", w=4)
        xt_ps = bank[1][:, 0:4 * PW].rearrange("p (w n) -> p w n", w=4)
        y_ps = bank[2][:, 0:4 * (F + 1)].rearrange("p (w f) -> p w f", w=4)
        h_ps = [bank[3], bank[4]]
        sd_ps = bank[5][0:PW, :].rearrange("p (r c) -> p r c", r=2)[:, :, 0:8]
        ds_ps = bank[6][:, 0:288].rearrange("p (r w c) -> p r w c", r=3, w=16)
        row_ps = bank[7][0:16, 0:P]
        weight_ps = bank[7][:, P:P + 16]
        sum_ps = bank[7][:, P + 16:P + 32]

        s_iota = sem("s_iota")
        s_weights = [sem(f"s_weights{i}") for i in range(11)]
        s_ds = sem("s_ds")
        s_pad = sem("s_pad")
        s_parted = sem("s_parted")
        s_ident = sem("s_ident")
        s_wt = sem("s_wt")
        s_a2t = sem("s_a2t")
        s_ew = sem("s_ew")
        s_holds = sem("s_holds")
        s_rows = sem("s_rows")
        s_local = sem("s_local")
        s_local16 = sem("s_local16")
        s_srcf = sem("s_srcf")
        s_loc_t = sem("s_loc_t")
        s_src_t = sem("s_src_t")
        s_starts = sem("s_starts")
        s_wdst = sem("s_wdst")
        s_wsrc = sem("s_wsrc")
        s_wef = sem("s_wef")
        s_wef_out = sem("s_wef_out")
        s_pair16 = sem("s_pair16")
        s_pair_out = sem("s_pair_out")
        s_local_out = sem("s_local_out")
        s_batch_local = sem("s_batch_local")
        s_setup = sem("s_setup")
        s_src = sem("s_src")
        s_gath = [sem(f"s_gath{i}") for i in range(RING)]
        s_ef = [sem(f"s_ef{i}") for i in range(RING)]
        s_x = [sem(f"s_x{i}") for i in range(RING)]
        s_loc = [sem(f"s_loc{i}") for i in range(4)]
        s_tr = sem("s_tr")
        s_cp = sem("s_cp")
        s_ys = sem("s_ys")
        s_ycp = sem("s_ycp")
        s_hot_t = sem("s_hot_t")
        s_parts = sem("s_parts")
        s_score = sem("s_score")
        s_dst_part = sem("s_dst_part")
        s_logit = sem("s_logit")
        s_links = sem("s_links")
        s_row = sem("s_row")
        s_soft = sem("s_soft")
        s_exp = sem("s_exp")
        s_col = sem("s_col")
        s_alpha_step = sem("s_alpha_step")
        s_alpha = sem("s_alpha")
        s_hot = sem("s_hot")
        s_h = sem("s_h")
        s_r = sem("s_r")
        s_stat = sem("s_stat")
        s_var = sem("s_var")
        s_ln = sem("s_ln")
        s_shift = sem("s_shift")
        s_norm = sem("s_norm")
        s_store = [sem(f"s_store{i}") for i in range(3)]

        s_first_out = sem("s_first_out")
        s_first_row = sem("s_first_row")
        s_total = sem("s_total")
        s_fix = sem("s_fix")
        s_where = sem("s_where")
        s_c_src = sem("s_c_src")
        s_c_dst = sem("s_c_dst")
        s_c_ef = sem("s_c_ef")
        s_c_x = sem("s_c_x")
        s_c_gath = sem("s_c_gath")
        s_c_tr = sem("s_c_tr")
        s_c_cp = sem("s_c_cp")
        s_c_prod = sem("s_c_prod")
        s_c_max = sem("s_c_max")
        s_c_exp = sem("s_c_exp")
        s_c_weight = sem("s_c_weight")
        s_c_wt = sem("s_c_wt")
        s_c_wcp = sem("s_c_wcp")
        s_c_z = sem("s_c_z")
        s_c_var = sem("s_c_var")
        s_c_ln = sem("s_c_ln")
        s_c_rstd = sem("s_c_rstd")
        s_c_out = sem("s_c_out")
        s_c_store = sem("s_c_store")
        FIX_STEPS = 28

        def ge(eng, s, n):
            if not (isinstance(n, int) and n <= 0):
                eng.wait_ge(s, n)

        def part(eng):
            eng.sem_inc(s_parted, 1)

        def quads(eng, step, last_step):
            for q in range(2 * RING):
                step(q, q % RING, q // RING)
            n_rounds = NQ // RING
            with eng.Fori(2, n_rounds) as i:
                for j in range(RING):
                    step(i * RING + j, j, i)
            for q in range(n_rounds * RING, last_step + 1):
                step(q, q % RING, q // RING)

        def all_stored(eng):
            for slot in range(3):
                n = len(range(slot, NQ, 3))
                extra = NW - 4 * (NQ - 1) - 1 if (NQ - 1) % 3 == slot else 0
                eng.wait_ge(s_store[slot], 16 * (n + extra + 1))

        def repair(eng, fix):
            eng.wait_ge(s_total, 1)
            total = eng.value_load(total_i[0:1, 0:1], min_val=0, max_val=2 * NW + N_EDGES // P)
            with eng.If(total > 0):
                with eng.Fori(0, total) as g:
                    fix(g)

        def is_quad(q):
            return not isinstance(q, int) or 0 <= q < NQ

        def is_pair_step(q, j):
            return j % 2 == 0 and is_quad(q - 12)

        def is_batch_step(q, j, lag):
            return (j - lag) % 4 == 3 and (not isinstance(q, int) or 3 <= q - lag < 4 * NSB)

        def slot_round(j, i, lag, ring):
            k = j - lag
            return k % ring, i * (RING // ring) + k // ring + 1

        block = ctx.enter_context(nc.Block())

        @block.sync
        def _(sp):
            for slot in range(3):
                sp.sem_inc(s_store[slot], 16)
            sp.sem_inc(s_norm, 4)
            sp.dma_start(dst_rows_i[:], dst.rearrange("(q e) -> q e", e=RE)).then_inc(s_weights[0], 16)
            sp.wait_ge(s_pad, 1)
            sp.dma_start(prev_i[1:RQ, :], dst[0:(RQ - 1) * RE].rearrange("(q e) -> q e", e=RE)[:, RE - 1:RE],
                         allow_slow_non_contiguous=True).then_inc(s_weights[1], 16)
            sp.dma_start(proj_sb[:], proj_w).then_inc(s_weights[3], 16)
            sp.dma_start(a2_sb[:], apply_w[:, F:2 * F]).then_inc(s_weights[4], 16)
            sp.dma_start(a1_twice[:, 0:F], apply_w[:, 0:F]).then_inc(s_weights[5], 16)
            sp.dma_start(a1_twice[:, F:2 * F], apply_w[:, 0:F]).then_inc(s_weights[6], 16)
            sp.dma_start(edge_w[0:F, F:F + 1], attn_w[:, 0:F].rearrange("o f -> f o"),
                         allow_slow_non_contiguous=True).then_inc(s_weights[7], 16)
            sp.dma_start(attn_dst[0:F, 0:1], attn_w[:, F:2 * F].rearrange("o f -> f o"),
                         allow_slow_non_contiguous=True).then_inc(s_weights[8], 16)
            sp.dma_start(attn_dst[F:P, 1:2], attn_w[:, F:2 * F].rearrange("o f -> f o"),
                         allow_slow_non_contiguous=True).then_inc(s_weights[8], 16)
            sp.dma_start(attn_b_col[:], attn_b.unsqueeze(0).to_broadcast([P, 1])).then_inc(s_weights[9], 16)
            sp.dma_start(bias_f[:], apply_b.unsqueeze(0).to_broadcast([3, F])).then_inc(s_weights[10], 16)
            sp.wait_ge(s_starts, 1)
            sp.dma_start(first_scratch.rearrange("(c p) -> p c", c=5), first_edge[:],
                         allow_slow_non_contiguous=True).then_inc(s_first_out, 16)
            def edge_features(c):
                sp.wait_ge(s_wef, 16 * (c + 1))
                sp.dma_start(ef_scratch[c * WC:(c + 1) * WC, :], win_ef[:]).then_inc(s_wef_out, 16)
            edge_features(0)
            sp.wait_ge(s_local16, 1)
            sp.dma_start(local_scratch.rearrange("(c p) e -> p c e", c=5), local16[:]).then_inc(s_local_out, 16)
            sp.wait_ge(s_pair16, 1)
            sp.dma_start(pair_scratch.rearrange("(c p) e -> p c e", c=5), pair16[:]).then_inc(s_pair_out, 16)
            sp.wait_ge(s_local_out, 16)
            sp.dma_start(batch_local[:], local_scratch[0:NSB * 16, :].rearrange("(k g) e -> g k e", g=16)
                         ).then_inc(s_batch_local, 16)
            sp.wait_ge(s_pair_out, 16)
            sp.wait_ge(s_wef_out, 16)

            sp.wait_ge(s_first_out, 16)
            sp.dma_start(first_row[:], first_scratch.unsqueeze(0).to_broadcast([P, NWP])).then_inc(s_first_row, 16)

            def load(q, j):
                if not is_quad(q):
                    return
                ge(sp, s_r, q - RING + 1)
                ge(sp, s_tr, q - RING + 1)
                if isinstance(q, int) and q == NQ - 1:
                    for w in range(NW - 4 * (NQ - 1)):
                        g = 4 * q + w
                        n_here = min(NPB, N_NODES - g * NPB)
                        sp.dma_start(x_sb[0:n_here // 2, j, w, :],
                                     x[g * NPB:g * NPB + n_here, :].rearrange("(p j) f -> p (j f)", j=2)
                                     ).then_inc(s_x[j], 16)
                else:
                    sp.dma_start(x_sb[:, j, :, :],
                                 x[bass.ds(q * (4 * NPB), 4 * NPB), :].rearrange("(w p j) f -> p w (j f)", w=4, j=2)
                                 ).then_inc(s_x[j], 16)
                sp.dma_start(v_sb[:, j, :, F:FV],
                             ef_scratch[bass.ds(q * 4, 4), :].rearrange("w (e f) -> e w f", f=FE)
                             ).then_inc(s_ef[j], 16)
                ge(sp, s_hot_t, q - 3)
                sp.dma_start(pair_b[:, j % 4, :],
                             pair_scratch[bass.ds(q * 4, 4), :].rearrange("w e -> (w e)").unsqueeze(0)
                             .to_broadcast([PW, 4 * P])).then_inc(s_loc[j % 4], 16)

            def step(q, j, i):
                if isinstance(q, int) and q in (4, 6, 8, 10):
                    edge_features(q // 2 - 1)
                if isinstance(q, int) and q == RING - 1:
                    sp.wait_ge(s_wef_out, 80)
                load(q + 1, (j + 1) % RING)
                m = q - 13
                if is_quad(m):
                    slot = (j - 13) % 3
                    sp.wait_ge(s_norm, m + 5)
                    if isinstance(m, int) and m == NQ - 1:
                        for w in range(NW - 4 * (NQ - 1)):
                            g = 4 * m + w
                            n_here = min(NPB, N_NODES - g * NPB)
                            sp.dma_start(out[g * NPB:g * NPB + n_here, :].rearrange("(p j) f -> p (j f)", j=2),
                                         out_sb[0:n_here // 2, slot, 2 * w:2 * w + 2, :]
                                         .rearrange("p c f -> p (c f)")).then_inc(s_store[slot], 16)
                    else:
                        sp.dma_start(out[bass.ds(m * (4 * NPB), 4 * NPB), :]
                                     .rearrange("(w p j) f -> p w (j f)", w=4, j=2),
                                     out_sb[:, slot, :, :].rearrange("p (w j) f -> p w (j f)", w=4)
                                     ).then_inc(s_store[slot], 16)
            load(0, 0)
            quads(sp, step, NQ - 1 + 13)
            all_stored(sp)


        @block.gpsimd
        def _(pool):
            nc.gpsimd.iota(iota_i[:, 0:P], pattern=[[1, P]], base=0, channel_multiplier=-1).then_inc(s_iota, 1)
            nc.gpsimd.iota(order_i[:], pattern=[[1, PW]], base=0, channel_multiplier=0).then_inc(s_iota, 1)
            nc.gpsimd.iota(node_i[:], pattern=[[1, 2]], base=0, channel_multiplier=2).then_inc(s_iota, 1)
            nc.gpsimd.iota(base_i[:], pattern=[[NPB * WC, 5]], base=0, channel_multiplier=NPB).then_inc(s_iota, 1)
            nc.gpsimd.iota(part_i[:], pattern=[[0, 1]], base=0, channel_multiplier=1).then_inc(s_iota, 1)
            pool.wait_ge(s_ident, 1)
            nc.gpsimd.iota(iota_i[:], pattern=[[NPB, NWP]], base=0, channel_multiplier=0).then_inc(s_iota, 1)
            pool.wait_ge(s_starts, 1)
            def edge_features(c):
                ge(pool, s_wef_out, 16 * c)
                pool.indirect_dma_start(out=win_ef[:], out_offset=None,
                                        in_=ef.rearrange("a b -> (a b)").unsqueeze(0),
                                        in_offset=bass.IndirectOffsetOnAxis(ap=start_ef[:, c:c + 1], axis=1)
                                        ).then_inc(s_wef, 16)
            edge_features(0)
            for c in range(5):
                pool.indirect_dma_start(out=win_src_i[:, c, :], out_offset=None, in_=src.unsqueeze(0),
                                        in_offset=bass.IndirectOffsetOnAxis(ap=start_i[:, c:c + 1], axis=1)
                                        ).then_inc(s_wsrc, 16)
            for c in range(5):
                pool.indirect_dma_start(out=win_dst_i[:, c, :], out_offset=None, in_=dst.unsqueeze(0),
                                        in_offset=bass.IndirectOffsetOnAxis(ap=start_i[:, c:c + 1], axis=1)
                                        ).then_inc(s_wdst, 16)


            def step(q, j, i):
                if not is_quad(q):
                    return
                if isinstance(q, int) and q in (4, 6, 8, 10):
                    edge_features(q // 2 - 1)
                if j % 6 == 0:
                    pool.wait_ge(s_src, i * 2 + j // 6 + 1)
                ge(pool, s_tr, q - RING + 1)
                part(pool)
                for w in range(4):
                    pool.indirect_dma_start(out=v_sb[:, j, w, 0:F], out_offset=None, in_=x,
                                            in_offset=bass.IndirectOffsetOnAxis(
                                                ap=src_now[:, j // 6, 4 * (j % 6) + w:4 * (j % 6) + w + 1], axis=0)
                                            ).then_inc(s_gath[j], 16)
            quads(pool, step, NQ - 1)

            def fix(g):
                pool.wait_ge(s_where, g + 1)
                part(pool)
                edge = pool.value_load(chunk_i[0:1, 0:1], min_val=0, max_val=N_EDGES - P)
                node = pool.value_load(chunk_i[0:1, 1:2], min_val=0, max_val=N_NODES - NPB)
                pool.dma_start(c_src[:], src[bass.ds(edge, P)].unsqueeze(1),
                               allow_slow_non_contiguous=True).then_inc(s_c_src, 16)
                pool.dma_start(c_x[:], x[bass.ds(node, NPB), :].rearrange("(p j) f -> p (j f)", j=2)
                               ).then_inc(s_c_x, 16)
                pool.dma_start(c_v[:, F:FV], ef[bass.ds(edge, P), :]).then_inc(s_c_ef, 16)
                pool.wait_ge(s_c_src, g * 16 + 16)
                part(pool)
                pool.indirect_dma_start(out=c_v[:, 0:F], out_offset=None, in_=x,
                                        in_offset=bass.IndirectOffsetOnAxis(ap=c_src[:, 0:1], axis=0)
                                        ).then_inc(s_c_gath, 16)
                pool.dma_start(c_dst_i[:], dst[bass.ds(edge, P)].unsqueeze(0).to_broadcast([PW, P])
                               ).then_inc(s_c_dst, 16)
                pool.wait_ge(s_c_out, g + 1)
                part(pool)
                all_stored(pool)
                pool.dma_start(out[bass.ds(node, NPB), :].rearrange("(p j) f -> p (j f)", j=2),
                               c_out[:].rearrange("p j f -> p (j f)")).then_inc(s_c_store, 16)
                pool.wait_ge(s_c_store, g * 16 + 16)
                part(pool)
            repair(pool, fix)

        @block.scalar
        def _(act):
            nc.scalar.preload_act_table_set("natural_log_exp_and_others")

            def step(q, j, i):
                a, m = q - 1, q - 13
                if is_quad(a):
                    act.wait_ge(s_ys, a + 1)
                    nc.scalar.copy(y_sb[:, (j - 1) % RING, :, :], y_ps).then_inc(s_ycp, 1)
                if is_quad(q):
                    act.wait_ge(s_tr, q + 1)
                    ge(act, s_ys, q - 1)
                    nc.scalar.copy(vt_sb[:, j % 2, :, :], vt_ps)
                    ge(act, s_h, q - RING + 1)
                    nc.scalar.copy(xt_sb[:, j, :, :], xt_ps).then_inc(s_cp, 1)
                    if j % 6 == 5 and not (isinstance(q, int) and q + 7 >= NQ):
                        act.wait_ge(s_setup, 1)
                        nc.scalar.copy(src_now[:, j // 6, :], src_col[:, bass.ds((q + 7) * 4, 24)]).then_inc(s_src, 1)
                if is_pair_step(q, j):
                    t, at = i * 6 + (j - 12) // 2, (j - 12) % 4
                    act.wait_ge(s_var, t * 3 + 3)
                    nc.scalar.activation(ln_var[:, at:at + 2, :], var64[:, at:at + 2, :], ACT.Ln,
                                         bias=eps_col[0:PW, :], scale=1.0 / F).then_inc(s_ln, 1)
                if is_pair_step(q, j):
                    act.wait_ge(s_ln, t * 2 + 1)
                    nc.scalar.activation(rstd[:, at:at + 2, :], ln_var[:, at:at + 2, :], ACT.Exp,
                                         scale=-0.5).then_inc(s_ln, 1)
                if is_quad(m):
                    act.wait_ge(s_shift, i * 6 + (j - 13) // 2 + 1)
                    slot, n = slot_round(j, i, 13, 3)
                    act.wait_ge(s_store[slot], 16 * n)
                    for b in range(8):
                        last = nc.scalar.activation(out_sb[:, slot, b, :], r_sb[:, (j - 13) % 4, b, :], ACT.Identity,
                                                    bias=shift[:, (j - 13) % 4, b:b + 1],
                                                    scale=rstd[:, (j - 13) % 4, b:b + 1])
                    last.then_inc(s_norm, 1)
                if is_batch_step(q, j, 3):
                    k = i * 3 + (j - 6) // 4
                    act.wait_ge(s_soft, k * 6 + 3)
                    ge(act, s_col, k)
                    nc.scalar.activation(weight[:], shifted[:], ACT.Exp).then_inc(s_exp, 1)
            quads(act, step, NQ - 1 + 13)

            def fix(g):
                act.wait_ge(s_c_max, g + 1)
                nc.scalar.activation(scale[:], drop[:], ACT.Exp)
                for half in range(2):
                    last = nc.scalar.activation(c_exp[:, half, :], c_logit[:, half, :], ACT.Exp,
                                                bias=minus_max[:, half:half + 1])
                last.then_inc(s_c_exp, 1)
                act.wait_ge(s_c_var, g + 1)
                nc.scalar.activation(c_ln[:], c_moments[:, :, 1], ACT.Ln, bias=eps_col[0:PW, :]
                                     ).then_inc(s_c_ln, 1)
                act.wait_ge(s_c_ln, g + 1)
                nc.scalar.activation(c_rstd[:], c_ln[:], ACT.Exp, scale=-0.5).then_inc(s_c_rstd, 1)
            repair(act, fix)

        @block.tensor
        def _(pe):
            pe.wait_ge(s_ident, 2)
            pe.wait_ge(s_weights[4], 16)
            nc.tensor.transpose(bank[0][0:F, 0:F], a2_sb[:], ident[0:F, 0:F])
            pe.wait_ge(s_weights[5], 16)
            pe.wait_ge(s_weights[6], 16)
            nc.tensor.transpose(bank[0][:, 64:128], a1_twice[:], ident[0:F, 0:F]).then_inc(s_wt, 1)
            pe.wait_ge(s_a2t, 1)
            pe.wait_ge(s_weights[3], 16)
            nc.tensor.matmul(bank[1][0:FV, 0:F], proj_sb[:], a2_t[:], start=True, stop=True).then_inc(s_ew, 1)
            pe.wait_ge(s_holds, 1)
            for c in range(5):
                nc.tensor.matmul(bank[2][0:WC, c:c + 1], above_last[:, c * WC:(c + 1) * WC], ones_col[0:RQ, :],
                                 start=True, stop=True)
            for c in range(5):
                nc.tensor.matmul(bank[3 + c][0:WC, 0:RE], holds[:, c * WC:(c + 1) * WC], dst_rows[:],
                                 start=True, stop=True).then_inc(s_rows, 1)
            pe.wait_ge(s_srcf, 1)
            for c in range(4):
                nc.tensor.transpose(bank[1][:, c * WC:(c + 1) * WC], win_src[:, c, :], ident[0:WC, 0:WC])
            nc.tensor.transpose(bank[3][:, 0:WC], win_src[:, 4, :], ident[0:WC, 0:WC]).then_inc(s_src_t, 1)
            pe.wait_ge(s_local, 1)
            for c in range(4):
                nc.tensor.transpose(bank[0][:, c * WC:(c + 1) * WC], local[:, c, :], ident[0:WC, 0:WC])
            nc.tensor.transpose(bank[2][:, 0:WC], local[:, 4, :], ident[0:WC, 0:WC]).then_inc(s_loc_t, 1)
            pe.wait_ge(s_setup, 1)

            def step(q, j, i):
                a, b, c = q - 1, q - 2, q - 9
                if is_quad(a):
                    pe.wait_ge(s_cp, a + 1)
                    ge(pe, s_ycp, a)
                    for w in range(4):
                        at = w * (F + 1)
                        nc.tensor.matmul(bank[2][:, at:at + P], vt_sb[:, (j - 1) % 2, w, :], edge_w[:],
                                         start=True, stop=True)
                    ge(pe, s_parts, a * 4 - 2)
                    for w in range(4):
                        at = 256 * ((j - 1) % 2) + 2 * w
                        last = nc.tensor.matmul(bank[5][0:PW, at:at + PW],
                                                xt_sb[:, (j - 1) % RING, w, :], attn_dst[:], start=True, stop=True)
                    last.then_inc(s_ys, 1)
                if is_quad(b):
                    pe.wait_ge(s_parts, b * 4 + 4)
                    pe.wait_ge(s_hot_t, b + 1)
                    kd = (j - 2) // 4 % 3
                    if (j - 2) % 4 == 0:
                        ge(pe, s_dst_part, i * 3 + (j - 2) // 4)
                    for w in range(4):
                        last = nc.tensor.matmul(ds_ps[:, kd, 4 * ((j - 2) % 4) + w, :],
                                                hot_t[:, (j - 2) % 2, w * P:(w + 1) * P],
                                                sd_parts[:, (j - 2) % 2, 2 * w:2 * w + 2, :]
                                                .rearrange("p j t -> p (j t)"), start=True, stop=True)
                    last.then_inc(s_score, 1)
                if is_batch_step(q, j, 3):
                    k = i * 3 + (j - 6) // 4
                    pe.wait_ge(s_logit, k * 3 + 3)
                    ge(pe, s_alpha, k)
                    nc.tensor.transpose(row_ps, logit_l[:], ident[:]).then_inc(s_row, 1)
                if is_batch_step(q, j, 5):
                    k = i * 3 + (j - 8) // 4
                    pe.wait_ge(s_soft, k * 6 + 6)
                    part(pe)
                    nc.tensor.transpose(weight_ps, weight[:], ident[0:16, 0:16])
                    nc.tensor.transpose(sum_ps, seg_sum[:], ident[0:16, 0:16]).then_inc(s_col, 1)
                if is_quad(q):
                    pe.wait_ge(s_gath[j], i * 64 + 64)
                    pe.wait_ge(s_ef[j], i * 16 + 16)
                    ge(pe, s_cp, q)
                    for w in range(4):
                        nc.tensor.transpose(vt_ps[:, w, :], v_sb[:, j, w, :], ident[:])
                    pe.wait_ge(s_x[j], i * 16 + 16)
                    for w in range(4):
                        last = nc.tensor.transpose(xt_ps[:, w, :], x_sb[:, j, w, :], ident[0:PW, 0:PW])
                    last.then_inc(s_tr, 1)
                if is_quad(c):
                    h = h_ps[(j - 9) % 2]
                    ge(pe, s_r, c - 1)
                    nc.tensor.matmul(h[0:PW, :], ones3[:, 0:PW], bias3[:], start=True, stop=False)
                    for w in range(4):
                        at = w * 2 * F
                        nc.tensor.matmul(h[0:PW, at:at + 2 * F], xt_sb[:, (j - 9) % RING, w, :], node_w[:],
                                         start=False, stop=False)
                        if w == 0:
                            pe.wait_ge(s_hot, c + 1)
                        last = nc.tensor.matmul(h[0:PW, at:at + 2 * F], hot[:, (j - 9) % 2, w, :],
                                                y2[:, (j - 9) % 2, w, :, :].rearrange("p j f -> p (j f)"),
                                                start=False, stop=(w == 3))
                    last.then_inc(s_h, 1)
            quads(pe, step, NQ - 1 + 9)

            pe.wait_ge(s_cp, NQ)
            pe.wait_ge(s_parts, 4 * NQ)
            pe.wait_ge(s_r, NQ)

            def fix(g):
                pe.wait_ge(s_c_x, g * 16 + 16)
                nc.tensor.transpose(bank[1][:, 0:PW], c_x[:], ident[0:PW, 0:PW])
                pe.wait_ge(s_c_gath, g * 16 + 16)
                pe.wait_ge(s_c_ef, g * 16 + 16)
                nc.tensor.transpose(bank[1][0:FV, P:2 * P], c_v[:], ident[:]).then_inc(s_c_tr, 1)
                pe.wait_ge(s_c_cp, g + 1)
                nc.tensor.matmul(bank[5][0:PW, 0:P], attn_src_wide[:], c_vt[:], start=True, stop=True)
                nc.tensor.matmul(bank[5][0:PW, P:P + 2], c_xt[:], attn_dst[:, 0:2], start=True, stop=True)
                nc.tensor.matmul(bank[5][:, 256:256 + F], c_vt[:], edge_w[:, 0:F], start=True, stop=True
                                 ).then_inc(s_c_prod, 1)
                nc.tensor.matmul(bank[3][0:PW, 0:2 * F], c_xt[:], node_w[:], start=True, stop=False)
                nc.tensor.matmul(bank[3][0:PW, 0:2 * F], ones3[:, 0:PW], bias3[:, 0:2 * F], start=False, stop=True)
                pe.wait_ge(s_c_weight, g + 1)
                for half in range(2):
                    last = nc.tensor.transpose(bank[1][:, half * PW:(half + 1) * PW], c_weight[:, half, :],
                                               ident[0:PW, 0:PW])
                last.then_inc(s_c_wt, 1)
                pe.wait_ge(s_c_wcp, g + 1)
                for half in range(2):
                    last = nc.tensor.matmul(bank[4][0:PW, half * F:(half + 1) * F], c_weight_t[:, half, :], c_y[:],
                                            start=True, stop=True)
                last.then_inc(s_c_z, 1)
            repair(pe, fix)

        @block.vector
        def _(dve):
            steps = [0]

            def done(ins):
                steps[0] += 1
                ins.then_inc(s_ds, 1)
                dve.wait_ge(s_ds, steps[0])

            nc.vector.memset(prev_i[:], -1)
            nc.vector.memset(edge_w[:], 0.0)
            nc.vector.memset(attn_dst[:], 0.0).then_inc(s_pad, 1)
            nc.vector.memset(ones_col[:], 1.0)
            dve.wait_ge(s_iota, 1)
            nc.vector.tensor_copy(ident[:], iota_i[:, 0:P]).then_inc(s_ident, 1)
            dve.wait_ge(s_ident, 1)
            nc.vector.tensor_scalar(ident[:], ident[:], 0.0, None, ALU.is_equal).then_inc(s_ident, 1)
            dve.wait_ge(s_iota, 6)
            nc.vector.tensor_copy(order[:], order_i[:])
            nc.vector.tensor_copy(node_id[:], node_i[:])
            nc.vector.tensor_copy(base[:], base_i[:])
            nc.vector.tensor_copy(part_f[:], part_i[:])
            nc.vector.tensor_copy(starts[:], iota_i[:])
            for s in range(2):
                dve.wait_ge(s_weights[s], 16)
            nc.vector.tensor_copy(dst_rows[:], dst_rows_i[:])
            done(nc.vector.tensor_copy(prev_f[:], prev_i[:]))
            nc.vector.tensor_scalar(above_last[:], starts[0:RQ, :], dst_rows[:, RE - 1:RE], None, ALU.is_gt)
            done(nc.vector.tensor_scalar(holds[:], starts[0:RQ, :], prev_f[:], None, ALU.is_gt))
            nc.vector.tensor_tensor(holds[:], holds[:], above_last[:], ALU.subtract).then_inc(s_holds, 1)
            nc.vector.memset(ones3[:], 1.0)
            nc.vector.memset(eps_col[:], EPS)
            nc.vector.memset(same[:, :, 0:1], 0.0)
            nc.vector.memset(same[:, :, P:P + 1], 0.0)
            done(nc.vector.memset(node_w[:], 0.0))
            dve.wait_ge(s_wt, 1)
            nc.vector.tensor_copy(a2_t[:], bank[0][0:F, 0:F]).then_inc(s_a2t, 1)
            nc.vector.tensor_copy(node_w[0:F, 0:F], bank[0][0:F, 64:128])
            nc.vector.tensor_copy(node_w[F:P, F:2 * F], bank[0][F:P, 64:128])
            for c in range(5):
                dve.wait_ge(s_rows, c + 1)
                done(nc.vector.tensor_scalar(below[:], bank[3 + c][0:WC, 0:RE], base[0:WC, c:c + 1], None, ALU.is_lt,
                                             ALU.add, accum_out=count_in_row[:, c:c + 1]))
            done(nc.vector.scalar_tensor_tensor(first_edge[:], bank[2][0:WC, 0:5], float(RE), count_in_row[:],
                                                ALU.mult, ALU.add))
            done(nc.vector.tensor_scalar(first_edge[:], first_edge[:], float(N_EDGES), None, ALU.min))
            done(nc.vector.tensor_scalar(start_f[:], first_edge[:], float(N_EDGES - P), None, ALU.min))
            nc.vector.tensor_copy(start_i[:], start_f[:])
            nc.vector.tensor_scalar(start_ef[:], start_f[:], float(FE), None, ALU.mult).then_inc(s_starts, 1)
            dve.wait_ge(s_ew, 1)
            dve.wait_ge(s_weights[7], 16)
            nc.vector.tensor_copy(edge_w[:, 0:F], bank[1][0:FV, 0:F])
            dve.wait_ge(s_weights[10], 16)
            done(nc.vector.tensor_copy(bias_hi[:], bias_f[:]))
            done(nc.vector.tensor_tensor(bias_rest[:], bias_f[:], bias_hi[:], ALU.subtract))
            done(nc.vector.tensor_copy(bias_mid[:], bias_rest[:]))
            nc.vector.tensor_tensor(bias_lo[:], bias_rest[:], bias_mid[:], ALU.subtract)
            for k in range(3):
                last = nc.vector.tensor_scalar(pick[:, k:k + 1], part_f[0:3, :], float(k), None, ALU.is_equal)
            done(last)
            done(nc.vector.tensor_scalar(bias_sum[:], bias_hi[:], pick[:, 0:1], None, ALU.mult))
            done(nc.vector.scalar_tensor_tensor(bias_sum[:], bias_mid[:], pick[:, 1:2], bias_sum[:],
                                                ALU.mult, ALU.add))
            done(nc.vector.scalar_tensor_tensor(bias_sum[:], bias_lo[:], pick[:, 2:3], bias_sum[:],
                                                ALU.mult, ALU.add))
            done(nc.vector.tensor_copy(bias3[:].rearrange("p (n f) -> p n f", f=F),
                                       bias_sum[:].unsqueeze(1).to_broadcast([3, 8, F])))
            dve.wait_ge(s_wsrc, 80)
            nc.vector.tensor_copy(win_src[:], win_src_i[:]).then_inc(s_srcf, 1)
            dve.wait_ge(s_src_t, 1)
            nc.vector.tensor_copy(src_col[:, 0:4 * WC], bank[1][:, 0:4 * WC])
            done(nc.vector.tensor_copy(src_col[:, 4 * WC:NWP], bank[3][:, 0:WC]))
            nc.vector.tensor_copy(src_now[:].rearrange("p h c -> p (h c)"), src_col[:, 0:48]).then_inc(s_src, 2)
            dve.wait_ge(s_wdst, 80)
            done(nc.vector.tensor_copy(win_dst[:], win_dst_i[:]))
            for c in range(5):
                last = nc.vector.tensor_scalar(local[:, c, :], win_dst[:, c, :], base[0:WC, c:c + 1], -1.0,
                                               ALU.subtract, ALU.max)
            done(last)
            nc.vector.tensor_scalar(local[:], local[:], float(NPB), None, ALU.min).then_inc(s_local, 1)
            dve.wait_ge(s_local, 1)
            nc.vector.tensor_copy(local16[:], local[:]).then_inc(s_local16, 1)
            done(nc.vector.tensor_copy(pair_i[:], local[:]))
            done(nc.vector.tensor_scalar(pair_i[:], pair_i[:], 1, None, ALU.arith_shift_right))
            nc.vector.tensor_copy(pair16[:], pair_i[:]).then_inc(s_pair16, 1)
            dve.wait_ge(s_loc_t, 1)
            nc.vector.tensor_copy(local_col[:, 0:4 * WC], bank[0][:, 0:4 * WC])
            done(nc.vector.tensor_copy(local_col[:, 4 * WC:NWP], bank[2][:, 0:WC]))
            dve.wait_ge(s_weights[8], 32)
            dve.wait_ge(s_weights[9], 16)
            nc.vector.memset(alpha[:], 0.0).then_inc(s_setup, 1)
            done(nc.vector.tensor_copy(pair_col_i[:], local_col[:]))
            done(nc.vector.tensor_scalar(pair_col_i[:], pair_col_i[:], 1, None, ALU.arith_shift_right))
            done(nc.vector.tensor_copy(pair_col[:], pair_col_i[:]))
            done(nc.vector.scalar_tensor_tensor(parity[:, :, 1], pair_col[:], -2.0, local_col[:],
                                                ALU.mult, ALU.add))
            nc.vector.tensor_scalar(parity[:, :, 0], parity[:, :, 1], -1.0, 1.0, ALU.mult, ALU.add)
            def chunk_table(n):
                if n == 1:
                    dve.wait_ge(s_first_row, 16)
                    nc.vector.memset(ones_row[:], 1.0)
                    nc.vector.tensor_copy(begin[:], first_row[:, 0:NW])
                    done(nc.vector.tensor_tensor(n_edges[:], first_row[:, 1:NW + 1], first_row[:, 0:NW],
                                                 ALU.subtract))
                elif n == 2:
                    nc.vector.tensor_copy(begin[:, NW - 1:NW], first_row[:, NW - 2:NW - 1])
                    done(nc.vector.tensor_scalar(crowded[:], n_edges[:], float(P), None, ALU.is_gt))
                elif n == 3:
                    done(nc.vector.scalar_tensor_tensor(span_i[:], first_row[:, 1:NW + 1], float(P - 1), begin[:],
                                                        ALU.add, ALU.subtract))
                elif n == 4:
                    done(nc.vector.tensor_scalar(span_i[:], span_i[:], 7, None, ALU.arith_shift_right))
                elif n == 5:
                    done(nc.vector.tensor_tensor(n_chunks[:], span_i[:], crowded[:], ALU.mult))
                elif n == 6:
                    done(nc.vector.tensor_tensor_scan(chunks_to[:], ones_row[:], n_chunks[:], 0.0, ALU.mult,
                                                      ALU.add))
                    nc.vector.tensor_copy(total_i[:], chunks_to[:, NW - 1:NW]).then_inc(s_total, 1)
                elif n == 7:
                    done(nc.vector.tensor_tensor(rest[:], n_chunks[:], chunks_to[:], ALU.subtract))
                elif n == 8:
                    nc.vector.memset(chunk_no[:], 0.0)
                    done(nc.vector.scalar_tensor_tensor(key[:], rest[:], float(P), begin[:], ALU.mult, ALU.add))

            def where(then, n):
                if n == 1:
                    then(nc.vector.tensor_scalar(rest[:], chunks_to[:], chunk_no[:], None, ALU.is_le, ALU.add,
                                                 accum_out=block_no[:]))
                    then(nc.vector.tensor_scalar(block_node[:], block_no[:], float(NPB), None, ALU.mult))
                elif n == 2:
                    then(nc.vector.tensor_scalar(rest[:], starts[:, 0:NW], block_node[:], None, ALU.is_equal))
                elif n == 3:
                    then(nc.vector.tensor_tensor(rest[:], rest[:], key[:], ALU.mult))
                elif n == 4:
                    then(nc.vector.tensor_reduce(block_key[:], rest[:], AX.X, ALU.add))
                else:
                    nc.vector.tensor_scalar(chunk_node[:], block_node[:], float(N_NODES - NPB), None, ALU.min)
                    then(nc.vector.scalar_tensor_tensor(chunk_begin[:], chunk_no[:], float(P), block_key[:],
                                                        ALU.mult, ALU.add))
                    nc.vector.tensor_scalar(chunk_no[:], chunk_no[:], 1.0, None, ALU.add)
                    then(nc.vector.tensor_scalar(chunk_edge[:], chunk_begin[:], float(N_EDGES - P), None, ALU.min))
                    nc.vector.tensor_copy(chunk_i[:, 0:1], chunk_edge[:])
                    nc.vector.tensor_copy(chunk_i[:, 1:2], chunk_node[:]).then_inc(s_where, 1)

            def link():
                dve.wait_ge(s_batch_local, 16)
                done(nc.vector.tensor_tensor(same[:, :, 1:P], batch_local[:, :, 1:P], batch_local[:, :, 0:P - 1],
                                             ALU.is_equal))
                nc.vector.tensor_scalar(apart, same, -1.0, 1.0, ALU.mult, ALU.add)
                done(nc.vector.tensor_scalar(wall, same, -1.0, BIG, ALU.add, ALU.mult))

            def step(q, j, i):
                a, c, e = q - 1, q - 9, q - 10
                if isinstance(q, int) and q == 3:
                    link()
                if isinstance(q, int) and 3 < q < RING:
                    chunk_table(q - 3)
                if isinstance(q, int) and q == RING - 1:
                    for n in range(1, 6):
                        where(done, n)

                def variance(n):
                    if not is_pair_step(q, j):
                        return
                    k, at = i * 6 + (j - 12) // 2, (j - 12) % 4
                    mine = [v[:, at:at + 2, :] for v in (halves, mean2, moment, spread, var64)]
                    if n == 1:
                        st = stats[:, at:at + 2, :, :]
                        upto = min(q - 10, NQ) if isinstance(q, int) else q - 10
                        dve.wait_ge(s_stat, upto)
                        nc.vector.tensor_tensor(mine[0], st[:, :, :, 1], st[:, :, :, 4], ALU.subtract)
                        nc.vector.tensor_tensor(mine[1], st[:, :, :, 1], st[:, :, :, 4], ALU.add)
                        nc.vector.tensor_tensor(mine[2], st[:, :, :, 2], st[:, :, :, 5], ALU.add
                                                ).then_inc(s_var, 1)
                    elif n == 2:
                        dve.wait_ge(s_var, k * 3 + 1)
                        nc.vector.scalar_tensor_tensor(mine[3], mine[0], F / 4.0, mine[0], ALU.mult, ALU.mult
                                                       ).then_inc(s_var, 1)
                    else:
                        dve.wait_ge(s_var, k * 3 + 2)
                        nc.vector.tensor_tensor(mine[4], mine[3], mine[2], ALU.add).then_inc(s_var, 1)

                if j % 2 == 1 and is_quad(q - 13):
                    k, at = i * 6 + (j - 13) // 2, (j - 13) % 4
                    dve.wait_ge(s_ln, k * 2 + 2)
                    nc.vector.scalar_tensor_tensor(shift[:, at:at + 2, :], mean2[:, at:at + 2, :], -0.5,
                                                   rstd[:, at:at + 2, :], ALU.mult, ALU.mult).then_inc(s_shift, 1)
                if is_quad(c):
                    ge(dve, s_h, c - 1)
                    nc.vector.tensor_tensor(hot[:, (j - 9) % 2, :, :],
                                            order[:].unsqueeze(1).to_broadcast([P, 4, PW]),
                                            pair_col[:, bass.ds(c * 4, 4)].unsqueeze(2).to_broadcast([P, 4, PW]),
                                            ALU.is_equal)
                variance(1)
                if is_quad(c):
                    kc, at = (j - 9) // 4, 4 * ((j - 9) % 4)
                    dve.wait_ge(s_alpha, i * 3 + kc + 1)
                    nc.vector.tensor_tensor(y2[:, (j - 9) % 2, :, :, :],
                                            y_sb[:, (j - 9) % RING, :, 0:F].unsqueeze(2)
                                            .to_broadcast([P, 4, 2, F]),
                                            alpha[:, kc % 3, at:at + 4, :].unsqueeze(3).to_broadcast([P, 4, 2, F]),
                                            ALU.mult).then_inc(s_hot, 1)
                variance(2)
                if is_quad(a):
                    slot, n = slot_round(j, i, 1, 4)
                    dve.wait_ge(s_loc[slot], n * 16)
                    ge(dve, s_score, a - 1)
                    nc.vector.tensor_scalar(hot_t[:, (j - 1) % 2, :], pair_b[:, slot, :], part_f[0:PW, :], None,
                                            ALU.is_equal).then_inc(s_hot_t, 1)
                variance(3)
                if is_quad(e):
                    dve.wait_ge(s_h, e + 1)
                    dve.wait_ge(s_norm, e + 1)
                    nc.vector.scalar_tensor_tensor(r_sb[:, (j - 10) % 4, :, :].rearrange("p c f -> p (c f)"),
                                                   h_ps[(j - 10) % 2][0:PW, :], 0.0,
                                                   x_sb[:, (j - 10) % RING, :, :].rearrange("p w f -> p (w f)"),
                                                   ALU.max, ALU.add).then_inc(s_r, 1)

                part16 = [sd_parts[:, (j - 1) % 2, :, t] for t in range(3)]
                scores = sd_ps[:, (j - 1) % 2, :]
                same_now, apart_now, wall_now = [links_now[:, t, :] for t in range(3)]

                def moments(first, end):
                    if not is_quad(e):
                        return
                    if first == 0:
                        dve.wait_ge(s_r, e + 1)
                    for b in range(first, end):
                        last = nc.vector.bn_stats(stats[:, (j - 10) % 4, b, :], r_sb[:, (j - 10) % 4, b, :])
                    if end == 8:
                        last.then_inc(s_stat, 1)

                def split(n):
                    if not is_quad(a):
                        return
                    if n == 0:
                        dve.wait_ge(s_ys, a + 1)
                        nc.vector.tensor_copy(part16[0], scores).then_inc(s_parts, 1)
                        return
                    dve.wait_ge(s_parts, a * 4 + n)
                    if n == 1:
                        nc.vector.tensor_tensor(sd_rest[:, (j - 1) % 2, :], scores, part16[0],
                                                ALU.subtract).then_inc(s_parts, 1)
                    elif n == 2:
                        nc.vector.tensor_copy(part16[1], sd_rest[:, (j - 1) % 2, :]).then_inc(s_parts, 1)
                    else:
                        nc.vector.tensor_tensor(part16[2], sd_rest[:, (j - 1) % 2, :], part16[1],
                                                ALU.subtract).then_inc(s_parts, 1)

                def batch(n):
                    if is_batch_step(q, j, 2):
                        logits(n, i * 3 + (j - 5) // 4)
                    elif is_batch_step(q, j, 3):
                        maxima(n, i * 3 + (j - 6) // 4)
                    elif is_batch_step(q, j, 4):
                        sums(n, i * 3 + (j - 7) // 4)
                    elif is_batch_step(q, j, 5):
                        alphas(n, i * 3 + (j - 8) // 4)

                def logits(n, k):
                    if n == 1:
                        upto = min(q - 1, NQ) if isinstance(q, int) else q - 1
                        dve.wait_ge(s_score, upto)
                        nc.vector.tensor_tensor(ds_parts[:].rearrange("p w (j t) -> p w j t", j=2),
                                                ds_ps[:, (j - 5) // 4 % 3, :, :]
                                                .rearrange("p w (j t) -> p w j t", j=2),
                                                parity[:, bass.ds(k * 16, 16), :].unsqueeze(3)
                                                .to_broadcast([P, 16, 2, 3]), ALU.mult).then_inc(s_dst_part, 1)
                    elif n == 2:
                        dve.wait_ge(s_dst_part, k + 1)
                        nc.vector.tensor_reduce(dst_score[:], ds_parts[:], AX.X, ALU.add).then_inc(s_logit, 1)
                    elif n == 3:
                        sl = (j - 5) % RING
                        upto = min(q - 1, NQ) if isinstance(q, int) else q - 1
                        dve.wait_ge(s_ycp, upto)
                        dve.wait_ge(s_logit, k * 3 + 1)
                        nc.vector.scalar_tensor_tensor(logit[:].rearrange("p (a w) -> p a w", w=4),
                                                       dst_score[:].rearrange("p (a w) -> p a w", w=4),
                                                       attn_b_col[:], y_sb[:, sl:sl + 4, :, F], ALU.add, ALU.add
                                                       ).then_inc(s_logit, 1)
                    elif n == 4:
                        dve.wait_ge(s_logit, k * 3 + 2)
                        ge(dve, s_row, k)
                        nc.vector.scalar_tensor_tensor(logit_l[:], logit[:], LEAK, logit[:], ALU.mult, ALU.max
                                                       ).then_inc(s_logit, 1)
                    elif n == 5:
                        nc.vector.tensor_copy(links_now[:].rearrange("p t e -> p (t e)"),
                                              links[:, bass.ds(k, 1), :, :].rearrange("p o t e -> p (o t e)")
                                              ).then_inc(s_links, 1)

                def maxima(n, k):
                    if n == 1:
                        dve.wait_ge(s_links, k + 1)
                        dve.wait_ge(s_row, k + 1)
                        nc.vector.tensor_tensor_scan(run_max[:], wall_now[:, 0:P], row_ps, -BIG, ALU.add, ALU.max
                                                     ).then_inc(s_soft, 1)
                    elif n == 2:
                        dve.wait_ge(s_soft, k * 6 + 1)
                        nc.vector.tensor_tensor_scan(seg_max[:, ::-1], wall_now[:, P:0:-1], run_max[:, ::-1], -BIG,
                                                     ALU.add, ALU.max).then_inc(s_soft, 1)
                    elif n == 3:
                        dve.wait_ge(s_soft, k * 6 + 2)
                        nc.vector.tensor_tensor(shifted[:], row_ps, seg_max[:], ALU.subtract).then_inc(s_soft, 1)

                def sums(n, k):
                    if n == 1:
                        dve.wait_ge(s_exp, k + 1)
                        nc.vector.tensor_tensor_scan(run_sum[:], same_now[:, 0:P], weight[:], 0.0, ALU.mult, ALU.add
                                                     ).then_inc(s_soft, 1)
                    elif n == 2:
                        dve.wait_ge(s_soft, k * 6 + 4)
                        nc.vector.tensor_tensor(last_sum[:], run_sum[:], apart_now[:, 1:P + 1], ALU.mult
                                                ).then_inc(s_soft, 1)
                    elif n == 3:
                        dve.wait_ge(s_soft, k * 6 + 5)
                        ge(dve, s_col, k)
                        nc.vector.tensor_tensor_scan(seg_sum[:, ::-1], same_now[:, P:0:-1], last_sum[:, ::-1], 0.0,
                                                     ALU.mult, ALU.add).then_inc(s_soft, 1)

                def alphas(n, k):
                    if n == 1:
                        dve.wait_ge(s_col, k + 1)
                        nc.vector.reciprocal(col_rcp[:], sum_ps).then_inc(s_alpha_step, 1)
                    elif n == 2:
                        dve.wait_ge(s_alpha_step, k * 2 + 1)
                        nc.vector.tensor_tensor(col_alpha[:], weight_ps, col_rcp[:], ALU.mult
                                                ).then_inc(s_alpha_step, 1)
                    elif n == 3:
                        dve.wait_ge(s_alpha_step, k * 2 + 2)
                        nc.vector.tensor_tensor(alpha[:, (j - 8) // 4 % 3, :, :],
                                                col_alpha[:].unsqueeze(2).to_broadcast([P, 16, 2]),
                                                parity[:, bass.ds(k * 16, 16), :], ALU.mult).then_inc(s_alpha, 1)

                if is_batch_step(q, j, 4):
                    moments(0, 2)
                    batch(1)
                else:
                    batch(1)
                    moments(0, 2)
                split(0)
                batch(2)
                moments(2, 4)
                split(1)
                batch(3)
                moments(4, 6)
                split(2)
                batch(4)
                moments(6, 8)
                split(3)
                batch(5)
            quads(dve, step, NQ - 1 + 13)

            nc.vector.memset(last_node[:], -1.0)
            nc.vector.memset(new_max[:], -BIG)
            nc.vector.memset(z_sum[:], 0.0)
            nc.vector.tensor_copy(attn_src_wide[:], edge_w[:, F:F + 1].to_broadcast([FV, PW]))
            done(nc.vector.memset(z_acc[:], 0.0))

            def fix(g):
                fixed = [0]

                def then(ins):
                    fixed[0] += 1
                    ins.then_inc(s_fix, 1)
                    dve.wait_ge(s_fix, g * FIX_STEPS + fixed[0])

                nc.vector.tensor_scalar(node_now[:], node_id[:], chunk_node[:], None, ALU.add)
                nc.vector.tensor_tensor(goes_on[:], block_node[:], last_node[:], ALU.is_equal)
                then(nc.vector.tensor_tensor(overlap[:], chunk_begin[:], chunk_edge[:], ALU.subtract))
                nc.vector.tensor_scalar(overlap[:], overlap[:], float(NPB), None, ALU.mult)
                nc.vector.tensor_copy(last_node[:], block_node[:])
                then(nc.vector.tensor_scalar(reset[:], goes_on[:], -1.0, BIG, ALU.add, ALU.mult))
                nc.vector.tensor_scalar(old_max[:], new_max[:], goes_on[0:PW, :], reset[0:PW, :],
                                        ALU.mult, ALU.add)
                then(nc.vector.tensor_scalar(valid[:], starts[:, 0:P], overlap[:], None, ALU.is_ge))
                dve.wait_ge(s_c_dst, g * 16 + 16)
                then(nc.vector.tensor_copy(c_dst[:], c_dst_i[:]))
                for half in range(2):
                    last = nc.vector.scalar_tensor_tensor(c_mask[:, half, :], c_dst[:],
                                                          node_now[0:PW, half:half + 1], valid[0:PW, :],
                                                          ALU.is_equal, ALU.mult)
                then(last)
                nc.vector.tensor_scalar(c_wall[:], c_mask[:], -1.0, BIG, ALU.add, ALU.mult)
                dve.wait_ge(s_c_tr, g + 1)
                nc.vector.tensor_copy(c_xt[:], bank[1][:, 0:PW])
                nc.vector.tensor_copy(c_vt[:], bank[1][0:FV, P:2 * P]).then_inc(s_c_cp, 1)
                where(then, 1)
                where(then, 2)
                dve.wait_ge(s_c_prod, g + 1)
                nc.vector.tensor_copy(c_y[:], bank[5][:, 256:256 + F])
                then(nc.vector.tensor_scalar(c_own[:], bank[5][0:PW, P:P + 2], attn_b_col[0:PW, :], None, ALU.add))
                for half in range(2):
                    last = nc.vector.tensor_scalar(c_logit[:, half, :], bank[5][0:PW, 0:P],
                                                   c_own[:, half:half + 1], None, ALU.add)
                then(last)
                then(nc.vector.scalar_tensor_tensor(c_leaky[:], c_logit[:], LEAK, c_logit[:], ALU.mult, ALU.max))
                then(nc.vector.tensor_tensor(c_leaky[:], c_leaky[:], c_mask[:], ALU.mult))
                then(nc.vector.tensor_tensor(c_logit[:], c_leaky[:], c_wall[:], ALU.add))
                then(nc.vector.tensor_reduce(c_max[:], c_logit[:], AX.X, ALU.max))
                then(nc.vector.tensor_tensor(new_max[:], old_max[:], c_max[:], ALU.max))
                nc.vector.tensor_scalar(minus_max[:], new_max[:], -1.0, None, ALU.mult)
                nc.vector.tensor_tensor(drop[:], old_max[:], new_max[:], ALU.subtract).then_inc(s_c_max, 1)
                where(then, 3)
                dve.wait_ge(s_c_exp, g + 1)
                nc.vector.tensor_tensor(c_weight[:], c_exp[:], c_mask[:], ALU.mult).then_inc(s_c_weight, 1)
                dve.wait_ge(s_c_weight, g + 1)
                nc.vector.tensor_reduce(c_sum[:], c_weight[:], AX.X, ALU.add)
                then(nc.vector.tensor_scalar(scale[:], scale[:], goes_on[0:PW, :], None, ALU.mult))
                then(nc.vector.tensor_tensor(z_sum[:], z_sum[:], scale[:], ALU.mult))
                then(nc.vector.tensor_tensor(z_sum[:], z_sum[:], c_sum[:], ALU.add))
                then(nc.vector.scalar_tensor_tensor(divisor[:], z_sum[:], 0.0, z_sum[:], ALU.is_equal, ALU.add))
                then(nc.vector.reciprocal(inverse[:], divisor[:]))
                dve.wait_ge(s_c_wt, g + 1)
                nc.vector.tensor_copy(c_weight_t[:].rearrange("p j n -> p (j n)"), bank[1][:, 0:2 * PW]
                                      ).then_inc(s_c_wcp, 1)
                where(then, 4)
                dve.wait_ge(s_c_z, g + 1)
                for half in range(2):
                    last = nc.vector.scalar_tensor_tensor(z_acc[:, half, :], z_acc[:, half, :],
                                                          scale[:, half:half + 1],
                                                          bank[4][0:PW, half * F:(half + 1) * F],
                                                          ALU.mult, ALU.add)
                then(last)
                for half in range(2):
                    last = nc.vector.scalar_tensor_tensor(c_h[:, half, :], z_acc[:, half, :],
                                                          inverse[:, half:half + 1],
                                                          bank[3][0:PW, half * F:(half + 1) * F],
                                                          ALU.mult, ALU.add)
                then(last)
                then(nc.vector.scalar_tensor_tensor(c_r[:].rearrange("p j f -> p (j f)"),
                                                    c_h[:].rearrange("p j f -> p (j f)"), 0.0, c_x[:],
                                                    ALU.max, ALU.add))
                for half in range(2):
                    last = nc.vector.bn_stats(c_stats[:, half, :], c_r[:, half, :])
                then(last)
                part(dve)
                for half in range(2):
                    last = nc.vector.bn_aggr(c_moments[:, half, :], c_stats[:, half, :])
                last.then_inc(s_c_var, 1)
                where(then, 5)
                dve.wait_ge(s_c_rstd, g + 1)
                for half in range(2):
                    last = nc.vector.tensor_scalar(c_out[:, half, :], c_r[:, half, :], c_moments[:, half, 0:1],
                                                   c_rstd[:, half:half + 1], ALU.subtract, ALU.mult)
                last.then_inc(s_c_out, 1)
                assert fixed[0] == FIX_STEPS, fixed[0]
            repair(dve, fix)


_INS = ["x", "src", "dst", "edge_attr_32", "L0_gnn_proj_w", "L0_gnn_attn_w", "L0_gnn_attn_b", "L0_gnn_apply_w",
        "L0_gnn_apply_b"]


def kernel(**inputs):
    import numpy as _np
    import concourse.bacc as _bacc
    from concourse import mybir as _mybir
    from concourse.bass_utils import run_bass_kernel_spmd as _run

    nc = _bacc.Bacc("TRN2", target_bir_lowering=False, num_devices=1)
    arrays, args = {}, []
    for name in _INS:
        a = _np.ascontiguousarray(inputs[name])
        arrays[f"in_{name}"] = a
        args.append(nc.dram_tensor(f"in_{name}", a.shape, _mybir.dt.from_np(a.dtype), kind="ExternalInput").ap())
    args.append(nc.dram_tensor("out_0", (N_NODES, F), _mybir.dt.float32, kind="ExternalOutput").ap())
    gnn_kernel(nc, *args)
    r = _run(nc, [arrays], core_ids=[0])
    return r.results[0]["out_0"]
```
